# Optimizing a Trainium2 kernel written in Bass

```python
import numpy as np
import jax
import jax.numpy as jnp

def _softmax(x, axis=-1):
    return jax.nn.softmax(x, axis=axis)

def _gelu(x):
    return jax.nn.gelu(x, approximate=True)

def _silu(x):
    return jax.nn.silu(x)

def _sigmoid(x):
    return jax.nn.sigmoid(x)

def _layernorm(x, axis=-1, eps=1e-05):
    m = jnp.mean(x, axis=axis, keepdims=True)
    v = jnp.var(x, axis=axis, keepdims=True)
    return (x - m) / jnp.sqrt(v + eps)

def _scatter_add(tgt, idx, src, axis=0):
    return tgt.at[idx].add(src)

def _segment_sum(src, seg, n):
    return jax.ops.segment_sum(src, seg, n)
kernel_name = 'mk_gnn_ffn_d2_gnn_r32_6ed72a'

def setup_inputs(seed: int=0):
    np.random.seed(seed)
    _w = jnp.asarray

    def _rec_inputs():
        import jax
        import jax.numpy as jnp
        _gk = jax.random.key(seed)
        x = -0.0003713 + 1 * jax.random.normal(jax.random.fold_in(_gk, 1), (3125, 256), jnp.float32)
        src = jax.random.randint(jax.random.fold_in(_gk, 2), (50000,), 0, 3125, jnp.int32)
        dst = jnp.minimum((3125 * jax.random.uniform(jax.random.fold_in(_gk, 3), (50000,)) ** 2.0).astype(jnp.int32), 99999)
        _o = jnp.argsort(dst, stable=True)
        src = src[_o]
        dst = dst[_o]
        edge_attr_3 = -0.000563758 + 1.00031 * jax.random.normal(jax.random.fold_in(_gk, 11), (50000, 3), jnp.float32)
        edge_type_64 = jax.random.randint(jax.random.fold_in(_gk, 13), (50000,), 0, 64, jnp.int32)
        return (x, src, dst, edge_attr_3, edge_type_64)
    x, src, dst, edge_attr_3, edge_type_64 = _rec_inputs()

    def _L0_gnn_setup():
        import jax, jax.numpy as jnp
        import numpy as np
        N_NODES = 50000
        N_EDGES = 15625
        IN_DIM = 256
        HID = 64
        HEADS = 4
        N_REL = 64
        key = jax.random.key(seed)
        ks = jax.random.split(key, 16)
        s = 0.02
        return {'node_features': jax.random.normal(ks[0], (N_NODES, IN_DIM), jnp.float32), 'edge_index': jax.random.randint(ks[1], (2, N_EDGES), 0, N_NODES, jnp.int32), 'edge_relations': jax.random.randint(ks[2], (N_EDGES,), 0, N_REL, jnp.int32), 'query_emb': jax.random.normal(ks[3], (IN_DIM,), jnp.float32), 'Wq': jax.random.normal(ks[4], (IN_DIM, HID * HEADS), jnp.float32) * s, 'bq': jnp.zeros((HID * HEADS,), jnp.float32), 'Wk': jax.random.normal(ks[5], (IN_DIM, HID * HEADS), jnp.float32) * s, 'bk': jnp.zeros((HID * HEADS,), jnp.float32), 'Wv': jax.random.normal(ks[6], (IN_DIM, HID * HEADS), jnp.float32) * s, 'bv': jnp.zeros((HID * HEADS,), jnp.float32), 'rel_w': jax.random.normal(ks[7], (N_REL, HID), jnp.float32) * s, 'Wo': jax.random.normal(ks[8], (HID * HEADS, IN_DIM), jnp.float32) * s, 'bo': jnp.zeros((IN_DIM,), jnp.float32), 'gamma': jnp.ones((IN_DIM,), jnp.float32), 'beta': jnp.zeros((IN_DIM,), jnp.float32)}
    _L0_gnn_all = _L0_gnn_setup()
    _L0_gnn_in = {k: v for k, v in _L0_gnn_all.items() if k in ('query_emb', 'Wq', 'bq', 'Wk', 'bk', 'Wv', 'bv', 'rel_w', 'Wo', 'bo', 'gamma', 'beta')}
    del _L0_gnn_all

    def _L0_ffn_setup():
        import jax, jax.numpy as jnp
        import numpy as np
        B, S, D = (8, 128, 256)
        H = 4 * D
        CAPACITY = 0.5
        key = jax.random.key(seed)
        ks = jax.random.split(key, 6)
        x = jax.random.normal(ks[0], (B, S, D), dtype=jnp.float32)
        attention_mask = jnp.zeros((B, 1, 1, S), dtype=jnp.float32)
        wr = jax.random.normal(ks[1], (D, 1), dtype=jnp.float32) * 0.02
        br = jnp.zeros((1,), dtype=jnp.float32)
        w1 = jax.random.normal(ks[2], (D, H), dtype=jnp.float32) * 0.02
        b1 = jnp.zeros((H,), dtype=jnp.float32)
        w2 = jax.random.normal(ks[3], (H, D), dtype=jnp.float32) * 0.02
        b2 = jnp.zeros((D,), dtype=jnp.float32)
        return {'x': x, 'attention_mask': attention_mask, 'wr': wr, 'br': br, 'w1': w1, 'b1': b1, 'w2': w2, 'b2': b2}
    _L0_ffn_all = _L0_ffn_setup()
    _L0_ffn_in = {k: v for k, v in _L0_ffn_all.items() if k in ('attention_mask', 'wr', 'br', 'w1', 'b1', 'w2', 'b2')}
    del _L0_ffn_all

    def _L1_gnn_setup():
        import jax, jax.numpy as jnp
        import numpy as np
        MUL = 64
        N_NODES = 10000
        N_EDGES = 10000
        DIM = MUL + 3 * MUL
        SQ3 = float(np.sqrt(3.0))
        INV_MUL = float(1.0 / np.sqrt(MUL))
        INV_TP = float(1.0 / np.sqrt(2 * MUL))

        def _split(f):
            return (f[:, :MUL], f[:, MUL:].reshape(f.shape[0], MUL, 3))

        def _lin(x0, x1, w0, w1):
            return (x0 @ w0 * INV_MUL, jnp.einsum('eum,uv->evm', x1, w1) * INV_MUL)

        def _fctp(x0, x1, sh1, w00, w11, w01, w10):
            dot = jnp.einsum('eum,em->eu', x1, sh1) / SQ3
            out0 = (x0 @ w00 + dot @ w11) * INV_TP
            out1 = (jnp.einsum('eu,uv->ev', x0, w01)[:, :, None] * sh1[:, None, :] + jnp.einsum('eum,uv->evm', x1, w10)) * INV_TP
            return (out0, out1)

        def _forward(atom_feature, edge_vector, weights, edge_index):
            ls0, ls1, ld0, ld1, t1_00, t1_11, t1_01, t1_10, t2_00, t2_11, t2_01, t2_10, lh0, lh1, lsc = weights
            src, dst = (edge_index[0], edge_index[1])
            r = edge_vector / (jnp.linalg.norm(edge_vector, axis=-1, keepdims=True) + 1e-12)
            sh1 = SQ3 * r
            x0, x1 = _split(atom_feature)
            s0, s1 = _lin(x0[src], x1[src], ls0, ls1)
            d0, d1 = _lin(x0[dst], x1[dst], ld0, ld1)
            h0, h1 = _fctp(s0, s1, sh1, t1_00, t1_11, t1_01, t1_10)
            h0, h1 = _lin(h0, h1, lh0, lh1)
            sc = jax.nn.leaky_relu(h0) @ lsc * INV_MUL
            full = jnp.concatenate([sc, jnp.zeros((sc.shape[0], 3 * MUL), sc.dtype)], axis=-1)
            act = jax.nn.softmax(full, axis=-1)
            o0, o1 = _fctp(h0, h1, sh1, t2_00, t2_11, t2_01, t2_10)
            tp2_flat = jnp.concatenate([o0, o1.reshape(o1.shape[0], 3 * MUL)], axis=-1)
            msgs = act * tp2_flat
            agg = jax.ops.segment_sum(msgs, dst, num_segments=atom_feature.shape[0])
            return atom_feature + agg
        _WNAMES = ['lin_src_w0', 'lin_src_w1', 'lin_dst_w0', 'lin_dst_w1', 'tp1_w00', 'tp1_w11', 'tp1_w01', 'tp1_w10', 'tp2_w00', 'tp2_w11', 'tp2_w01', 'tp2_w10', 'lin_hidden_w0', 'lin_hidden_w1', 'lin_scalar_w']
        key = jax.random.key(seed)
        ks = jax.random.split(key, 18)
        inp = {n: jax.random.normal(ks[i], (MUL, MUL), jnp.float32) for i, n in enumerate(_WNAMES)}
        inp['atom_feature'] = jax.random.normal(ks[15], (N_NODES, DIM), jnp.float32)
        inp['edge_vector'] = jax.random.normal(ks[16], (N_EDGES, 3), jnp.float32)
        inp['edge_index'] = jax.random.randint(ks[17], (2, N_EDGES), 0, N_NODES, dtype=jnp.int32)
        return inp
    _L1_gnn_all = _L1_gnn_setup()
    _L1_gnn_in = {k: v for k, v in _L1_gnn_all.items() if k in ('lin_src_w0', 'lin_src_w1', 'lin_dst_w0', 'lin_dst_w1', 'tp1_w00', 'tp1_w11', 'tp1_w01', 'tp1_w10', 'tp2_w00', 'tp2_w11', 'tp2_w01', 'tp2_w10', 'lin_hidden_w0', 'lin_hidden_w1', 'lin_scalar_w')}
    del _L1_gnn_all

    def _L1_ffn_setup():
        import jax, jax.numpy as jnp
        import numpy as np
        B, S, D, F, E, K = (8, 64, 256, 1024, 8, 2)
        key = jax.random.key(seed)
        ks = jax.random.split(key, 10)
        s = 0.02
        return {'x': jax.random.normal(ks[0], (B, S, D), dtype=jnp.float32), 'Wr': jax.random.normal(ks[1], (D, E), dtype=jnp.float32) * s, 'W1s': jax.random.normal(ks[2], (D, F), dtype=jnp.float32) * s, 'b1s': jnp.zeros((F,), dtype=jnp.float32), 'W2s': jax.random.normal(ks[3], (F, D), dtype=jnp.float32) * s, 'b2s': jnp.zeros((D,), dtype=jnp.float32), 'W1p': jax.random.normal(ks[4], (E, D, F), dtype=jnp.float32) * s, 'b1p': jnp.zeros((E, F), dtype=jnp.float32), 'W2p': jax.random.normal(ks[5], (E, F, D), dtype=jnp.float32) * s, 'b2p': jnp.zeros((E, D), dtype=jnp.float32)}
    _L1_ffn_all = _L1_ffn_setup()
    _L1_ffn_in = {k: v for k, v in _L1_ffn_all.items() if k in ('Wr', 'W1s', 'b1s', 'W2s', 'b2s', 'W1p', 'b1p', 'W2p', 'b2p')}
    del _L1_ffn_all
    return {'x': x, 'src': src, 'dst': dst, 'edge_attr_3': edge_attr_3, 'edge_type_64': edge_type_64, 'L0_gnn_query_emb': _L0_gnn_in['query_emb'], 'L0_gnn_Wq': _L0_gnn_in['Wq'], 'L0_gnn_bq': _L0_gnn_in['bq'], 'L0_gnn_Wk': _L0_gnn_in['Wk'], 'L0_gnn_bk': _L0_gnn_in['bk'], 'L0_gnn_Wv': _L0_gnn_in['Wv'], 'L0_gnn_bv': _L0_gnn_in['bv'], 'L0_gnn_rel_w': _L0_gnn_in['rel_w'], 'L0_gnn_Wo': _L0_gnn_in['Wo'], 'L0_gnn_bo': _L0_gnn_in['bo'], 'L0_gnn_gamma': _L0_gnn_in['gamma'], 'L0_gnn_beta': _L0_gnn_in['beta'], 'L0_ffn_attention_mask': _L0_ffn_in['attention_mask'], 'L0_ffn_wr': _L0_ffn_in['wr'], 'L0_ffn_br': _L0_ffn_in['br'], 'L0_ffn_w1': _L0_ffn_in['w1'], 'L0_ffn_b1': _L0_ffn_in['b1'], 'L0_ffn_w2': _L0_ffn_in['w2'], 'L0_ffn_b2': _L0_ffn_in['b2'], 'L1_gnn_lin_src_w0': _L1_gnn_in['lin_src_w0'], 'L1_gnn_lin_src_w1': _L1_gnn_in['lin_src_w1'], 'L1_gnn_lin_dst_w0': _L1_gnn_in['lin_dst_w0'], 'L1_gnn_lin_dst_w1': _L1_gnn_in['lin_dst_w1'], 'L1_gnn_tp1_w00': _L1_gnn_in['tp1_w00'], 'L1_gnn_tp1_w11': _L1_gnn_in['tp1_w11'], 'L1_gnn_tp1_w01': _L1_gnn_in['tp1_w01'], 'L1_gnn_tp1_w10': _L1_gnn_in['tp1_w10'], 'L1_gnn_tp2_w00': _L1_gnn_in['tp2_w00'], 'L1_gnn_tp2_w11': _L1_gnn_in['tp2_w11'], 'L1_gnn_tp2_w01': _L1_gnn_in['tp2_w01'], 'L1_gnn_tp2_w10': _L1_gnn_in['tp2_w10'], 'L1_gnn_lin_hidden_w0': _L1_gnn_in['lin_hidden_w0'], 'L1_gnn_lin_hidden_w1': _L1_gnn_in['lin_hidden_w1'], 'L1_gnn_lin_scalar_w': _L1_gnn_in['lin_scalar_w'], 'L1_ffn_Wr': _L1_ffn_in['Wr'], 'L1_ffn_W1s': _L1_ffn_in['W1s'], 'L1_ffn_b1s': _L1_ffn_in['b1s'], 'L1_ffn_W2s': _L1_ffn_in['W2s'], 'L1_ffn_b2s': _L1_ffn_in['b2s'], 'L1_ffn_W1p': _L1_ffn_in['W1p'], 'L1_ffn_b1p': _L1_ffn_in['b1p'], 'L1_ffn_W2p': _L1_ffn_in['W2p'], 'L1_ffn_b2p': _L1_ffn_in['b2p']}

def reference(x, src, dst, edge_attr_3, edge_type_64, L0_gnn_query_emb, L0_gnn_Wq, L0_gnn_bq, L0_gnn_Wk, L0_gnn_bk, L0_gnn_Wv, L0_gnn_bv, L0_gnn_rel_w, L0_gnn_Wo, L0_gnn_bo, L0_gnn_gamma, L0_gnn_beta, L0_ffn_attention_mask, L0_ffn_wr, L0_ffn_br, L0_ffn_w1, L0_ffn_b1, L0_ffn_w2, L0_ffn_b2, L1_gnn_lin_src_w0, L1_gnn_lin_src_w1, L1_gnn_lin_dst_w0, L1_gnn_lin_dst_w1, L1_gnn_tp1_w00, L1_gnn_tp1_w11, L1_gnn_tp1_w01, L1_gnn_tp1_w10, L1_gnn_tp2_w00, L1_gnn_tp2_w11, L1_gnn_tp2_w01, L1_gnn_tp2_w10, L1_gnn_lin_hidden_w0, L1_gnn_lin_hidden_w1, L1_gnn_lin_scalar_w, L1_ffn_Wr, L1_ffn_W1s, L1_ffn_b1s, L1_ffn_W2s, L1_ffn_b2s, L1_ffn_W1p, L1_ffn_b1p, L1_ffn_W2p, L1_ffn_b2p):
    import jax
    import jax.numpy as jnp

    def _L0_gnn_ref(node_features, edge_index, edge_relations, query_emb, Wq, bq, Wk, bk, Wv, bv, rel_w, Wo, bo, gamma, beta):
        import jax, jax.numpy as jnp
        import numpy as np
        N_NODES = 50000
        N_EDGES = 15625
        IN_DIM = 256
        HID = 64
        HEADS = 4
        N_REL = 64
        N = node_features.shape[0]
        D = rel_w.shape[1]
        H = Wq.shape[1] // D
        enh = node_features + 0.1 * query_emb[None, :]
        Q = (enh @ Wq + bq).reshape(N, H, D)
        K = (enh @ Wk + bk).reshape(N, H, D)
        V = (enh @ Wv + bv).reshape(N, H, D)
        src, dst = (edge_index[0], edge_index[1])
        rel = rel_w[edge_relations]
        mod_k = K[src] + 0.2 * rel[:, None, :]
        scores = jnp.einsum('ehd,ehd->eh', Q[dst], mod_k) / D ** 0.5
        seg_max = jax.ops.segment_max(scores, dst, num_segments=N)
        ex = jnp.exp(scores - seg_max[dst])
        denom = jax.ops.segment_sum(ex, dst, num_segments=N)
        w = ex / denom[dst]
        agg = jax.ops.segment_sum(w[:, :, None] * V[src], dst, num_segments=N)
        deg = jax.ops.segment_sum(jnp.ones((src.shape[0],), jnp.float32), dst, num_segments=N)
        msgs = jnp.where(deg[:, None, None] > 0, agg, V)
        out = msgs.reshape(N, H * D) @ Wo + bo
        x = out + node_features
        mu = jnp.mean(x, axis=-1, keepdims=True)
        var = jnp.var(x, axis=-1, keepdims=True)
        return (x - mu) / jnp.sqrt(var + 1e-05) * gamma + beta

    def _L0_ffn_ref(x, attention_mask, wr, br, w1, b1, w2, b2):
        import jax, jax.numpy as jnp
        import numpy as np
        B, S, D = (8, 128, 256)
        H = 4 * D
        CAPACITY = 0.5
        b, s, d = x.shape
        weights = (jnp.einsum('bsd,do->bso', x, wr) + br)[..., 0]
        k = max(1, int(CAPACITY * s))
        kk = k - 1 if k > 1 else 1
        _, idx = jax.lax.top_k(weights, k)
        sel_idx = idx[:, :kk]
        sel = jnp.take_along_axis(x, sel_idx[:, :, None], axis=1)
        h = jax.nn.gelu(jnp.einsum('bkd,dh->bkh', sel, w1) + b1)
        y = jnp.einsum('bkh,hd->bkd', h, w2) + b2
        w_sel = jnp.take_along_axis(weights, sel_idx, axis=1)
        y = y * w_sel[..., None]
        batch_idx = jnp.arange(b)[:, None]
        processed = jnp.zeros_like(x).at[batch_idx, sel_idx].set(y)
        return processed + x

    def _L1_gnn_ref(atom_feature, edge_vector, lin_src_w0, lin_src_w1, lin_dst_w0, lin_dst_w1, tp1_w00, tp1_w11, tp1_w01, tp1_w10, tp2_w00, tp2_w11, tp2_w01, tp2_w10, lin_hidden_w0, lin_hidden_w1, lin_scalar_w, edge_index):
        import jax, jax.numpy as jnp
        import numpy as np
        MUL = 64
        N_NODES = 10000
        N_EDGES = 10000
        DIM = MUL + 3 * MUL
        SQ3 = float(np.sqrt(3.0))
        INV_MUL = float(1.0 / np.sqrt(MUL))
        INV_TP = float(1.0 / np.sqrt(2 * MUL))

        def _split(f):
            return (f[:, :MUL], f[:, MUL:].reshape(f.shape[0], MUL, 3))

        def _lin(x0, x1, w0, w1):
            return (x0 @ w0 * INV_MUL, jnp.einsum('eum,uv->evm', x1, w1) * INV_MUL)

        def _fctp(x0, x1, sh1, w00, w11, w01, w10):
            dot = jnp.einsum('eum,em->eu', x1, sh1) / SQ3
            out0 = (x0 @ w00 + dot @ w11) * INV_TP
            out1 = (jnp.einsum('eu,uv->ev', x0, w01)[:, :, None] * sh1[:, None, :] + jnp.einsum('eum,uv->evm', x1, w10)) * INV_TP
            return (out0, out1)

        def _forward(atom_feature, edge_vector, weights, edge_index):
            ls0, ls1, ld0, ld1, t1_00, t1_11, t1_01, t1_10, t2_00, t2_11, t2_01, t2_10, lh0, lh1, lsc = weights
            src, dst = (edge_index[0], edge_index[1])
            r = edge_vector / (jnp.linalg.norm(edge_vector, axis=-1, keepdims=True) + 1e-12)
            sh1 = SQ3 * r
            x0, x1 = _split(atom_feature)
            s0, s1 = _lin(x0[src], x1[src], ls0, ls1)
            d0, d1 = _lin(x0[dst], x1[dst], ld0, ld1)
            h0, h1 = _fctp(s0, s1, sh1, t1_00, t1_11, t1_01, t1_10)
            h0, h1 = _lin(h0, h1, lh0, lh1)
            sc = jax.nn.leaky_relu(h0) @ lsc * INV_MUL
            full = jnp.concatenate([sc, jnp.zeros((sc.shape[0], 3 * MUL), sc.dtype)], axis=-1)
            act = jax.nn.softmax(full, axis=-1)
            o0, o1 = _fctp(h0, h1, sh1, t2_00, t2_11, t2_01, t2_10)
            tp2_flat = jnp.concatenate([o0, o1.reshape(o1.shape[0], 3 * MUL)], axis=-1)
            msgs = act * tp2_flat
            agg = jax.ops.segment_sum(msgs, dst, num_segments=atom_feature.shape[0])
            return atom_feature + agg
        _WNAMES = ['lin_src_w0', 'lin_src_w1', 'lin_dst_w0', 'lin_dst_w1', 'tp1_w00', 'tp1_w11', 'tp1_w01', 'tp1_w10', 'tp2_w00', 'tp2_w11', 'tp2_w01', 'tp2_w10', 'lin_hidden_w0', 'lin_hidden_w1', 'lin_scalar_w']
        weights = (lin_src_w0, lin_src_w1, lin_dst_w0, lin_dst_w1, tp1_w00, tp1_w11, tp1_w01, tp1_w10, tp2_w00, tp2_w11, tp2_w01, tp2_w10, lin_hidden_w0, lin_hidden_w1, lin_scalar_w)
        return _forward(atom_feature, edge_vector, weights, edge_index)

    def _L1_ffn_ref(x, Wr, W1s, b1s, W2s, b2s, W1p, b1p, W2p, b2p):
        import jax, jax.numpy as jnp
        import numpy as np
        B, S, D, F, E, K = (8, 64, 256, 1024, 8, 2)
        gelu = lambda t: jax.nn.gelu(t, approximate=False)
        shared = gelu(x @ W1s + b1s) @ W2s + b2s
        rw = jax.nn.softmax(x @ Wr, axis=-1)
        topw, topi = jax.lax.top_k(rw, K)
        topw = topw / jnp.sum(topw, axis=-1, keepdims=True)
        mask = jnp.sum(jax.nn.one_hot(topi, E, dtype=topw.dtype) * topw[..., None], axis=-2)
        h = gelu(jnp.einsum('bsd,edf->bsef', x, W1p) + b1p)
        priv = jnp.einsum('bsef,efd->bsed', h, W2p) + b2p
        routed = jnp.einsum('bsed,bse->bsd', priv, mask)
        return shared + routed
    edge_index = jnp.stack([src, dst])
    x = x + _L0_gnn_ref(_layernorm(x, axis=-1), edge_index, edge_type_64, L0_gnn_query_emb, L0_gnn_Wq, L0_gnn_bq, L0_gnn_Wk, L0_gnn_bk, L0_gnn_Wv, L0_gnn_bv, L0_gnn_rel_w, L0_gnn_Wo, L0_gnn_bo, L0_gnn_gamma, L0_gnn_beta)
    x = x + _L0_ffn_ref(_layernorm(x, axis=-1)[None], L0_ffn_attention_mask, L0_ffn_wr, L0_ffn_br, L0_ffn_w1, L0_ffn_b1, L0_ffn_w2, L0_ffn_b2)[0]
    x = x + _L1_gnn_ref(_layernorm(x, axis=-1), edge_attr_3, L1_gnn_lin_src_w0, L1_gnn_lin_src_w1, L1_gnn_lin_dst_w0, L1_gnn_lin_dst_w1, L1_gnn_tp1_w00, L1_gnn_tp1_w11, L1_gnn_tp1_w01, L1_gnn_tp1_w10, L1_gnn_tp2_w00, L1_gnn_tp2_w11, L1_gnn_tp2_w01, L1_gnn_tp2_w10, L1_gnn_lin_hidden_w0, L1_gnn_lin_hidden_w1, L1_gnn_lin_scalar_w, edge_index)
    x = x + _L1_ffn_ref(_layernorm(x, axis=-1)[None], L1_ffn_Wr, L1_ffn_W1s, L1_ffn_b1s, L1_ffn_W2s, L1_ffn_b2s, L1_ffn_W1p, L1_ffn_b1p, L1_ffn_W2p, L1_ffn_b2p)[0]
    return x

_drawn_inputs = setup_inputs


def setup_inputs(seed=0):
    import zlib

    import numpy as np

    out = dict(_drawn_inputs(seed))
    spreads = {'L0_gnn_bq': (0.0, 0.8),
     'L0_gnn_bk': (0.0, 2.0),
     'L0_gnn_bv': (0.0, 0.492),
     'L0_gnn_bo': (0.0, 0.1),
     'L0_gnn_gamma': (1.0, 0.2),
     'L0_gnn_beta': (0.0, 0.1),
     'L0_ffn_b1': (0.0, 0.8),
     'L0_ffn_b2': (0.0, 0.8),
     'L1_ffn_b1s': (0.0, 2.0),
     'L1_ffn_b2s': (0.0, 2.0),
     'L1_ffn_b1p': (0.0, 2.0),
     'L1_ffn_b2p': (0.0, 2.0)}
    factors = {'edge_attr_3': 8.0,
     'L0_gnn_query_emb': 8.0,
     'L0_gnn_Wq': 8.0,
     'L0_gnn_Wk': 8.0,
     'L0_gnn_Wv': 3.395,
     'L0_gnn_rel_w': 8.0,
     'L0_ffn_wr': 5.646,
     'L0_ffn_w1': 6.794,
     'L0_ffn_w2': 6.404,
     'L1_gnn_lin_src_w0': 8.0,
     'L1_gnn_lin_src_w1': 8.0,
     'L1_gnn_tp1_w00': 8.0,
     'L1_gnn_tp1_w11': 8.0,
     'L1_gnn_tp1_w01': 8.0,
     'L1_gnn_tp1_w10': 8.0,
     'L1_gnn_tp2_w00': 8.0,
     'L1_gnn_tp2_w11': 8.0,
     'L1_gnn_tp2_w01': 8.0,
     'L1_gnn_tp2_w10': 8.0,
     'L1_gnn_lin_hidden_w0': 8.0,
     'L1_gnn_lin_hidden_w1': 8.0,
     'L1_gnn_lin_scalar_w': 8.0,
     'L1_ffn_W1p': 23.352,
     'L1_ffn_W2p': 21.816,
     'L1_ffn_Wr': 8.0,
     'L1_ffn_W1s': 64.0,
     'L1_ffn_W2s': 64.0}
    for name, (base, spread) in spreads.items():
        noise = np.random.default_rng([zlib.crc32(name.encode()), seed]).standard_normal(out[name].shape)
        drawn = base * np.exp(spread * noise) if base else spread * noise
        out[name] = jnp.asarray(drawn.astype(out[name].dtype))
    for name, factor in factors.items():
        out[name] = (out[name] * factor).astype(out[name].dtype)
    return out
```

```python
from contextlib import ExitStack

import numpy as np
import concourse.bass as bass
from concourse import mybir

ALU = mybir.AluOpType
ACT = mybir.ActivationFunctionType
F32 = mybir.dt.float32
BF16 = mybir.dt.bfloat16
I32 = mybir.dt.int32
U32 = mybir.dt.uint32
AX = mybir.AxisListType
ds = bass.ds

N = 3125
E = 50000
D = 256
P = 125
NT = N // P
G = 5
NG = NT // G
H, HD = 4, 64
NREL = 64
EP = 128
U = 4
CH = U * P
SORT_STEPS = E // CH
T = -(-((E + NT * (EP - 1)) // EP) // (2 * U)) * 2 * U
STEPS = T // U
TX = T + 2 * U
REC = 8
R_SRC, R_LO, R_TYPE, R_VEC, R_DST = 0, 1, 2, 3, 6
BIG = 1.0e30
FF = 1024
NF = FF // 128
NE = 8
KEPT = max(1, N // 2) - 1
EPS = 1e-5
NBLK = T * H // 128
SPLIT = (0, 320, G * P)


class Sems:

    def __init__(self, nc, ctx):
        self.nc, self.ctx = nc, ctx

    def __call__(self, name):
        return self.nc.alloc_semaphore(name)


def stage(build_stage):
    def staged(nc, *args, **kw):
        with nc.cleanup_on_exit():
            build_stage(nc, *args, **kw)
    return staged


class Chain:

    def __init__(self, eng, sem):
        self.eng, self.sem, self.n = eng, sem, 0

    def __call__(self, ins):
        self.n += 1
        ins.then_inc(self.sem, 1)
        self.eng.wait_ge(self.sem, self.n)


@stage
def build_constants(nc, m):
    with ExitStack() as ctx:
        sem = Sems(nc, ctx)
        s_made = sem("c_made")
        s_cast = sem("c_cast")
        block = ctx.enter_context(nc.Block())

        @block.gpsimd
        def _(pool):
            ch = Chain(pool, s_made)
            ch(pool.memset(m.ones[:, :], 1.0))
            ch(pool.iota(m.iota_i[:, :], pattern=[[1, T]], base=0, channel_multiplier=0))
            ch(pool.iota(m.part_i[:, :], pattern=[[0, 1]], base=0, channel_multiplier=1))
            ch(pool.memset(m.ident[:, :], 0.0))
            ch(pool.affine_select(out=m.ident[:, :], in_=m.ident[:, :], compare_op=ALU.not_equal, fill=1.0,
                                  base=0, pattern=[[-1, 128]], channel_multiplier=1))
            ch(pool.affine_select(out=m.before[:, :], in_=m.ones[:, :], compare_op=ALU.is_gt, fill=0.0,
                                  base=0, pattern=[[-1, 128]], channel_multiplier=1))
            ch(pool.affine_select(out=m.after[:, :], in_=m.ones[:, :], compare_op=ALU.is_gt, fill=0.0,
                                  base=0, pattern=[[1, 128]], channel_multiplier=-1))

        @block.vector
        def _(dve):
            ch = Chain(dve, s_cast)
            dve.wait_ge(s_made, 7)
            ch(dve.tensor_copy(m.iota[:, :], m.iota_i[:, :]))
            ch(dve.tensor_copy(m.part[:, :], m.part_i[:, :]))
            ch(dve.tensor_copy(m.ident_b[:, :], m.ident[:, :]))


@stage
def build_sort(nc, m, a):
    with ExitStack() as ctx:
        sem = Sems(nc, ctx)

        def sb(name, shape, dt=F32):
            return ctx.enter_context(nc.sbuf_tensor(name, shape, dt))

        Q = 100
        NB = E // (Q * P)
        rec_in = sb("rec_in", [P, SORT_STEPS * U, REC])
        hi = sb("hi", [P, SORT_STEPS * U])
        lo = sb("lo", [P, SORT_STEPS * U])
        hi_hot = sb("hi_hot", [P, SORT_STEPS * U, NT], BF16)
        lo_hot = [sb(f"lo_hot{i}", [P, U, P], BF16) for i in range(2)]
        start = sb("start", [P, NT])
        row_d = m.row_d

        with ExitStack() as c1:
            def sb1(name, shape, dt=F32):
                return c1.enter_context(nc.sbuf_tensor(name, shape, dt))

            sem1 = Sems(nc, c1)
            nat_i = [sb1(f"nat_i{i}", [Q, NB, P], I32) for i in range(3)]
            nat_v = sb1("nat_v", [Q, NB, 3 * P])
            nat_f = [sb1(f"nat_f{i}", [Q, NB, P]) for i in range(3)]
            nat_hi = [sb1(f"nat_hi{i}", [Q, NB, P]) for i in range(2)]
            nat_lo = sb1("nat_lo", [Q, NB, P])
            empty = sb1("empty", [EP, TX, REC])
            ps = [c1.enter_context(nc.psum_tensor(f"ps_f{i}", [P, 512], F32)) for i in range(8)]
            s_in = [sem1(f"s_in{i}") for i in range(4)]
            s_flt = sem1("s_flt")
            s_lo = sem1("s_lo")
            s_tr = sem1("s_tr")
            s_empty = sem1("s_empty")
            s_row = sem1("s_row")
            s_fill = sem1("s_fill")
            s_rec = sem1("s_rec")
            s_hot = sem1("s_hot")
            block = c1.enter_context(nc.Block())
            cols = [(nat_f[1], None, R_SRC), (nat_lo, None, R_LO), (nat_f[2], None, R_TYPE),
                    (nat_v, 0, R_VEC), (nat_v, 1, R_VEC + 1), (nat_v, 2, R_VEC + 2), (nat_f[0], None, R_DST),
                    (nat_hi[0], None, None)]

            @block.sync
            def _(sp):
                for i, x in enumerate((a["dst"], a["src"], a["edge_type_64"])):
                    sp.dma_start(nat_i[i][:, :, :], x.rearrange("(b q p) -> q b p", b=NB, q=Q)).then_inc(s_in[i], 16)
                sp.dma_start(nat_v[:, :, :], a["edge_attr_3"].rearrange("(b q p) c -> q b (p c)", b=NB, q=Q)
                             ).then_inc(s_in[3], 16)
                sp.wait_ge(s_empty, 3)
                sp.dma_start(m.rec_d.rearrange("(p t) c -> p t c", p=EP), empty[:, :, :]).then_inc(s_fill, 16)
                sp.wait_ge(s_lo, 26)
                sp.dma_start(row_d[1, :].rearrange("(b q p) -> q b p", b=NB, q=Q), nat_lo[:, :, :]
                             ).then_inc(s_row, 16)
                sp.dma_start(row_d[0, :].rearrange("(b q p) -> q b p", b=NB, q=Q), nat_f[0][:, :, :]
                             ).then_inc(s_row, 16)
                sp.wait_ge(s_row, 32)
                sp.wait_ge(s_fill, 16)

            @block.gpsimd
            def _(pool):
                ch = Chain(pool, s_empty)
                ch(pool.memset(empty[:, :, :], 0.0))
                ch(pool.memset(empty[:, :, R_LO:R_LO + 1], -1.0))
                ch(pool.memset(empty[:, :, R_DST:R_DST + 1], -1.0))

            @block.vector
            def _(dve):
                for i in range(3):
                    dve.wait_ge(s_in[i], 16)
                    dve.tensor_copy(nat_f[i][:, :, :], nat_i[i][:, :, :]).then_inc(s_flt, 1)
                dve.wait_ge(s_flt, 3)
                ch = Chain(dve, s_lo)
                ch(dve.memset(nat_hi[0][:, :, :], 0.0))
                for k in range(1, NT):
                    ch(dve.scalar_tensor_tensor(nat_hi[k % 2][:, :, :], nat_f[0][:, :, :], float(k * P),
                                                nat_hi[(k + 1) % 2][:, :, :], ALU.is_ge, ALU.add))
                ch(dve.scalar_tensor_tensor(nat_lo[:, :, :], nat_hi[0][:, :, :], -float(P), nat_f[0][:, :, :],
                                            ALU.mult, ALU.add))
                dve.memset(rec_in[:, :, :], 0.0).then_inc(s_rec, 1)
                dve.wait_ge(s_rec, 1)
                for k, (_, _, field) in enumerate(cols):
                    dve.wait_ge(s_tr, k + 1)
                    to = hi[:, :] if field is None else rec_in[:, :, field]
                    dve.tensor_copy(to, ps[k][:, 0:NB * Q]).then_inc(s_rec, 1)
                dve.wait_ge(s_rec, 9)
                dve.tensor_copy(lo[:, :], rec_in[:, :, R_LO]).then_inc(s_hot, 1)
                dve.tensor_tensor(hi_hot[:, :, :], m.iota[0:P, None, 0:NT].to_broadcast([P, SORT_STEPS * U, NT]),
                                  hi[:, :, None].to_broadcast([P, SORT_STEPS * U, NT]), ALU.is_equal
                                  ).then_inc(s_hot, 1)

            @block.tensor
            def _(pe):
                pe.wait_ge(s_lo, 26)
                pe.wait_ge(s_in[3], 16)
                for k, (tile, comp, _) in enumerate(cols):
                    for b in range(NB):
                        src = tile[:, b, :] if comp is None else tile[:, b, comp::3]
                        last = pe.transpose(ps[k][:, b * Q:(b + 1) * Q], src, m.ident[0:Q, 0:Q])
                    last.then_inc(s_tr, 1)

        with ExitStack() as c1:
            sem1 = Sems(nc, c1)
            ps_hist = c1.enter_context(nc.psum_tensor("ps_hist", [P, 512], F32))
            ps_sum = c1.enter_context(nc.psum_tensor("ps_sum", [P, 512], F32))
            ps_pre = c1.enter_context(nc.psum_tensor("ps_pre", [P, 512], F32))
            hist = c1.enter_context(nc.sbuf_tensor("hist", [P, NT], F32))
            tiles_f = c1.enter_context(nc.sbuf_tensor("tiles_f", [P, NT], F32))
            tiles_i = c1.enter_context(nc.sbuf_tensor("tiles_i", [P, 2, NT], I32))
            tile_end = c1.enter_context(nc.sbuf_tensor("tile_end", [P, NT], F32))
            passed = c1.enter_context(nc.sbuf_tensor("passed", [1, T, NT], F32))
            of_tile = c1.enter_context(nc.sbuf_tensor("of_tile", [1, T], F32))
            s_made = sem1("s_lo_made")
            s_used = sem1("s_lo_used")
            s_hist = sem1("s_hist")
            s_ch = sem1("s_pre_ch")
            s_sum = sem1("s_sum")
            block = c1.enter_context(nc.Block())

            @block.vector
            def _(dve):
                def hot(step, b):
                    dve.tensor_tensor(lo_hot[b][:, :, :], m.iota[0:P, None, 0:P].to_broadcast([P, U, P]),
                                      lo[:, ds(step * U, U), None].to_broadcast([P, U, P]), ALU.is_equal
                                      ).then_inc(s_made, 1)

                hot(0, 0)
                hot(1, 1)
                with dve.Fori(1, SORT_STEPS // 2) as it:
                    for b in range(2):
                        dve.wait_ge(s_used, 2 * it + b - 1)
                        hot(2 * it + b, b)
                ch = Chain(dve, s_ch)
                dve.wait_ge(s_hist, 1)
                ch(dve.tensor_copy(hist[:, :], ps_hist[:, 0:NT]))
                dve.wait_ge(s_sum, 1)
                ch(dve.tensor_scalar(tiles_f[:, :], ps_sum[:, 0:NT], float(EP - 1), None, ALU.add))
                ch(dve.tensor_copy(tiles_i[:, 0, :], tiles_f[:, :]))
                ch(dve.tensor_scalar(tiles_i[:, 1, :], tiles_i[:, 0, :], EP.bit_length() - 1, None,
                                     ALU.arith_shift_right))
                ch(dve.tensor_copy(tiles_f[:, :], tiles_i[:, 1, :]))
                ch(dve.tensor_tensor_scan(tile_end[:, :], m.ones[0:P, 0:NT], tiles_f[:, :], 0.0, ALU.mult, ALU.add))
                ch(dve.tensor_tensor(tiles_f[:, :], tile_end[:, :], tiles_f[:, :], ALU.subtract))
                ch(dve.scalar_tensor_tensor(start[:, :], tiles_f[:, :], float(EP), ps_pre[:, 0:NT],
                                            ALU.mult, ALU.add))
                ch(dve.tensor_tensor(passed[:, :, :], m.iota[0:1, 0:T, None].to_broadcast([1, T, NT]),
                                     tile_end[0:1, None, :].to_broadcast([1, T, NT]), ALU.is_ge))
                ch(dve.tensor_reduce(of_tile[:, :], passed[:, :, :], AX.X, ALU.add))
                ch(dve.tensor_scalar(of_tile[:, :], of_tile[:, :], float(NT - 1), None, ALU.min))
                ch(dve.tensor_copy(m.node_tile[0:1, 0:T], of_tile[:, :]))

            @block.tensor
            def _(pe):
                def count(step, b, start_, stop_):
                    for u in range(U):
                        last = pe.matmul(ps_hist[:, 0:NT], lo_hot[b][:, u, :], hi_hot[:, step * U + u, :],
                                         start=start_ and u == 0, stop=stop_ and u == U - 1,
                                         skip_group_check=True)
                    last.then_inc(s_used, 1)
                    return last

                pe.wait_ge(s_made, 1)
                count(0, 0, True, False)
                pe.wait_ge(s_made, 2)
                count(1, 1, False, False)
                with pe.Fori(1, SORT_STEPS // 2) as it:
                    for b in range(2):
                        pe.wait_ge(s_made, 2 * it + b + 1)
                        count(2 * it + b, b, False, False)
                pe.wait_ge(s_used, SORT_STEPS)
                pe.sem_inc(s_hist, 1)
                pe.wait_ge(s_ch, 1)
                pe.matmul(ps_sum[:, 0:NT], m.ones[0:P, 0:P], hist[:, :], start=True, stop=True)
                pe.matmul(ps_pre[:, 0:NT], m.after[0:P, 0:P], hist[:, :], start=True, stop=True).then_inc(s_sum, 1)

        with ExitStack() as c1:
            sem1 = Sems(nc, c1)

            def sb1(name, shape, dt=F32):
                return c1.enter_context(nc.sbuf_tensor(name, shape, dt))

            row = [sb1(f"row{b}", [1, 2, CH]) for b in range(2)]
            lo_hot_t = [sb1(f"lo_hot_t{b}", [P, U, P]) for b in range(2)]
            earlier = [sb1(f"earlier{b}", [P, U]) for b in range(2)]
            junk = sb1("junk", [P, U, CH], BF16)
            mask = sb1("mask", [P, U, CH], BF16)
            picked = [sb1(f"picked{b}", [P, U, NT]) for b in range(2)]
            base = [sb1(f"base{b}", [P, U]) for b in range(2)]
            place = [sb1(f"place{b}", [P, U], U32) for b in range(2)]
            rec_s = [sb1(f"rec_s{b}", [P, U, REC]) for b in range(2)]
            ps_dst = [c1.enter_context(nc.psum_tensor(f"ps_dst{b}", [P, 512], F32)) for b in range(2)]
            ps_lo = [c1.enter_context(nc.psum_tensor(f"ps_lo{b}", [P, 512], F32)) for b in range(2)]
            ps_base = [c1.enter_context(nc.psum_tensor(f"ps_base{b}", [P, 512], F32)) for b in range(2)]
            ps_cnt = [c1.enter_context(nc.psum_tensor(f"ps_cnt{b}", [P, 512], F32)) for b in range(2)]
            s_mask = sem1("s_mask")
            s_rowl = [sem1(f"s_rowl{b}") for b in range(2)]
            s_rows = sem1("s_rows")
            s_hot = sem1("s_hot2")
            s_rank = sem1("s_rank")
            s_look = sem1("s_look")
            s_pick = sem1("s_pick")
            s_base = sem1("s_base")
            s_run = sem1("s_run")
            s_place = sem1("s_place")
            s_recs = sem1("s_recs")
            s_sent = [sem1(f"s_sent{b}") for b in range(2)]
            s_go = sem1("s_go")
            block = c1.enter_context(nc.Block())

            @block.sync
            def _(sp):
                sp.sem_inc(s_rows, 2)
                with sp.Fori(0, SORT_STEPS // 2) as it:
                    for b in range(2):
                        s = 2 * it + b
                        sp.wait_ge(s_rows, s + 1)
                        sp.dma_start(row[b][:, :, :], row_d[None, :, ds(s * CH, CH)]).then_inc(s_rowl[b], 16)

            @block.tensor
            def _(pe):
                pe.wait_ge(s_mask, 5)
                with pe.Fori(0, SORT_STEPS // 2) as it:
                    for b in range(2):
                        s = 2 * it + b
                        pe.wait_ge(s_rowl[b], 16 * it + 16)
                        pe.wait_ge(s_rank, s + 1)
                        pe.matmul(ps_dst[b][:, 0:CH], m.ones[0:1, 0:P], row[b][:, 0, :], start=True, stop=True)
                        pe.matmul(ps_lo[b][:, 0:CH], m.ones[0:1, 0:P], row[b][:, 1, :], start=True, stop=True
                                  ).then_inc(s_rows, 1)
                        pe.wait_ge(s_hot, s + 1)
                        pe.wait_ge(s_run, s + 1)
                        for u in range(U):
                            pe.matmul(ps_base[b][:, u * NT:(u + 1) * NT], lo_hot_t[b][:, u, :], start[:, :],
                                      start=True, stop=True)
                        for u in range(U):
                            last = pe.matmul(ps_cnt[b][:, 0:NT], lo_hot[b][:, u, :], hi_hot[:, s * U + u, :],
                                             start=u == 0, stop=u == U - 1)
                        last.then_inc(s_look, 1)

            @block.vector
            def _(dve):
                dve.memset(mask[:, :, :], 0.0).then_inc(s_mask, 1)
                dve.wait_ge(s_mask, 1)
                for u in range(U):
                    if u:
                        dve.memset(mask[:, u, 0:u * P], 1.0)
                    dve.tensor_copy(mask[:, u, u * P:(u + 1) * P], m.before[0:P, 0:P]).then_inc(s_mask, 1)
                dve.sem_inc(s_run, 1)
                dve.sem_inc(s_rank, 2)
                dve.wait_ge(s_mask, 5)
                def rank(s, it, b):
                    dve.wait_ge(s_rows, s + 3)
                    dve.tensor_scalar(lo_hot_t[b].rearrange("p u q -> p (u q)"), ps_lo[b][:, 0:CH],
                                      m.part[0:P, 0:1], None, ALU.is_equal)
                    dve.tensor_tensor(lo_hot[b][:, :, :], m.iota[0:P, None, 0:P].to_broadcast([P, U, P]),
                                      lo[:, ds(s * U, U), None].to_broadcast([P, U, P]), ALU.is_equal
                                      ).then_inc(s_hot, 1)
                    for u in range(U):
                        n = (u + 1) * P
                        last = dve.scalar_tensor_tensor(junk[:, u, 0:n], ps_dst[b][:, 0:n],
                                                        rec_in[:, s * U + u, R_DST:R_DST + 1], mask[:, u, 0:n],
                                                        ALU.is_equal, ALU.mult, accum_out=earlier[b][:, u:u + 1])
                    last.then_inc(s_rank, 1)
                    dve.wait_ge(s_look, s + 1)
                    dve.tensor_tensor(start[:, :], start[:, :], ps_cnt[b][:, 0:NT], ALU.add)
                    dve.tensor_tensor(picked[b][:, :, :], ps_base[b][:, 0:U * NT].rearrange("p (u n) -> p u n", u=U),
                                      hi_hot[:, ds(s * U, U), :], ALU.mult).then_inc(s_run, 1)
                    dve.wait_ge(s_run, s + 2)
                    dve.tensor_reduce(base[b][:, :], picked[b][:, :, :], AX.X, ALU.add).then_inc(s_base, 1)
                    dve.wait_ge(s_base, s + 1)
                    dve.wait_ge(s_rank, s + 3)
                    if not known(it):
                        dve.wait_ge(s_sent[b], 16 * U * it)
                    dve.tensor_tensor(place[b][:, :], base[b][:, :], earlier[b][:, :], ALU.add).then_inc(s_place, 1)

                rank(0, 0, 0)
                rank(1, 0, 1)
                with dve.Fori(1, SORT_STEPS // 2) as it:
                    for b in range(2):
                        rank(2 * it + b, it, b)

            @block.scalar
            def _(act):
                def pack(s, it, b):
                    if not known(it):
                        act.wait_ge(s_sent[b], 16 * U * it)
                    act.activation(rec_s[b][:, :, :], rec_in[:, ds(s * U, U), :], ACT.Copy).then_inc(s_recs, 1)

                pack(0, 0, 0)
                pack(1, 0, 1)
                with act.Fori(1, SORT_STEPS // 2) as it:
                    for b in range(2):
                        pack(2 * it + b, it, b)

            @block.gpsimd
            def _(pool):
                with pool.Fori(0, SORT_STEPS // 2) as it:
                    for b in range(2):
                        s = 2 * it + b
                        pool.wait_ge(s_place, s + 1)
                        pool.sem_inc(s_go, 1)
                        pool.wait_ge(s_recs, s + 1)
                        pool.sem_inc(s_go, 1)
                        for u in range(U):
                            pool.indirect_dma_start(
                                out=m.rec_d[:, :], out_offset=bass.IndirectOffsetOnAxis(ap=place[b][:, u:u + 1], axis=0),
                                in_=rec_s[b][:, u, :], in_offset=None).then_inc(s_sent[b], 16)
                for b in range(2):
                    pool.wait_ge(s_sent[b], 16 * U * SORT_STEPS // 2)


@stage
def build_reload(nc, m):
    with ExitStack() as ctx:
        sem = Sems(nc, ctx)
        s_rec = [sem(f"s_recl{i}") for i in range(4)]
        s_ch = sem("s_vec")
        s_sq = sem("s_sq")
        sq = ctx.enter_context(nc.sbuf_tensor("vsq", [EP, TX, 3], F32))
        n2 = ctx.enter_context(nc.sbuf_tensor("vn2", [EP, TX], F32))
        block = ctx.enter_context(nc.Block())
        cut = [0, TX // 4, TX // 2, 3 * TX // 4, TX]
        view = m.rec_d.rearrange("(t p) c -> p t c", p=EP)

        @block.sync
        def _(sp):
            for i in range(0, 4, 2):
                sp.dma_start(m.rec[:, cut[i]:cut[i + 1], :], view[:, cut[i]:cut[i + 1], :]).then_inc(s_rec[i], 16)

        @block.scalar
        def _(act):
            for i in range(1, 4, 2):
                act.dma_start(m.rec[:, cut[i]:cut[i + 1], :], view[:, cut[i]:cut[i + 1], :]).then_inc(s_rec[i], 16)
            act.wait_ge(s_ch, 3)
            act.activation(n2[:, :], n2[:, :], ACT.Sqrt).then_inc(s_sq, 1)

        @block.vector
        def _(dve):
            for i in range(4):
                dve.wait_ge(s_rec[i], 16)
            ch = Chain(dve, s_ch)
            vec = m.rec[:, :, R_VEC:R_VEC + 3]
            ch(dve.tensor_copy(m.src[:, :], m.rec[:, :, R_SRC]))
            ch(dve.tensor_tensor(sq[:, :, :], vec, vec, ALU.mult))
            ch(dve.tensor_reduce(n2[:, :], sq[:, :, :], AX.X, ALU.add))
            dve.wait_ge(s_sq, 1)
            ch(dve.tensor_scalar(n2[:, :], n2[:, :], 1e-12, None, ALU.add))
            ch(dve.reciprocal(n2[:, :], n2[:, :]))
            ch(dve.tensor_tensor(m.unit[:, :, :], vec, n2[:, :, None].to_broadcast([EP, TX, 3]), ALU.mult))
            ch(dve.tensor_tensor(sq[:, :, :], m.unit[:, :, :], m.unit[:, :, :], ALU.mult))
            ch(dve.tensor_reduce(m.unit2[:, :], sq[:, :, :], AX.X, ALU.add))


@stage
def layer_norm(nc, m, tag, x, y, gamma=None, beta=None):
    with ExitStack() as ctx:
        sem = Sems(nc, ctx)
        st = ctx.enter_context(nc.sbuf_tensor(f"st_{tag}", [P, NT, 6], F32))
        mv = ctx.enter_context(nc.sbuf_tensor(f"mv_{tag}", [P, NT, 2], F32))
        rs = ctx.enter_context(nc.sbuf_tensor(f"rs_{tag}", [P, NT], F32))
        s_st = sem(f"s_st_{tag}")
        s_sq = sem(f"s_sq_{tag}")
        s_ch = sem(f"s_ch_{tag}")
        block = ctx.enter_context(nc.Block())

        @block.vector
        def _(dve):
            with dve.Fori(0, NG) as g:
                for u in range(G):
                    dve.bn_stats(st[:, G * g + u, :], x[:, G * g + u, :]).then_inc(s_st, 1)
            dve.wait_ge(s_st, NT)
            ch = Chain(dve, s_ch)
            ch(dve.tensor_tensor(mv[:, :, 0], st[:, :, 1], st[:, :, 4], ALU.subtract))
            ch(dve.tensor_tensor(mv[:, :, 0], mv[:, :, 0], mv[:, :, 0], ALU.mult))
            ch(dve.tensor_tensor(rs[:, :], st[:, :, 2], st[:, :, 5], ALU.add))
            ch(dve.tensor_scalar(rs[:, :], rs[:, :], 1.0 / D, EPS, ALU.mult, ALU.add))
            ch(dve.scalar_tensor_tensor(rs[:, :], mv[:, :, 0], 0.25, rs[:, :], ALU.mult, ALU.add))
            ch(dve.tensor_tensor(mv[:, :, 0], st[:, :, 1], st[:, :, 4], ALU.add))
            ch(dve.tensor_scalar(mv[:, :, 0], mv[:, :, 0], 0.5, None, ALU.mult))
            dve.wait_ge(s_sq, 1)
            ch(dve.reciprocal(rs[:, :], rs[:, :]))
            ch(dve.tensor_tensor(y[:, :, :], x[:, :, :], mv[:, :, 0:1].to_broadcast([P, NT, D]), ALU.subtract))
            ch(dve.tensor_tensor(y[:, :, :], y[:, :, :], rs[:, :, None].to_broadcast([P, NT, D]), ALU.mult))
            if gamma is not None:
                ch(dve.tensor_tensor(y[:, :, :], y[:, :, :], gamma[:, None, :].to_broadcast([P, NT, D]), ALU.mult))
                ch(dve.tensor_tensor(y[:, :, :], y[:, :, :], beta[:, None, :].to_broadcast([P, NT, D]), ALU.add))

        @block.scalar
        def _(act):
            act.wait_ge(s_ch, 5)
            act.activation(rs[:, :], rs[:, :], ACT.Sqrt).then_inc(s_sq, 1)


@stage
def add_all(nc, tag, pairs):
    with ExitStack() as ctx:
        s_ch = Sems(nc, ctx)(f"s_add_{tag}")
        block = ctx.enter_context(nc.Block())

        @block.vector
        def _(dve):
            ch = Chain(dve, s_ch)
            for out, x, y in pairs:
                ch(dve.tensor_tensor(out, x, y, ALU.add))


@stage
def project(nc, m, tag, prepare, weights, width, finish, keep=None, halves=2, own=0):
    NW = len(weights)
    with ExitStack() as ctx:
        sem = Sems(nc, ctx)
        rows = ctx.enter_context(nc.sbuf_tensor(f"rows_{tag}", [P, G, 256], F32))
        rows_t = ctx.enter_context(nc.sbuf_tensor(f"rows_t_{tag}", [128, G, 2, P], F32))
        ps_t = ctx.enter_context(nc.psum_tensor(f"ps_t_{tag}", [128, 6, 256], F32))
        ps_o = ctx.enter_context(nc.psum_tensor(f"ps_o_{tag}", [128, 6, 256], F32))
        s_prep = sem(f"s_prep_{tag}")
        s_tr = sem(f"s_tr_{tag}")
        s_evac = sem(f"s_evac_{tag}")
        s_mm = sem(f"s_mm_{tag}")
        s_fin = sem(f"s_fin_{tag}")
        s_own = sem(f"s_own_{tag}")
        block = ctx.enter_context(nc.Block())

        @block.vector
        def _(dve):
            dve.sem_inc(s_tr, 1)
            with dve.Fori(0, NG) as g:
                count = [0]

                def ch(ins):
                    count[0] += 1
                    ins.then_inc(s_own, 1)
                    dve.wait_ge(s_own, g * own + count[0])

                dve.wait_ge(s_tr, g + 1)
                prepare(dve, g, rows, ch).then_inc(s_prep, 1)
                for c in range(NW):
                    dve.wait_ge(s_mm, NW * g + c + 1)
                    finish(dve, g, c, ps_o[0:P, 0:G, 0:width], ch).then_inc(s_fin, 1)
                assert count[0] == own

        @block.tensor
        def _(pe):
            pe.sem_inc(s_evac, 1)
            pe.sem_inc(s_fin, 1)
            with pe.Fori(0, NG) as g:
                pe.wait_ge(s_prep, g + 1)
                pe.wait_ge(s_evac, g + 1)
                for u in range(G):
                    for k in range(halves):
                        last = pe.transpose(ps_t[:, u, k * 128:k * 128 + P], rows[:, u, k * 128:(k + 1) * 128],
                                            m.ident[0:P, 0:P])
                last.then_inc(s_tr, 1)
                pe.wait_ge(s_evac, g + 2)
                for c, w in enumerate(weights):
                    pe.wait_ge(s_fin, NW * g + c + 1)
                    for u in range(G):
                        for k in range(halves):
                            last = pe.matmul(ps_o[0:P, u, 0:width], rows_t[:, u, k, :], w[:, k, :],
                                             start=k == 0, stop=k == halves - 1)
                    last.then_inc(s_mm, 1)

        @block.scalar
        def _(act):
            with act.Fori(0, NG) as g:
                act.wait_ge(s_tr, g + 2)
                act.wait_ge(s_fin, NW * g + 1)
                view = ps_t[:, 0:G, :].rearrange("p u (k n) -> p u k n", k=2)[:, :, 0:halves, 0:P]
                if keep is not None:
                    for k in range(halves):
                        act.activation(keep(g, k), view[:, :, k, :], ACT.Copy)
                act.activation(rows_t[:, :, 0:halves, :], view, ACT.Copy).then_inc(s_evac, 1)


def known(s):
    return isinstance(s, int)


@stage
def build_scores(nc, m):
    with ExitStack() as ctx:
        sem = Sems(nc, ctx)

        def sb(name, shape, dt=F32):
            return ctx.enter_context(nc.sbuf_tensor(name, shape, dt))

        idx = [sb(f"a_idx{b}", [EP, U], U32) for b in range(2)]
        k_rows = [sb(f"a_k{b}", [EP, U, D]) for b in range(2)]
        hot = [sb(f"a_hot{b}", [EP, U, P], BF16) for b in range(2)]
        rel_hot = [sb(f"a_rhot{b}", [EP, U, NREL], BF16) for b in range(2)]
        hot_t = [sb(f"a_hott{b}", [P, U, EP]) for b in range(2)]
        rel_t = [sb(f"a_rhott{b}", [NREL, U, EP]) for b in range(2)]
        kmod = [sb("a_kmod", [EP, U, D])] * 2
        prod = kmod
        ps_q = [ctx.enter_context(nc.psum_tensor(f"a_psq{b}", [EP, U, D], F32)) for b in range(2)]
        ps_t = [ctx.enter_context(nc.psum_tensor(f"a_pst{b}", [128, 2, U, EP], BF16)) for b in range(2)]
        ps_r = [ctx.enter_context(nc.psum_tensor(f"a_psr{b}", [EP, 2 * U, HD], F32)) for b in range(2)]
        s_idx = sem("a_idx")
        s_k = [sem(f"a_k_{b}") for b in range(2)]
        s_go = sem("a_go")
        s_hot = sem("a_hot")
        s_tr = sem("a_tr")
        s_ev = sem("a_ev")
        s_exp = sem("a_exp")
        s_kmod = sem("a_kmod")
        s_prod = sem("a_prod")
        s_sum = sem("a_sum")
        block = ctx.enter_context(nc.Block())

        @block.gpsimd
        def _(pool):
            def body(s, b):
                pool.wait_ge(s_idx, s + 1)
                pool.sem_inc(s_go, 1)
                if not (known(s) and s < 2):
                    pool.wait_ge(s_kmod, s - 1)
                    pool.sem_inc(s_go, 1)
                for u in range(U):
                    pool.indirect_dma_start(out=k_rows[b][:, u, :], out_offset=None, in_=m.k_d[:, :],
                                            in_offset=bass.IndirectOffsetOnAxis(ap=idx[b][:, u:u + 1], axis=0)
                                            ).then_inc(s_k[b], 16)

            body(0, 0)
            body(1, 1)
            with pool.Fori(1, STEPS // 2) as it:
                for b in range(2):
                    body(2 * it + b, b)

        @block.scalar
        def _(act):
            def body(s, b):
                if not (known(s) and s < 2):
                    act.wait_ge(s_kmod, s - 1)
                act.activation(idx[b][:, :], m.src[:, ds(s * U, U)], ACT.Copy).then_inc(s_idx, 1)
                act.wait_ge(s_tr, s + 1)
                if not (known(s) and s < 2):
                    act.wait_ge(s_exp, s - 1)
                act.activation(hot_t[b][:, :, :], ps_t[b][0:P, 0, :, :], ACT.Copy)
                act.activation(rel_t[b][:, :, :], ps_t[b][0:NREL, 1, :, :], ACT.Copy).then_inc(s_ev, 1)

            body(0, 0)
            body(1, 1)
            with act.Fori(1, STEPS // 2) as it:
                for b in range(2):
                    body(2 * it + b, b)

        @block.tensor
        def _(pe):
            def turn(s, b):
                pe.wait_ge(s_hot, s + 1)
                if not (known(s) and s < 2):
                    pe.wait_ge(s_ev, s - 1)
                for u in range(U):
                    pe.transpose(ps_t[b][0:P, 0, u, :], hot[b][:, u, :], m.ident_b[:, :])
                    last = pe.transpose(ps_t[b][0:NREL, 1, u, :], rel_hot[b][:, u, :], m.ident_b[:, :])
                last.then_inc(s_tr, 1)

            def expand(s, b):
                pe.wait_ge(s_ev, s + 1)
                if not (known(s) and s < 2):
                    pe.wait_ge(s_prod, s - 1)
                for u in range(U):
                    j = pe.value_load(m.node_tile[0:1, ds(s * U + u, 1)], min_val=0, max_val=NT - 1)
                    pe.matmul(ps_q[b][:, u, :], hot_t[b][:, u, :], m.q[:, j, :], start=True, stop=True)
                    last = pe.matmul(ps_r[b][:, u, :], rel_t[b][:, u, :], m.rel[:, :], start=True, stop=True)
                last.then_inc(s_exp, 1)

            turn(0, 0)
            turn(1, 1)
            expand(0, 0)
            with pe.Fori(0, (STEPS - 2) // 2) as it:
                for b in range(2):
                    turn(2 * it + 2 + b, b)
                    expand(2 * it + 1 + b, 1 - b)
            expand(STEPS - 1, 1)

        @block.vector
        def _(dve):
            def make(s, b):
                if not (known(s) and s < 2):
                    dve.wait_ge(s_tr, s - 1)
                dve.tensor_tensor(hot[b][:, :, :], m.iota[:, None, 0:P].to_broadcast([EP, U, P]),
                                  m.rec[:, ds(s * U, U), R_LO:R_LO + 1].to_broadcast([EP, U, P]), ALU.is_equal)
                dve.tensor_tensor(rel_hot[b][:, :, :], m.iota[:, None, 0:NREL].to_broadcast([EP, U, NREL]),
                                  m.rec[:, ds(s * U, U), R_TYPE:R_TYPE + 1].to_broadcast([EP, U, NREL]),
                                  ALU.is_equal).then_inc(s_hot, 1)

            def score(s, it, b):
                dve.wait_ge(s_k[b], 16 * U * it + 16 * U)
                dve.wait_ge(s_exp, s + 1)
                dve.wait_ge(s_sum, s + 1)
                dve.tensor_tensor(kmod[b].rearrange("p u (h d) -> p u h d", h=H),
                                  k_rows[b].rearrange("p u (h d) -> p u h d", h=H),
                                  ps_r[b][:, 0:U, None, :].to_broadcast([EP, U, H, HD]), ALU.add).then_inc(s_kmod, 1)
                dve.wait_ge(s_kmod, s + 1)
                dve.tensor_tensor(prod[b][:, :, :], kmod[b][:, :, :], ps_q[b][:, :, :], ALU.mult).then_inc(s_prod, 1)
                dve.wait_ge(s_prod, s + 1)
                dve.tensor_reduce(m.s[:, ds(s * U, U), :].rearrange("p u h -> p (u h)"),
                                  prod[b].rearrange("p u (h d) -> p (u h) d", h=H), AX.X, ALU.add).then_inc(s_sum, 1)

            dve.sem_inc(s_sum, 1)
            make(0, 0)
            make(1, 1)
            with dve.Fori(0, (STEPS - 2) // 2) as it:
                for b in range(2):
                    make(2 * it + 2 + b, b)
                    score(2 * it + b, it, b)
            for b in range(2):
                score(STEPS - 2 + b, (STEPS - 2) // 2, b)


@stage
def build_weights(nc, m):
    with ExitStack() as ctx:
        sem = Sems(nc, ctx)

        def sb(name, shape, dt=F32):
            return ctx.enter_context(nc.sbuf_tensor(name, shape, dt))

        W = NBLK * 128
        st = sb("x_st", [128, W])
        dt = sb("x_dt", [128, W])
        cut = sb("x_cut", [128, W + 1])
        dst4 = cut[:, 0:W].rearrange("p (t h) -> p t h", h=H)
        fwd = sb("x_fwd", [128, W])
        bwd = sb("x_bwd", [128, W])
        ends = sb("x_ends", [128, 4, NBLK])
        ends_t = sb("x_ends_t", [4 * NBLK, 128])
        spare = m.agg[0:1, :, :].rearrange("p j c -> p (j c)")
        er = spare[:, 0:4 * W].rearrange("p (c w) -> p c w", c=4)
        link = sb("x_link", [1, W + H])
        both = spare[:, 4 * W:6 * W].rearrange("p (c w) -> p c w", c=2)
        run = sb("x_run", [1, 2, W + 2 * H])
        carry = er[:, 0:2, :]
        carry_t = sb("x_carry_t", [2 * NBLK, 128])
        cc = sb("x_cc", [128, 2, NBLK])
        tmp = bwd[:, :].rearrange("p (b e) -> p b e", e=128)
        NBK = -(-W // 512)
        ps_a = ctx.enter_context(nc.psum_tensor("x_psa", [128, NBK * 512], F32))
        ps_b = ctx.enter_context(nc.psum_tensor("x_psb", [128, NBK * 512], F32))
        s_ch = sem("x_ch")
        s_pe = sem("x_pe")
        s_d = [sem(f"x_d{i}") for i in range(4)]
        s_fin = sem("x_fin")
        block = ctx.enter_context(nc.Block())
        marks = {}

        @block.vector
        def _(dve):
            ch = Chain(dve, s_ch)
            b3 = lambda t: t.rearrange("p (b e) -> p b e", e=128)
            ch(dve.tensor_copy(dst4[:, :, :], m.rec[:, 0:T, R_DST:R_DST + 1].to_broadcast([EP, T, H])))
            marks["dst4"] = ch.n
            dve.wait_ge(s_pe, 1)
            ch(dve.tensor_copy(st[:, :], ps_a[:, 0:W]))
            ch(dve.tensor_copy(dt[:, :], ps_b[:, 0:W]))
            ch(dve.tensor_tensor(cut[:, 1:W], dt[:, 1:W], dt[:, 0:W - 1], ALU.not_equal))
            ch(dve.tensor_scalar(cut[:, 1:W], cut[:, 1:W], -BIG, None, ALU.mult))
            ch(dve.memset(cut[:, 0:W].rearrange("p (b e) -> p b e", e=128)[:, :, 0:1], -BIG))
            ch(dve.memset(cut[:, W:W + 1], -BIG))
            ch(dve.tensor_tensor_scan(fwd[:, :], cut[:, 0:W], st[:, :], -BIG, ALU.add, ALU.max))
            ch(dve.tensor_tensor_scan(bwd[:, ::-1], cut[:, 1:W + 1][:, ::-1], st[:, ::-1], -BIG, ALU.add, ALU.max))
            ch(dve.tensor_tensor(fwd[:, :], fwd[:, :], bwd[:, :], ALU.max))
            ch(dve.tensor_copy(ends[:, 0, :], b3(fwd)[:, :, 0]))
            ch(dve.tensor_copy(ends[:, 1, :], b3(fwd)[:, :, 127]))
            ch(dve.tensor_copy(ends[:, 2, :], b3(dt)[:, :, 0]))
            ch(dve.tensor_copy(ends[:, 3, :], b3(dt)[:, :, 127]))
            marks["ends"] = ch.n
            dve.wait_ge(s_pe, 2)
            ch(dve.tensor_copy(ends_t[:, :], ps_a[0:4 * NBLK, 0:128]))
            marks["ends_t"] = ch.n
            dve.wait_ge(s_d[1], 16)
            ch(dve.memset(link[:, :], -BIG))
            ch(dve.tensor_tensor(link[:, H:W], er[:, 2, H:W], er[:, 3, 0:W - H], ALU.not_equal))
            ch(dve.tensor_scalar(link[:, H:W], link[:, H:W], -BIG, None, ALU.mult))
            ch(dve.tensor_tensor(both[:, 0, :], er[:, 2, :], er[:, 3, :], ALU.not_equal))
            ch(dve.scalar_tensor_tensor(both[:, 1, :], both[:, 0, :], -BIG, link[:, H:W + H], ALU.mult, ALU.add))
            ch(dve.scalar_tensor_tensor(both[:, 0, :], both[:, 0, :], -BIG, link[:, 0:W], ALU.mult, ALU.add))
            ch(dve.memset(run[:, :, :], -BIG))
            for h in range(H):
                ch(dve.tensor_tensor_scan(run[:, 0, H + h:W + H:H], both[:, 0, h::H], er[:, 1, h::H], -BIG,
                                          ALU.add, ALU.max))
                ch(dve.tensor_tensor_scan(run[:, 1, h:W:H][:, ::-1], both[:, 1, h::H][:, ::-1],
                                          er[:, 0, h::H][:, ::-1], -BIG, ALU.add, ALU.max))
            ch(dve.tensor_tensor(carry[:, 0, :], run[:, 0, 0:W], link[:, 0:W], ALU.add))
            ch(dve.tensor_tensor(carry[:, 1, :], run[:, 1, H:W + H], link[:, H:W + H], ALU.add))
            marks["carry"] = ch.n
            dve.wait_ge(s_pe, 3)
            ch(dve.tensor_copy(cc.rearrange("p c b -> p (c b)"), ps_a[:, 0:2 * NBLK]))
            for side, at in ((0, 2), (1, 3)):
                ch(dve.tensor_tensor(tmp[:, :, :], b3(dt), ends[:, at, :, None].to_broadcast([128, NBLK, 128]),
                                     ALU.not_equal))
                ch(dve.scalar_tensor_tensor(tmp[:, :, :], tmp[:, :, :], -BIG,
                                            cc[:, side, :, None].to_broadcast([128, NBLK, 128]), ALU.mult, ALU.add))
                ch(dve.tensor_tensor(b3(fwd), b3(fwd), tmp[:, :, :], ALU.max))
            marks["max"] = ch.n
            dve.wait_ge(s_pe, 4)
            flat = m.s[:, 0:T, :].rearrange("p t h -> p (t h)")
            ch(dve.tensor_tensor(flat, flat, ps_b[:, 0:W], ALU.subtract))
            marks["sub"] = ch.n

        @block.tensor
        def _(pe):
            flat = m.s[:, 0:T, :].rearrange("p t h -> p (t h)")
            dflat = dst4.rearrange("p t h -> p (t h)")
            pe.wait_ge(s_ch, marks["dst4"])
            for b in range(NBLK):
                c = slice(b * 128, (b + 1) * 128)
                pe.transpose(ps_a[:, c], flat[:, c], m.ident[:, :])
                last = pe.transpose(ps_b[:, c], dflat[:, c], m.ident[:, :])
            last.then_inc(s_pe, 1)
            pe.wait_ge(s_ch, marks["ends"])
            pe.transpose(ps_a[0:4 * NBLK, 0:128], ends.rearrange("p c b -> p (c b)"), m.ident[:, :]).then_inc(s_pe, 1)
            pe.wait_ge(s_d[3], 16)
            pe.transpose(ps_a[:, 0:2 * NBLK], carry_t[:, :], m.ident[0:2 * NBLK, 0:2 * NBLK]).then_inc(s_pe, 1)
            pe.wait_ge(s_ch, marks["max"])
            for b in range(NBLK):
                c = slice(b * 128, (b + 1) * 128)
                last = pe.transpose(ps_b[:, c], fwd[:, c], m.ident[:, :])
            last.then_inc(s_pe, 1)

        @block.sync
        def _(sp):
            sp.wait_ge(s_ch, marks["ends_t"])
            sp.dma_start(m.ends_d[:, :], ends_t[:, :]).then_inc(s_d[0], 16)
            sp.wait_ge(s_d[0], 16)
            sp.dma_start(er[:, :, :], m.ends_d.rearrange("(a c b) e -> a c (b e)", a=1, c=4)).then_inc(s_d[1], 16)
            sp.wait_ge(s_ch, marks["carry"])
            sp.dma_start(m.carry_d.rearrange("(a c b) e -> a c (b e)", a=1, c=2), carry).then_inc(s_d[2], 16)
            sp.wait_ge(s_d[2], 16)
            sp.dma_start(carry_t[:, :], m.carry_d[:, :]).then_inc(s_d[3], 16)

        @block.scalar
        def _(act):
            act.wait_ge(s_ch, marks["sub"])
            act.activation(m.s[:, 0:T, :], m.s[:, 0:T, :], ACT.Exp).then_inc(s_fin, 1)


@stage
def build_values(nc, m):
    WD = D + H
    with ExitStack() as ctx:
        sem = Sems(nc, ctx)

        def sb(name, shape, dt=F32):
            return ctx.enter_context(nc.sbuf_tensor(name, shape, dt))

        idx = [sb(f"b_idx{b}", [EP, U], U32) for b in range(2)]
        v_rows = [sb(f"b_v{b}", [EP, U, D]) for b in range(2)]
        hot = [sb(f"b_hot{b}", [EP, U, P]) for b in range(2)]
        msg = [sb(f"b_msg{b}", [EP, U, WD]) for b in range(2)]
        ps = [ctx.enter_context(nc.psum_tensor(f"b_ps{i}", [P, 512], F32)) for i in range(2 * U)]
        s_idx = sem("b_idx")
        s_v = [sem(f"b_v_{b}") for b in range(2)]
        s_go = sem("b_go")
        s_msg = sem("b_msg")
        s_mm = sem("b_mm")
        s_add = sem("b_add")
        s_zero = sem("b_zero")
        block = ctx.enter_context(nc.Block())

        @block.gpsimd
        def _(pool):
            def body(s, b):
                pool.wait_ge(s_idx, s + 1)
                pool.sem_inc(s_go, 1)
                if not (known(s) and s < 2):
                    pool.wait_ge(s_msg, s - 1)
                    pool.sem_inc(s_go, 1)
                for u in range(U):
                    pool.indirect_dma_start(out=v_rows[b][:, u, :], out_offset=None, in_=m.v_d[:, :],
                                            in_offset=bass.IndirectOffsetOnAxis(ap=idx[b][:, u:u + 1], axis=0)
                                            ).then_inc(s_v[b], 16)

            body(0, 0)
            body(1, 1)
            with pool.Fori(1, STEPS // 2) as it:
                for b in range(2):
                    body(2 * it + b, b)

        @block.scalar
        def _(act):
            def body(s, b):
                if not (known(s) and s < 2):
                    act.wait_ge(s_msg, s - 1)
                act.activation(idx[b][:, :], m.src[:, ds(s * U, U)], ACT.Copy).then_inc(s_idx, 1)

            body(0, 0)
            body(1, 1)
            with act.Fori(1, STEPS // 2) as it:
                for b in range(2):
                    body(2 * it + b, b)

        @block.tensor
        def _(pe):
            def body(s, b):
                pe.wait_ge(s_msg, s + 1)
                if not (known(s) and s < 2):
                    pe.wait_ge(s_add, s - 1)
                for u in range(U):
                    last = pe.matmul(ps[b * U + u][:, 0:WD], hot[b][:, u, :], msg[b][:, u, :], start=True, stop=True)
                last.then_inc(s_mm, 1)

            body(0, 0)
            body(1, 1)
            with pe.Fori(1, STEPS // 2) as it:
                for b in range(2):
                    body(2 * it + b, b)

        @block.vector
        def _(dve):
            def make(s, it, b):
                if not (known(s) and s < 2):
                    dve.wait_ge(s_mm, s - 1)
                dve.tensor_tensor(hot[b][:, :, :], m.iota[:, None, 0:P].to_broadcast([EP, U, P]),
                                  m.rec[:, ds(s * U, U), R_LO:R_LO + 1].to_broadcast([EP, U, P]), ALU.is_equal)
                dve.tensor_copy(msg[b][:, :, D:WD], m.s[:, ds(s * U, U), :])
                dve.wait_ge(s_v[b], 16 * U * it + 16 * U)
                dve.tensor_tensor(msg[b][:, :, 0:D].rearrange("p u (h d) -> p u h d", h=H),
                                  v_rows[b].rearrange("p u (h d) -> p u h d", h=H),
                                  m.s[:, ds(s * U, U), :, None].to_broadcast([EP, U, H, HD]), ALU.mult
                                  ).then_inc(s_msg, 1)

            def add(s, b):
                dve.wait_ge(s_mm, s + 1)
                for u in range(U):
                    j = dve.value_load(m.node_tile[0:1, ds(s * U + u, 1)], min_val=0, max_val=NT - 1)
                    if not (known(s) and s == 0 and u == 0):
                        dve.wait_ge(s_zero, s * U + u + 1)
                    last = dve.tensor_tensor(m.agg[:, j, 0:WD], m.agg[:, j, 0:WD], ps[b * U + u][:, 0:WD], ALU.add)
                    last.then_inc(s_zero, 1)
                dve.wait_ge(s_zero, s * U + U + 1)
                dve.sem_inc(s_add, 1)

            dve.memset(m.agg[:, :, :], 0.0).then_inc(s_zero, 1)
            make(0, 0, 0)
            dve.wait_ge(s_zero, 1)
            make(1, 0, 1)
            add(0, 0)
            with dve.Fori(1, STEPS // 2) as it:
                make(2 * it, it, 0)
                add(2 * it - 1, 1)
                make(2 * it + 1, it, 1)
                add(2 * it, 0)
            add(STEPS - 1, 1)


@stage
def build_geometric(nc, m):
    MW = 64 + 192 + 192
    OWN = 9
    with ExitStack() as ctx:
        sem = Sems(nc, ctx)

        def sb(name, shape, dt=F32):
            return ctx.enter_context(nc.sbuf_tensor(name, shape, dt))

        idx = [sb(f"g_idx{b}", [EP, U], U32) for b in range(2)]
        rows = [sb(f"g_rows{b}", [EP, U, 64 + D]) for b in range(2)]
        xr = sb("g_xr", [EP, U, 64, 3])
        ut = [sb(f"g_ut{b}", [128, U, EP]) for b in range(2)]
        lk = [sb(f"g_lk{b}", [64, U, EP]) for b in range(2)]
        mx = sb("g_mx", [EP, U])
        nm = sb("g_nm", [EP, U])
        ex = sb("g_ex", [EP, U, 64])
        z = sb("g_z", [EP, U])
        en = sb("g_en", [EP, U])
        rz = sb("g_rz", [EP, U])
        al = sb("g_al", [EP, U])
        ar = sb("g_ar", [EP, U, 3])
        t1 = sb("g_t1", [EP, U, 64])
        hot = [sb(f"g_hot{b}", [EP, U, P]) for b in range(2)]
        msg = [sb(f"g_msg{b}", [EP, U, MW]) for b in range(2)]
        ps_t = ctx.enter_context(nc.psum_tensor("g_pst", [128, U, EP], F32))
        ps_h = ctx.enter_context(nc.psum_tensor("g_psh", [64, U, EP], F32))
        ps_s = ctx.enter_context(nc.psum_tensor("g_pss", [EP, 8, 64], F32))
        ps_o = ctx.enter_context(nc.psum_tensor("g_pso", [EP, U, 256], F32))
        ps_a = [ctx.enter_context(nc.psum_tensor(f"g_psa{i}", [P, 512], F32)) for i in range(2)]
        s_idx = sem("g_idx")
        s_x = [sem(f"g_x_{b}") for b in range(2)]
        s_go = sem("g_go")
        s_xr = sem("g_xr")
        s_y = sem("g_y")
        s_tr = sem("g_tr")
        s_ut = sem("g_ut")
        s_h = sem("g_h")
        s_lk = sem("g_lk")
        s_so = sem("g_so")
        s_nm = sem("g_nm")
        s_ex = sem("g_ex")
        s_al = sem("g_al")
        s_xm = sem("g_xm")
        s_msg = sem("g_msg")
        s_prod = sem("g_prod")
        s_sum = sem("g_sum")
        s_ch = sem("g_ch")
        block = ctx.enter_context(nc.Block())

        @block.gpsimd
        def _(pool):
            def body(s, b):
                pool.wait_ge(s_idx, s + 1)
                pool.sem_inc(s_go, 1)
                if not (known(s) and s < 2):
                    pool.wait_ge(s_tr, s - 1)
                    pool.sem_inc(s_go, 1)
                    pool.wait_ge(s_xm, s - 1)
                    pool.sem_inc(s_go, 1)
                for u in range(U):
                    pool.indirect_dma_start(out=rows[b][:, u, 64:64 + D], out_offset=None, in_=m.h_d[:, :],
                                            in_offset=bass.IndirectOffsetOnAxis(ap=idx[b][:, u:u + 1], axis=0)
                                            ).then_inc(s_x[b], 16)

            body(0, 0)
            body(1, 1)
            with pool.Fori(1, STEPS // 2) as it:
                for b in range(2):
                    body(2 * it + b, b)
            body(STEPS, 0)
            pool.wait_ge(s_x[0], 16 * U * (STEPS // 2 + 1))

        @block.scalar
        def _(act):
            def index(s, b):
                act.activation(idx[b][:, :], m.src[:, ds(s * U, U)], ACT.Copy).then_inc(s_idx, 1)

            def turned(s, b):
                act.wait_ge(s_tr, s + 1)
                act.activation(ut[b][:, :, :], ps_t[:, :, :], ACT.Copy).then_inc(s_ut, 1)
                act.wait_ge(s_h, s + 1)
                act.activation(lk[b][:, :, :], ps_h[:, :, :], ACT.Relu).then_inc(s_lk, 1)

            index(0, 0)
            index(1, 1)
            turned(0, 0)
            with act.Fori(0, STEPS // 2) as it:
                for b in range(2):
                    s = 2 * it + b
                    act.wait_ge(s_nm, s + 1)
                    act.activation(en[:, :], nm[:, :], ACT.Exp)
                    for u in range(U):
                        last = act.activation(ex[:, u, :], ps_s[:, u, :], ACT.Exp, bias=nm[:, u:u + 1],
                                              accum_out=z[:, u:u + 1])
                    last.then_inc(s_ex, 1)
                    turned(s + 1, 1 - b)
                    act.wait_ge(s_al, s + 1)
                    act.wait_ge(s_prod, s * U + U)
                    for u in range(U):
                        last = act.activation(msg[b][:, u, 64:256], rows[b][:, u, 128:320], ACT.Copy,
                                              scale=al[:, u:u + 1])
                    last.then_inc(s_xm, 1)
                    act.wait_ge(s_x[b], 16 * U * it + 16 * U)
                    index(s + 2, b)

        @block.tensor
        def _(pe):
            def turn(s, b):
                pe.wait_ge(s_y, s + 2)
                for u in range(U):
                    last = pe.transpose(ps_t[:, u, :], rows[b][:, u, 0:128], m.ident[:, :])
                last.then_inc(s_tr, 1)
                pe.wait_ge(s_ut, s + 1)
                pe.matmul(ps_h.rearrange("p u e -> p (u e)"), m.w_h[:, :],
                          ut[b].rearrange("p u e -> p (u e)"), start=True, stop=True).then_inc(s_h, 1)

            def out(s, b):
                for u in range(U):
                    pe.matmul(ps_o[:, u, 0:192], ut[b][:, u, :], m.w_o[:, :], start=True, stop=True)
                pe.wait_ge(s_lk, s + 1)
                for u in range(U):
                    pe.matmul(ps_s[:, u, :], ut[b][:, u, :], m.w_l[:, :], start=True, stop=False)
                    last = pe.matmul(ps_s[:, u, :], lk[b][:, u, :], m.w_s[:, :], start=False, stop=True)
                last.then_inc(s_so, 1)

            pe.sem_inc(s_prod, 2 * U)
            turn(0, 0)
            out(0, 0)
            with pe.Fori(0, STEPS // 2) as it:
                for b in range(2):
                    s = 2 * it + b
                    turn(s + 1, 1 - b)
                    pe.wait_ge(s_msg, s + 1)
                    out(s + 1, 1 - b)
                    pe.wait_ge(s_xm, s + 1)
                    for u in range(U):
                        pe.wait_ge(s_sum, s * U + u + 1)
                        pe.matmul(ps_a[u % 2][:, 0:MW], hot[b][:, u, :], msg[b][:, u, :], start=True, stop=True
                                  ).then_inc(s_prod, 1)

        @block.vector
        def _(dve):
            def lead(s, it, b):
                dve.wait_ge(s_x[b], 16 * U * it + 16 * U)
                dve.wait_ge(s_y, s + 1)
                dve.tensor_tensor(xr[:, :, :, :], rows[b][:, :, 128:320].rearrange("p u (c k) -> p u c k", k=3),
                                  m.unit[:, ds(s * U, U), None, :].to_broadcast([EP, U, 64, 3]), ALU.mult
                                  ).then_inc(s_xr, 1)
                dve.wait_ge(s_xr, s + 1)
                dve.tensor_reduce(rows[b][:, :, 0:64], xr[:, :, :, :], AX.X, ALU.add).then_inc(s_y, 1)

            def add(s):
                for u in range(U):
                    j = dve.value_load(m.node_tile[0:1, ds(s * U + u, 1)], min_val=0, max_val=NT - 1)
                    dve.wait_ge(s_prod, s * U + u + 1 + 2 * U)
                    dve.wait_ge(s_sum, s * U + u + 2)
                    dve.tensor_tensor(m.agg[:, j, 0:MW], m.agg[:, j, 0:MW], ps_a[u % 2][:, 0:MW], ALU.add
                                      ).then_inc(s_sum, 1)

            def body(s, next_it, b, first=False):
                count = [0]

                def ch(ins):
                    count[0] += 1
                    ins.then_inc(s_ch, 1)
                    dve.wait_ge(s_ch, s * OWN + count[0])

                lead(s + 1, next_it, 1 - b)
                dve.wait_ge(s_so, s + 1)
                ch(dve.tensor_reduce(mx[:, :], ps_s[:, 0:U, :], AX.X, ALU.max))
                dve.tensor_scalar(nm[:, :], mx[:, :], 0.0, -1.0, ALU.max, ALU.mult).then_inc(s_nm, 1)
                dve.wait_ge(s_prod, s * U + U)
                dve.tensor_tensor(hot[b][:, :, :], m.iota[:, None, 0:P].to_broadcast([EP, U, P]),
                                  m.rec[:, ds(s * U, U), R_LO:R_LO + 1].to_broadcast([EP, U, P]), ALU.is_equal)
                ch(dve.tensor_tensor(t1[:, :, :], ps_o[:, :, 128:192],
                                     m.unit2[:, ds(s * U, U), None].to_broadcast([EP, U, 64]), ALU.mult))
                ch(dve.tensor_tensor(t1[:, :, :], t1[:, :, :], ps_o[:, :, 0:64], ALU.add))
                if not first:
                    add(s - 1)
                dve.wait_ge(s_ex, s + 1)
                ch(dve.scalar_tensor_tensor(rz[:, :], en[:, :], 192.0, z[:, :], ALU.mult, ALU.add))
                ch(dve.reciprocal(rz[:, :], rz[:, :]))
                dve.tensor_tensor(al[:, :], en[:, :], rz[:, :], ALU.mult).then_inc(s_al, 1)
                dve.wait_ge(s_al, s + 1)
                ch(dve.tensor_tensor(ar[:, :, :], m.unit[:, ds(s * U, U), :],
                                     al[:, :, None].to_broadcast([EP, U, 3]), ALU.mult))
                ch(dve.tensor_tensor(t1[:, :, :], t1[:, :, :], rz[:, :, None].to_broadcast([EP, U, 64]), ALU.mult))
                ch(dve.tensor_tensor(msg[b][:, :, 0:64], t1[:, :, :], ex[:, :, :], ALU.mult))
                for u in range(U):
                    last = dve.tensor_tensor(msg[b][:, u, 256:448].rearrange("p (k c) -> p k c", k=3),
                                             ps_o[:, u, None, 64:128].to_broadcast([EP, 3, 64]),
                                             ar[:, u, :, None].to_broadcast([EP, 3, 64]), ALU.mult)
                    if u < U - 1:
                        continue
                    ch(last)
                dve.sem_inc(s_msg, 1)
                assert count[0] == OWN

            dve.memset(m.agg[:, :, :], 0.0).then_inc(s_sum, 2)
            dve.sem_inc(s_y, 1)
            lead(0, 0, 0)
            body(0, 0, 0, first=True)
            with dve.Fori(0, (STEPS - 2) // 2) as it:
                body(2 * it + 1, it + 1, 1)
                body(2 * it + 2, it + 1, 0)
            body(STEPS - 1, STEPS // 2, 1)
            add(STEPS - 1)


@stage
def build_geometric_weights(nc, m, a):
    c8 = 1.0 / 8.0
    ctp = float(1.0 / np.sqrt(128.0))
    kap = c8 * ctp * c8
    sq3 = float(np.sqrt(3.0))
    names = ["lin_src_w0", "lin_src_w1", "tp1_w00", "tp1_w11", "tp1_w01", "tp1_w10", "tp2_w00", "tp2_w11",
             "tp2_w01", "tp2_w10", "lin_hidden_w0", "lin_hidden_w1"]
    with ExitStack() as ctx:
        sem = Sems(nc, ctx)
        w = ctx.enter_context(nc.sbuf_tensor("gw_w", [64, 12, 64], F32))
        wt = ctx.enter_context(nc.sbuf_tensor("gw_wt", [64, 6, 64], F32))
        pr = ctx.enter_context(nc.sbuf_tensor("gw_pr", [64, 4, 64], F32))
        abt = ctx.enter_context(nc.sbuf_tensor("gw_abt", [64, 4, 64], F32))
        ab = ctx.enter_context(nc.sbuf_tensor("gw_ab", [64, 2, 64], F32))
        up = ctx.enter_context(nc.sbuf_tensor("gw_up", [64, 5, 64], F32))
        ps = [ctx.enter_context(nc.psum_tensor(f"gw_ps{i}", [64, 8, 64], F32)) for i in range(3)]
        s_in = sem("gw_in")
        s_tr = sem("gw_tr")
        s_ev = sem("gw_ev")
        s_z = sem("gw_z")
        s_mv = sem("gw_mv")
        block = ctx.enter_context(nc.Block())
        LS0, LS1, T00, T11, T01, T10, U00, U11, U01, U10, LH0, LH1 = range(12)

        @block.sync
        def _(sp):
            for i, n in enumerate(names):
                sp.dma_start(w[:, i, :], a["L1_gnn_" + n]).then_inc(s_in, 16)
            sp.wait_ge(s_ev, 7)
            sp.dma_start(m.w_h[64:128, :], up[:, 0, :]).then_inc(s_mv, 16)
            sp.dma_start(m.w_o[64:128, :], up[:, 1:4, :].rearrange("p c d -> p (c d)")).then_inc(s_mv, 16)
            sp.dma_start(m.w_d[64:128, 0, 64:128], m.w_d[0:64, 0, 0:64]).then_inc(s_mv, 16)
            sp.dma_start(m.w_l[64:128, :], up[:, 4, :]).then_inc(s_mv, 16)
            sp.wait_ge(s_mv, 64)

        @block.tensor
        def _(pe):
            i64 = m.ident[0:64, 0:64]
            pe.wait_ge(s_in, 16 * 12)
            for k, i in enumerate((LS0, LS1, T00, T11, T01, T10)):
                last = pe.transpose(ps[0][:, k, :], w[:, i, :], i64)
            last.then_inc(s_tr, 1)
            pe.wait_ge(s_ev, 1)
            for k, h in enumerate((LH0, LH0, LH1, LH1)):
                last = pe.matmul(ps[1][:, k, :], wt[:, 2 + k, :], w[:, h, :], start=True, stop=True)
            last.then_inc(s_tr, 1)
            pe.wait_ge(s_ev, 2)
            for k, l in enumerate((0, 1, 0, 1)):
                pe.matmul(ps[2][:, k, :], pr[:, k, :], wt[:, l, :], start=True, stop=True)
            for k in range(2):
                last = pe.matmul(ps[2][:, 4 + k, :], wt[:, k, :], pr[:, k, :], start=True, stop=True)
            last.then_inc(s_tr, 1)
            pe.wait_ge(s_ev, 4)
            prods = [(0, [(0, U00)]), (1, [(1, U00), (3, U11)]), (2, [(0, U01), (2, U10)]), (3, [(1, U01)]),
                     (4, [(2, U11)]), (5, [(3, U10)])]
            for slot, terms in prods:
                for n, (k, u) in enumerate(terms):
                    pe.matmul(ps[1][:, slot, :], abt[:, k, :], w[:, u, :], start=n == 0,
                              stop=n == len(terms) - 1)
            for k in range(2):
                last = pe.matmul(ps[1][:, 6 + k, :], abt[:, k, :], m.w_s[:, :], start=True, stop=True)
            last.then_inc(s_tr, 1)

        @block.vector
        def _(dve):
            dve.wait_ge(s_tr, 1)
            dve.tensor_copy(wt[:, :, :], ps[0][:, 0:6, :]).then_inc(s_ev, 1)
            dve.wait_ge(s_tr, 2)
            dve.tensor_copy(pr[:, :, :], ps[1][:, 0:4, :]).then_inc(s_ev, 1)
            dve.wait_ge(s_tr, 3)
            dve.tensor_scalar(abt[:, :, :], ps[2][:, 0:4, :], kap, None, ALU.mult).then_inc(s_ev, 1)
            dve.tensor_scalar(ab[:, :, :], ps[2][:, 4:6, :], kap, None, ALU.mult).then_inc(s_ev, 1)
            dve.memset(m.w_d[:, :, :], 0.0).then_inc(s_z, 1)
            dve.wait_ge(s_tr, 4)
            dve.wait_ge(s_ev, 4)
            dve.wait_ge(s_z, 1)
            dve.tensor_copy(up[:, 0, :], ab[:, 0, :])
            dve.tensor_scalar(up[:, 1, :], ps[1][:, 0, :], ctp, None, ALU.mult)
            dve.tensor_scalar(up[:, 2, :], ps[1][:, 2, :], sq3 * ctp, None, ALU.mult)
            dve.tensor_scalar(up[:, 4, :], ps[1][:, 6, :], 0.01, None, ALU.mult)
            dve.tensor_scalar(m.w_s[:, :], m.w_s[:, :], 0.99, None, ALU.mult)
            dve.tensor_scalar(up[:, 3, :], ps[1][:, 4, :], sq3 * ctp, None, ALU.mult).then_inc(s_ev, 1)
            dve.tensor_copy(m.w_h[0:64, :], ab[:, 1, :])
            dve.tensor_scalar(m.w_o[0:64, 0:64], ps[1][:, 1, :], ctp, None, ALU.mult)
            dve.tensor_scalar(m.w_o[0:64, 64:128], ps[1][:, 3, :], sq3 * ctp, None, ALU.mult)
            dve.memset(m.w_o[0:64, 128:192], 0.0).then_inc(s_ev, 1)
            dve.tensor_scalar(m.w_l[0:64, :], ps[1][:, 7, :], 0.01, None, ALU.mult)
            dve.tensor_scalar(m.w_d[0:64, 0, 0:64], ps[1][:, 5, :], ctp, None, ALU.mult)
            dve.tensor_scalar(m.w_d[0:64, 1, 128:192], ps[1][:, 5, :], ctp, None, ALU.mult).then_inc(s_ev, 1)


@stage
def feed_forward(nc, m, tag, act_func, first, rest, gate):
    n_rest = 0 if rest is None else rest[0].shape[0]
    with ExitStack() as ctx:
        sem = Sems(nc, ctx)

        def sb(name, shape, dt=F32):
            return ctx.enter_context(nc.sbuf_tensor(f"{name}_{tag}", shape, dt))

        w1 = [sb(f"w1{b}", [128, 2, FF]) for b in range(2)]
        w2 = [sb(f"w2{b}", [128, NF, D]) for b in range(2)]
        b1 = [sb(f"b1{b}", [128, NF]) for b in range(2)]
        b2 = [sb(f"b2{b}", [P, D]) for b in range(2)]
        hs = sb("hs", [128, NF, G * P])
        t = sb("t", [P, G, D])
        ps_h = [ctx.enter_context(nc.psum_tensor(f"ps_h{b}_{tag}", [128, 1024], F32)) for b in range(2)]
        ps_y = ctx.enter_context(nc.psum_tensor(f"ps_y_{tag}", [128, 6, 256], F32))
        s_w = [sem(f"s_w{b}_{tag}") for b in range(2)]
        s_h = sem(f"s_h_{tag}")
        s_g = sem(f"s_g_{tag}")
        s_y = sem(f"s_y_{tag}")
        s_t = sem(f"s_t_{tag}")
        s_ch = sem(f"s_ch_{tag}")
        s_exp = sem(f"s_exp_{tag}")
        block = ctx.enter_context(nc.Block())

        @block.sync
        def _(sp):
            def load(w, b):
                for dst, src in zip((w1[b][:, :, :], w2[b][:, :, :], b1[b][:, :], b2[b][:, :]), w):
                    sp.dma_start(dst, src).then_inc(s_w[b], 16)

            with nc.allow_non_contiguous_dma(reason="biases down the partitions, 4 KB each"):
                load([first[0].rearrange("(k p) f -> p k f", p=128), first[2].rearrange("(c p) d -> p c d", p=128),
                      first[1].rearrange("(c p) -> p c", p=128),
                      first[3].rearrange("(o d) -> o d", o=1).to_broadcast([P, D])], 0)
                if rest is not None:
                    def load_rest(e, b):
                        load([rest[0][ds(e, 1)].rearrange("o (k p) f -> p (o k) f", p=128),
                              rest[2][ds(e, 1)].rearrange("o (c p) d -> p (o c) d", p=128),
                              rest[1][ds(e, 1)].rearrange("o (c p) -> p (o c)", p=128),
                              rest[3][ds(e, 1)].to_broadcast([P, D])], b)

                    load_rest(0, 1)
                    with sp.Fori(1, n_rest // 2) as it:
                        sp.wait_ge(s_exp, 2 * it - 1)
                        load_rest(2 * it - 1, 0)
                        sp.wait_ge(s_exp, 2 * it)
                        load_rest(2 * it, 1)
                    sp.wait_ge(s_exp, n_rest - 1)
                    load_rest(n_rest - 1, 0)

        def networks(eng, body):
            with eng.Fori(0, NG) as g:
                body(0, 0, 0, g)
            if rest is not None:
                with eng.Fori(0, n_rest // 2) as it:
                    with eng.Fori(0, NG) as g:
                        body(2 * it + 1, it, 1, g)
                    with eng.Fori(0, NG) as g:
                        body(2 * it + 2, it + 1, 0, g)

        @block.tensor
        def _(pe):
            pe.sem_inc(s_g, 2)

            def body(e, it, b, g):
                n = e * NG + g
                pe.wait_ge(s_w[b], 64 * it + 64)
                for c in range(NF):
                    pe.wait_ge(s_g, n * NF + c + 1)
                    for i in range(2):
                        for k in range(2):
                            last = pe.matmul(ps_h[c % 2][:, 512 * i:512 * i + SPLIT[i + 1] - SPLIT[i]],
                                             w1[b][:, k, c * 128:(c + 1) * 128],
                                             m.h_t[:, k, ds(g * G * P + SPLIT[i], SPLIT[i + 1] - SPLIT[i])],
                                             start=k == 0, stop=k == 1)
                    last.then_inc(s_h, 1)
                pe.wait_ge(s_t, n + 1)
                pe.wait_ge(s_g, n * NF + NF + 2)
                for u in range(G):
                    for c in range(NF):
                        last = pe.matmul(ps_y[0:P, u, :], hs[:, c, u * P:(u + 1) * P], w2[b][:, c, :],
                                         start=c == 0, stop=c == NF - 1)
                last.then_inc(s_y, 1)

            networks(pe, body)

        @block.scalar
        def _(act):
            act.sem_inc(s_y, 1)

            def body(e, it, b, g):
                n = e * NG + g
                act.wait_ge(s_w[b], 64 * it + 64)
                act.wait_ge(s_y, n + 1)
                for c in range(NF):
                    act.wait_ge(s_h, n * NF + c + 1)
                    for i in range(2):
                        last = act.activation(hs[:, c, SPLIT[i]:SPLIT[i + 1]],
                                              ps_h[c % 2][:, 512 * i:512 * i + SPLIT[i + 1] - SPLIT[i]],
                                              act_func, bias=b1[b][:, c:c + 1])
                    last.then_inc(s_g, 1)

            networks(act, body)

        @block.vector
        def _(dve):
            dve.sem_inc(s_t, 1)

            def body(e, it, b, g):
                n = e * NG + g
                dve.wait_ge(s_w[b], 64 * it + 64)
                dve.wait_ge(s_y, n + 2)
                dve.tensor_tensor(t[:, :, :], ps_y[0:P, 0:G, :], b2[b][:, None, :].to_broadcast([P, G, D]), ALU.add
                                  ).then_inc(s_t, 1)
                dve.wait_ge(s_t, n + 2)
                f = gate(e, g)
                if f is not None:
                    dve.tensor_tensor(t[:, :, :], t[:, :, :], f.to_broadcast([P, G, D]), ALU.mult).then_inc(s_ch, 1)
                else:
                    dve.sem_inc(s_ch, 1)
                dve.wait_ge(s_ch, 2 * n + 1)
                x = m.x[:, ds(g * G, G), :]
                dve.tensor_tensor(x, x, t[:, :, :], ALU.add).then_inc(s_ch, 1)
                dve.wait_ge(s_ch, 2 * n + 2)

            with dve.Fori(0, NG) as g:
                body(0, 0, 0, g)
            dve.sem_inc(s_exp, 1)
            if rest is not None:
                with dve.Fori(0, n_rest // 2) as it:
                    with dve.Fori(0, NG) as g:
                        body(2 * it + 1, it, 1, g)
                    dve.sem_inc(s_exp, 1)
                    with dve.Fori(0, NG) as g:
                        body(2 * it + 2, it + 1, 0, g)
                    dve.sem_inc(s_exp, 1)


@stage
def build_top(nc, m):
    with ExitStack() as ctx:
        sem = Sems(nc, ctx)
        ps = ctx.enter_context(nc.psum_tensor("t_ps", [NT, 512], F32))
        wt = ctx.enter_context(nc.sbuf_tensor("t_wt", [NT, P], F32))
        row = ctx.enter_context(nc.sbuf_tensor("t_row", [P, N], F32))
        junk = ctx.enter_context(nc.sbuf_tensor("t_junk", [P, 4, N], BF16))
        part = ctx.enter_context(nc.sbuf_tensor("t_part", [P, NT, 4], F32))
        rank = ctx.enter_context(nc.sbuf_tensor("t_rank", [P, NT], F32))
        s_pe = sem("t_pe")
        s_wt = sem("t_wt")
        s_d = sem("t_d")
        s_r = sem("t_r")
        s_part = sem("t_part")
        s_ch = sem("t_ch")
        block = ctx.enter_context(nc.Block())

        @block.tensor
        def _(pe):
            pe.transpose(ps[:, 0:P], m.w[:, :], m.ident[0:P, 0:P]).then_inc(s_pe, 1)

        @block.sync
        def _(sp):
            sp.wait_ge(s_wt, 1)
            sp.dma_start(m.wrow_d.rearrange("(j p) -> j p", p=P), wt[:, :]).then_inc(s_d, 16)
            sp.wait_ge(s_d, 16)
            sp.dma_start(row[:, :], m.wrow_d.rearrange("(o n) -> o n", o=1).to_broadcast([P, N])).then_inc(s_r, 16)

        @block.vector
        def _(dve):
            dve.wait_ge(s_pe, 1)
            dve.tensor_copy(wt[:, :], ps[:, 0:P]).then_inc(s_wt, 1)
            dve.memset(part[:, :, :], 0.0).then_inc(s_part, 1)
            dve.wait_ge(s_part, 1)
            dve.wait_ge(s_r, 16)
            for j in range(NT):
                a, b = j * P, (j + 1) * P
                mine = m.w[:, j:j + 1]
                dve.wait_ge(s_part, j + 1)
                if j:
                    dve.tensor_scalar(junk[:, 0, 0:a], row[:, 0:a], mine, None, ALU.is_ge, ALU.add,
                                      accum_out=part[:, j, 0:1])
                if j < NT - 1:
                    dve.tensor_scalar(junk[:, 1, b:N], row[:, b:N], mine, None, ALU.is_gt, ALU.add,
                                      accum_out=part[:, j, 1:2])
                dve.tensor_scalar(junk[:, 2, a:b], row[:, a:b], mine, None, ALU.is_gt, ALU.add,
                                  accum_out=part[:, j, 2:3])
                dve.scalar_tensor_tensor(junk[:, 3, 0:P], row[:, a:b], mine,
                                         m.before[0:P, 0:P], ALU.is_equal, ALU.mult, accum_out=part[:, j, 3:4]
                                         ).then_inc(s_part, 1)
            dve.wait_ge(s_part, NT + 1)
            ch = Chain(dve, s_ch)
            ch(dve.tensor_reduce(rank[:, :], part[:, :, :], AX.X, ALU.add))
            ch(dve.tensor_scalar(rank[:, :], rank[:, :], float(KEPT), None, ALU.is_lt))
            ch(dve.tensor_tensor(m.w[:, :], m.w[:, :], rank[:, :], ALU.mult))


@stage
def build_router(nc, m):
    with ExitStack() as ctx:
        sem = Sems(nc, ctx)

        def sb(name, shape):
            return ctx.enter_context(nc.sbuf_tensor(f"r_{name}", shape, F32))

        mx = sb("mx", [P, NT])
        p = sb("p", [P, NT, NE])
        sm = sb("sm", [P, NT])
        cmp_ = sb("cmp", [P, NT, NE])
        rank = sb("rank", [P, NT, NE])
        s_ch = sem("r_ch")
        s_ex = sem("r_ex")
        block = ctx.enter_context(nc.Block())
        shape = [P, NT, NE]

        @block.scalar
        def _(act):
            act.wait_ge(s_ch, 2)
            act.activation(p[:, :, :], m.mask[:, :, :], ACT.Exp).then_inc(s_ex, 1)

        @block.vector
        def _(dve):
            ch = Chain(dve, s_ch)
            ch(dve.tensor_reduce(mx[:, :], m.mask[:, :, :], AX.X, ALU.max))
            ch(dve.tensor_tensor(m.mask[:, :, :], m.mask[:, :, :], mx[:, :, None].to_broadcast(shape), ALU.subtract))
            dve.wait_ge(s_ex, 1)
            ch(dve.tensor_reduce(sm[:, :], p[:, :, :], AX.X, ALU.add))
            ch(dve.reciprocal(sm[:, :], sm[:, :]))
            ch(dve.tensor_tensor(p[:, :, :], p[:, :, :], sm[:, :, None].to_broadcast(shape), ALU.mult))
            for e in range(NE):
                if e:
                    ch(dve.tensor_tensor(cmp_[:, :, 0:e], p[:, :, 0:e], p[:, :, e:e + 1].to_broadcast([P, NT, e]),
                                         ALU.is_ge))
                ch(dve.tensor_tensor(cmp_[:, :, e:NE], p[:, :, e:NE], p[:, :, e:e + 1].to_broadcast([P, NT, NE - e]),
                                     ALU.is_gt))
                ch(dve.tensor_reduce(rank[:, :, e], cmp_[:, :, :], AX.X, ALU.add))
            ch(dve.tensor_scalar(rank[:, :, :], rank[:, :, :], 2.0, None, ALU.is_lt))
            ch(dve.tensor_tensor(p[:, :, :], p[:, :, :], rank[:, :, :], ALU.mult))
            ch(dve.tensor_reduce(sm[:, :], p[:, :, :], AX.X, ALU.add))
            ch(dve.reciprocal(sm[:, :], sm[:, :]))
            ch(dve.tensor_tensor(m.mask[:, :, :], p[:, :, :], sm[:, :, None].to_broadcast(shape), ALU.mult))


@stage
def move(nc, tag, loads):
    with ExitStack() as ctx:
        sem = Sems(nc, ctx)
        s = [sem(f"mv_{tag}{i}") for i in range(2)]
        block = ctx.enter_context(nc.Block())

        def issue(eng, mine, s_mine):
            for dst, src in mine:
                eng.dma_start(dst, src).then_inc(s_mine, 16)
            if mine:
                eng.wait_ge(s_mine, 16 * len(mine))

        @block.sync
        def _(sp):
            issue(sp, loads[0::2], s[0])

        @block.scalar
        def _(act):
            issue(act, loads[1::2], s[1])


class Memory:
    pass


def build(nc, a, out):
    m = Memory()
    with ExitStack() as top:
        def sb(name, shape, dt=F32, to=top):
            return to.enter_context(nc.sbuf_tensor(name, shape, dt))

        def dram(name, shape, dt=F32):
            return nc.dram_tensor(name, shape, dt, kind="Internal").ap()

        m.rec_d = dram("rec_d", [TX * EP, REC])
        m.row_d = dram("row_d", [2, E])
        m.k_d = dram("k_d", [N, D])
        m.v_d = dram("v_d", [N, D])
        m.h_d = dram("h_d", [N, D])
        m.ends_d = dram("ends_d", [4 * NBLK, 128])
        m.carry_d = dram("carry_d", [2 * NBLK, 128])
        m.wrow_d = dram("wrow_d", [N])

        m.ident = sb("ident", [128, 128])
        m.ident_b = sb("ident_b", [128, 128], BF16)
        m.ones = sb("ones", [128, 128])
        m.before = sb("before", [128, 128])
        m.after = sb("after", [128, 128])
        m.iota_i = sb("iota_i", [128, T], I32)
        m.iota = sb("iota", [128, T])
        m.part_i = sb("part_i", [128, 1], I32)
        m.part = sb("part", [128, 1])
        m.node_tile = sb("node_tile", [1, T], I32)
        m.x = sb("x", [P, NT, D])
        m.h = sb("h", [P, NT, D])
        m.agg = sb("agg", [P, NT, 448])
        m.rec = sb("rec", [EP, TX, REC])
        m.src = sb("src", [EP, TX], U32)
        m.unit = sb("unit", [EP, TX, 3])
        m.unit2 = sb("unit2", [EP, TX])
        rows = lambda ap: ap.rearrange("(j p) d -> p j d", p=P)
        vec = lambda ap, n=P: ap.rearrange("(o d) -> o d", o=1).to_broadcast([n, ap.shape[0]])
        half = lambda ap: ap.rearrange("(k p) n -> p k n", p=128)

        build_constants(nc, m)
        build_sort(nc, m, a)
        build_reload(nc, m)

        with ExitStack() as l0:
            m.v = sb("v", [P, NT, D], to=l0)
            m.s = sb("s", [EP, T, H], to=l0)
            m.rel = sb("rel", [NREL, HD], to=l0)
            l0q = l0.enter_context(ExitStack())
            m.q = sb("q", [P, NT, D], to=l0q)
            move(nc, "x", [(m.x[:, :, :], rows(a["x"])), (m.rel[:, :], a["L0_gnn_rel_w"])])
            layer_norm(nc, m, "n0", m.x, m.h)
            with ExitStack() as c1:
                qe = sb("qe", [P, D], to=c1)
                bias = [sb(f"bias{i}", [P, D], to=c1) for i in range(3)]
                wqkv = [sb(f"wqkv{i}", [128, 2, D], to=c1) for i in range(3)]
                move(nc, "qkv", [(qe[:, :], vec(a["L0_gnn_query_emb"]))]
                     + [(bias[i][:, :], vec(a["L0_gnn_b" + c])) for i, c in enumerate("qkv")]
                     + [(wqkv[i][:, :, :], half(a["L0_gnn_W" + c])) for i, c in enumerate("qkv")])
                scale_qkv(nc, m, qe, bias[0])

                def enhance(dve, g, slot, ch):
                    return dve.tensor_tensor(slot[:, :, :], m.h[:, ds(g * G, G), :],
                                             qe[:, None, :].to_broadcast([P, G, D]), ALU.add)

                def take(dve, g, c, ps, ch):
                    b = bias[c][:, None, :].to_broadcast([P, G, D])
                    if c == 0:
                        return dve.scalar_tensor_tensor(m.q[:, ds(g * G, G), :], ps, 0.125, b, ALU.mult, ALU.add)
                    to = m.agg[:, ds(g * G, G), 0:D] if c == 1 else m.v[:, ds(g * G, G), :]
                    return dve.tensor_tensor(to, ps, b, ALU.add)

                project(nc, m, "qkv", enhance, wqkv, D, take)
            move(nc, "kv", [(rows(m.k_d), m.agg[:, :, 0:D]), (rows(m.v_d), m.v[:, :, :])])
            build_scores(nc, m)
            l0q.close()
            build_weights(nc, m)
            build_values(nc, m)
            m.q = sb("y", [P, NT, D], to=l0)
            with ExitStack() as c1:
                rd = sb("rd", [P, NT, H], to=c1)
                dz = sb("dz", [P, NT, H], to=c1)
                bo = sb("bo", [P, D], to=c1)
                wo = sb("wo", [128, 2, D], to=c1)
                tmp = sb("tmp", [P, G, D], to=c1)
                move(nc, "wo", [(bo[:, :], vec(a["L0_gnn_bo"])), (wo[:, :, :], half(a["L0_gnn_Wo"]))])
                divide_sums(nc, m, rd, dz)
                hd = lambda ap: ap.rearrange("p u (h d) -> p u h d", h=H)

                def normalise(dve, g, slot, ch):
                    gs = ds(g * G, G)
                    shape = [P, G, H, HD]
                    ch(dve.tensor_tensor(hd(slot[:, :, :]), hd(m.agg[:, gs, 0:D]),
                                         rd[:, gs, :, None].to_broadcast(shape), ALU.mult))
                    ch(dve.tensor_tensor(hd(tmp[:, :, :]), hd(m.v[:, gs, :]), dz[:, gs, :, None].to_broadcast(shape),
                                         ALU.mult))
                    return dve.tensor_tensor(slot[:, :, :], slot[:, :, :], tmp[:, :, :], ALU.add)

                def residual(dve, g, c, ps, ch):
                    ch(dve.tensor_tensor(tmp[:, :, :], ps, bo[:, None, :].to_broadcast([P, G, D]), ALU.add))
                    return dve.tensor_tensor(m.q[:, ds(g * G, G), :], tmp[:, :, :], m.h[:, ds(g * G, G), :], ALU.add)

                project(nc, m, "wo", normalise, [wo], D, residual, own=3)
            with ExitStack() as c1:
                gb = [sb(f"gb{i}", [P, D], to=c1) for i in range(2)]
                move(nc, "gb", [(gb[0][:, :], vec(a["L0_gnn_gamma"])), (gb[1][:, :], vec(a["L0_gnn_beta"]))])
                layer_norm(nc, m, "n1", m.q, m.v, gb[0], gb[1])
            add_all(nc, "l0", [(m.x[:, :, :], m.x[:, :, :], m.v[:, :, :])])

        layer_norm(nc, m, "n2", m.x, m.h)
        with ExitStack() as c0:
            m.h_t = sb("h_t0", [128, 2, N], to=c0)
            m.w = sb("w", [P, NT], to=c0)
            with ExitStack() as c1:
                wr = sb("wr", [128, 2, 1], to=c1)
                br = sb("br", [P, 1], to=c1)
                with nc.allow_non_contiguous_dma(reason="256 words, once"):
                    move(nc, "wr", [(wr[:, :, :], half(a["L0_ffn_wr"])), (br[:, :], vec(a["L0_ffn_br"]))])

                def copy_rows(dve, g, slot, ch):
                    return dve.tensor_copy(slot[:, :, :], m.h[:, ds(g * G, G), :])

                def keep(g, k):
                    return m.h_t[:, k, ds(g * G * P, G * P)].rearrange("p (u n) -> p u n", u=G)

                def take_w(dve, g, c, ps, ch):
                    return dve.tensor_scalar(m.w[:, ds(g * G, G)], ps[:, :, 0], br[:, 0:1], None, ALU.add)

                project(nc, m, "wr", copy_rows, [wr], 1, take_w, keep=keep)
            build_top(nc, m)
            add_all(nc, "f0", [(m.x[:, :, :], m.x[:, :, :], m.h[:, :, :])])
            feed_forward(nc, m, "f0", ACT.Gelu_apprx_tanh,
                         [a["L0_ffn_w1"], a["L0_ffn_b1"], a["L0_ffn_w2"], a["L0_ffn_b2"]], None,
                         lambda e, g: m.w[:, ds(g * G, G), None])

        layer_norm(nc, m, "n3", m.x, m.h)
        with ExitStack() as c0:
            m.w_h = sb("w_h", [128, 64], to=c0)
            m.w_o = sb("w_o", [128, 192], to=c0)
            m.w_d = sb("w_d", [128, 2, 192], to=c0)
            m.w_s = sb("w_s", [64, 64], to=c0)
            m.w_l = sb("w_l", [128, 64], to=c0)
            move(nc, "h", [(rows(m.h_d), m.h[:, :, :]), (m.w_s[:, :], a["L1_gnn_lin_scalar_w"])])
            scale_logits(nc, m)
            build_geometric_weights(nc, m, a)
            build_geometric(nc, m)
            with ExitStack() as c1:
                tmp = sb("tmp1", [P, G, D], to=c1)

                def vectors(dve, g, slot, ch):
                    ch(dve.memset(slot[:, :, 192:256], 0.0))
                    return dve.tensor_copy(slot[:, :, 0:192].rearrange("p u (k c) -> p u k c", k=3),
                                           m.agg[:, ds(g * G, G), 64:256].rearrange("p u (c k) -> p u k c", k=3))

                def joined(dve, g, c, ps, ch):
                    gs = ds(g * G, G)
                    ch(dve.tensor_copy(tmp[:, :, 0:64], m.agg[:, gs, 0:64]))
                    ch(dve.tensor_tensor(tmp[:, :, 64:256].rearrange("p u (c k) -> p u k c", k=3),
                                         ps.rearrange("p u (k c) -> p u k c", k=3),
                                         m.agg[:, gs, 256:448].rearrange("p u (k c) -> p u k c", k=3), ALU.add))
                    ch(dve.tensor_tensor(tmp[:, :, :], tmp[:, :, :], m.h[:, gs, :], ALU.add))
                    return dve.tensor_tensor(m.x[:, gs, :], m.x[:, gs, :], tmp[:, :, :], ALU.add)

                project(nc, m, "wd", vectors, [m.w_d], 192, joined, own=4)

        layer_norm(nc, m, "n4", m.x, m.h)
        with ExitStack() as c0:
            m.h_t = sb("h_t1", [128, 2, N], to=c0)
            m.mask = sb("mask1", [P, NT, NE], to=c0)
            with ExitStack() as c1:
                wr = sb("wr1", [128, 2, NE], to=c1)
                move(nc, "wr1", [(wr[:, :, :], half(a["L1_ffn_Wr"]))])

                def take_l(dve, g, c, ps, ch):
                    return dve.tensor_copy(m.mask[:, ds(g * G, G), :], ps)

                def keep1(g, k):
                    return m.h_t[:, k, ds(g * G * P, G * P)].rearrange("p (u n) -> p u n", u=G)

                project(nc, m, "wr1", lambda dve, g, slot, ch: dve.tensor_copy(slot[:, :, :], m.h[:, ds(g * G, G), :]),
                        [wr], NE, take_l, keep=keep1)
            build_router(nc, m)
            feed_forward(nc, m, "f1", ACT.Gelu,
                         [a["L1_ffn_W1s"], a["L1_ffn_b1s"], a["L1_ffn_W2s"], a["L1_ffn_b2s"]],
                         [a["L1_ffn_W1p"], a["L1_ffn_b1p"], a["L1_ffn_W2p"], a["L1_ffn_b2p"]],
                         lambda e, g: None if known(e) else m.mask[:, ds(g * G, G), ds(e - 1, 1)])
        move(nc, "out", [(rows(out), m.x[:, :, :])])


@stage
def scale_qkv(nc, m, qe, bq):
    with ExitStack() as ctx:
        s = Sems(nc, ctx)("sc_qkv")
        block = ctx.enter_context(nc.Block())

        @block.vector
        def _(dve):
            ch = Chain(dve, s)
            ch(dve.tensor_scalar(qe[:, :], qe[:, :], 0.1, None, ALU.mult))
            ch(dve.tensor_scalar(bq[:, :], bq[:, :], 0.125, None, ALU.mult))
            ch(dve.tensor_scalar(m.rel[:, :], m.rel[:, :], 0.2, None, ALU.mult))


@stage
def scale_logits(nc, m):
    with ExitStack() as ctx:
        s = Sems(nc, ctx)("sc_log")
        block = ctx.enter_context(nc.Block())

        @block.vector
        def _(dve):
            Chain(dve, s)(dve.tensor_scalar(m.w_s[:, :], m.w_s[:, :], 0.125, None, ALU.mult))


@stage
def divide_sums(nc, m, rd, dz):
    with ExitStack() as ctx:
        s = Sems(nc, ctx)("sc_div")
        block = ctx.enter_context(nc.Block())

        @block.vector
        def _(dve):
            ch = Chain(dve, s)
            ch(dve.tensor_scalar(dz[:, :, :], m.agg[:, :, D:D + H], 0.0, None, ALU.is_equal))
            ch(dve.tensor_tensor(rd[:, :, :], m.agg[:, :, D:D + H], dz[:, :, :], ALU.add))
            ch(dve.reciprocal(rd[:, :, :], rd[:, :, :]))


_INS = ["x", "src", "dst", "edge_attr_3", "edge_type_64", "L0_gnn_query_emb", "L0_gnn_Wq", "L0_gnn_bq", "L0_gnn_Wk",
        "L0_gnn_bk", "L0_gnn_Wv", "L0_gnn_bv", "L0_gnn_rel_w", "L0_gnn_Wo", "L0_gnn_bo", "L0_gnn_gamma",
        "L0_gnn_beta", "L0_ffn_wr", "L0_ffn_br", "L0_ffn_w1", "L0_ffn_b1", "L0_ffn_w2", "L0_ffn_b2",
        "L1_gnn_lin_src_w0", "L1_gnn_lin_src_w1", "L1_gnn_tp1_w00", "L1_gnn_tp1_w11", "L1_gnn_tp1_w01",
        "L1_gnn_tp1_w10", "L1_gnn_tp2_w00", "L1_gnn_tp2_w11", "L1_gnn_tp2_w01", "L1_gnn_tp2_w10",
        "L1_gnn_lin_hidden_w0", "L1_gnn_lin_hidden_w1", "L1_gnn_lin_scalar_w", "L1_ffn_Wr", "L1_ffn_W1s",
        "L1_ffn_b1s", "L1_ffn_W2s", "L1_ffn_b2s", "L1_ffn_W1p", "L1_ffn_b1p", "L1_ffn_W2p", "L1_ffn_b2p"]


def kernel(**inputs):
    import numpy as _np
    import concourse.bacc as _bacc
    from concourse import mybir as _mybir
    from concourse.bass_utils import run_bass_kernel_spmd as _run

    nc = _bacc.Bacc("TRN2", target_bir_lowering=False, num_devices=1)
    arrays, args = {}, {}
    for name in _INS:
        x = _np.ascontiguousarray(inputs[name])
        arrays[f"in_{name}"] = x
        args[name] = nc.dram_tensor(f"in_{name}", x.shape, _mybir.dt.from_np(x.dtype), kind="ExternalInput").ap()
    out = nc.dram_tensor("out_0", (N, D), _mybir.dt.float32, kind="ExternalOutput").ap()
    build(nc, args, out)
    r = _run(nc, [arrays], core_ids=[0])
    return r.results[0]["out_0"]
```

```python
from contextlib import ExitStack

import numpy as np
import concourse.bass as bass
from concourse import mybir

ALU = mybir.AluOpType
ACT = mybir.ActivationFunctionType
F32 = mybir.dt.float32
BF16 = mybir.dt.bfloat16
I32 = mybir.dt.int32
U32 = mybir.dt.uint32
AX = mybir.AxisListType
ds = bass.ds

N = 3125
E = 50000
D = 256
P = 125
NT = N // P
G = 5
NG = NT // G
H, HD = 4, 64
NREL = 64
EP = 128
U = 4
CH = U * P
SORT_STEPS = E // CH
T = -(-((E + NT * (EP - 1)) // EP) // (2 * U)) * 2 * U
STEPS = T // U
TX = T + 8 * U
REC = 8
R_SRC, R_LO, R_TYPE, R_VEC, R_DST = 0, 1, 2, 3, 6
BIG = 1.0e30
FF = 1024
NF = FF // 128
NE = 8
KEPT = max(1, N // 2) - 1
EPS = 1e-5
TOP = 2
ER = 4
ET = -(-((N * TOP + NE * (EP - 1)) // EP) // ER) * ER
ETX = ET + 2 * ER
NBLK = T * H // 128
SPLIT = (0, 320, G * P)


class Sems:

    def __init__(self, nc, ctx):
        self.nc, self.ctx = nc, ctx

    def __call__(self, name):
        return self.nc.alloc_semaphore(name)


def stage(build_stage):
    def staged(nc, *args, **kw):
        with nc.cleanup_on_exit():
            build_stage(nc, *args, **kw)
    return staged


class Chain:

    def __init__(self, eng, sem):
        self.eng, self.sem, self.n = eng, sem, 0

    def __call__(self, ins):
        self.n += 1
        ins.then_inc(self.sem, 1)
        self.eng.wait_ge(self.sem, self.n)


@stage
def build_constants(nc, m):
    with ExitStack() as ctx:
        sem = Sems(nc, ctx)
        iota_i = ctx.enter_context(nc.sbuf_tensor("iota_i", [128, T], I32))
        part_i = ctx.enter_context(nc.sbuf_tensor("part_i", [128, 1], I32))
        s_made = sem("c_made")
        s_cast = sem("c_cast")
        block = ctx.enter_context(nc.Block())

        @block.gpsimd
        def _(pool):
            ch = Chain(pool, s_made)
            ch(pool.memset(m.ones[:, :], 1.0))
            ch(pool.iota(iota_i[:, :], pattern=[[1, T]], base=0, channel_multiplier=0))
            ch(pool.iota(part_i[:, :], pattern=[[0, 1]], base=0, channel_multiplier=1))
            ch(pool.memset(m.ident[:, :], 0.0))
            ch(pool.affine_select(out=m.ident[:, :], in_=m.ident[:, :], compare_op=ALU.not_equal, fill=1.0,
                                  base=0, pattern=[[-1, 128]], channel_multiplier=1))
            ch(pool.affine_select(out=m.before[:, :], in_=m.ones[:, :], compare_op=ALU.is_gt, fill=0.0,
                                  base=0, pattern=[[-1, 128]], channel_multiplier=1))
            ch(pool.affine_select(out=m.after[:, :], in_=m.ones[:, :], compare_op=ALU.is_gt, fill=0.0,
                                  base=0, pattern=[[1, 128]], channel_multiplier=-1))

        @block.vector
        def _(dve):
            ch = Chain(dve, s_cast)
            dve.wait_ge(s_made, 7)
            ch(dve.tensor_copy(m.iota[:, :], iota_i[:, :]))
            ch(dve.tensor_copy(m.part[:, :], part_i[:, :]))
            ch(dve.tensor_copy(m.ident_b[:, :], m.ident[:, :]))


@stage
def build_sort(nc, m, a):
    with ExitStack() as ctx:
        sem = Sems(nc, ctx)

        def sb(name, shape, dt=F32):
            return ctx.enter_context(nc.sbuf_tensor(name, shape, dt))

        Q = 100
        NB = E // (Q * P)
        rec_in = sb("rec_in", [P, SORT_STEPS * U, REC])
        hi = sb("hi", [P, SORT_STEPS * U])
        lo = sb("lo", [P, SORT_STEPS * U])
        hi_hot = sb("hi_hot", [P, SORT_STEPS * U, NT], BF16)
        lo_hot = [sb(f"lo_hot{i}", [P, U, P], BF16) for i in range(2)]
        start = sb("start", [P, NT])
        row_d = m.row_d

        with ExitStack() as c1:
            def sb1(name, shape, dt=F32):
                return c1.enter_context(nc.sbuf_tensor(name, shape, dt))

            sem1 = Sems(nc, c1)
            nat_i = [sb1(f"nat_i{i}", [Q, NB, P], I32) for i in range(3)]
            nat_v = sb1("nat_v", [Q, NB, 3 * P])
            nat_f = [sb1(f"nat_f{i}", [Q, NB, P]) for i in range(3)]
            nat_hi = [sb1(f"nat_hi{i}", [Q, NB, P]) for i in range(2)]
            nat_lo = sb1("nat_lo", [Q, NB, P])
            empty = sb1("empty", [EP, TX, REC])
            ps = [c1.enter_context(nc.psum_tensor(f"ps_f{i}", [P, 512], F32)) for i in range(8)]
            s_in = [sem1(f"s_in{i}") for i in range(4)]
            s_flt = sem1("s_flt")
            s_lo = sem1("s_lo")
            s_tr = sem1("s_tr")
            s_empty = sem1("s_empty")
            s_row = sem1("s_row")
            s_fill = sem1("s_fill")
            s_rec = sem1("s_rec")
            s_hot = sem1("s_hot")
            block = c1.enter_context(nc.Block())
            cols = [(nat_f[1], None, R_SRC), (nat_lo, None, R_LO), (nat_f[2], None, R_TYPE),
                    (nat_v, 0, R_VEC), (nat_v, 1, R_VEC + 1), (nat_v, 2, R_VEC + 2), (nat_f[0], None, R_DST),
                    (nat_hi[0], None, None)]

            @block.sync
            def _(sp):
                for i, x in enumerate((a["dst"], a["src"], a["edge_type_64"])):
                    sp.dma_start(nat_i[i][:, :, :], x.rearrange("(b q p) -> q b p", b=NB, q=Q)).then_inc(s_in[i], 16)
                sp.dma_start(nat_v[:, :, :], a["edge_attr_3"].rearrange("(b q p) c -> q b (p c)", b=NB, q=Q)
                             ).then_inc(s_in[3], 16)
                sp.wait_ge(s_empty, 3)
                sp.dma_start(m.rec_d.rearrange("(p t) c -> p t c", p=EP), empty[:, :, :]).then_inc(s_fill, 16)
                sp.wait_ge(s_lo, 26)
                sp.dma_start(row_d[1, :].rearrange("(b q p) -> q b p", b=NB, q=Q), nat_lo[:, :, :]
                             ).then_inc(s_row, 16)
                sp.dma_start(row_d[0, :].rearrange("(b q p) -> q b p", b=NB, q=Q), nat_f[0][:, :, :]
                             ).then_inc(s_row, 16)
                sp.wait_ge(s_row, 32)
                sp.wait_ge(s_fill, 16)

            @block.gpsimd
            def _(pool):
                ch = Chain(pool, s_empty)
                ch(pool.memset(empty[:, :, :], 0.0))
                ch(pool.memset(empty[:, :, R_LO:R_LO + 1], -1.0))
                ch(pool.memset(empty[:, :, R_DST:R_DST + 1], -1.0))

            @block.vector
            def _(dve):
                for i in range(3):
                    dve.wait_ge(s_in[i], 16)
                    dve.tensor_copy(nat_f[i][:, :, :], nat_i[i][:, :, :]).then_inc(s_flt, 1)
                dve.wait_ge(s_flt, 3)
                ch = Chain(dve, s_lo)
                ch(dve.memset(nat_hi[0][:, :, :], 0.0))
                for k in range(1, NT):
                    ch(dve.scalar_tensor_tensor(nat_hi[k % 2][:, :, :], nat_f[0][:, :, :], float(k * P),
                                                nat_hi[(k + 1) % 2][:, :, :], ALU.is_ge, ALU.add))
                ch(dve.scalar_tensor_tensor(nat_lo[:, :, :], nat_hi[0][:, :, :], -float(P), nat_f[0][:, :, :],
                                            ALU.mult, ALU.add))
                dve.memset(rec_in[:, :, :], 0.0).then_inc(s_rec, 1)
                dve.wait_ge(s_rec, 1)
                for k, (_, _, field) in enumerate(cols):
                    dve.wait_ge(s_tr, k + 1)
                    to = hi[:, :] if field is None else rec_in[:, :, field]
                    dve.tensor_copy(to, ps[k][:, 0:NB * Q]).then_inc(s_rec, 1)
                dve.wait_ge(s_rec, 9)
                dve.tensor_copy(lo[:, :], rec_in[:, :, R_LO]).then_inc(s_hot, 1)
                dve.tensor_tensor(hi_hot[:, :, :], m.iota[0:P, None, 0:NT].to_broadcast([P, SORT_STEPS * U, NT]),
                                  hi[:, :, None].to_broadcast([P, SORT_STEPS * U, NT]), ALU.is_equal
                                  ).then_inc(s_hot, 1)

            @block.tensor
            def _(pe):
                pe.wait_ge(s_lo, 26)
                pe.wait_ge(s_in[3], 16)
                for k, (tile, comp, _) in enumerate(cols):
                    for b in range(NB):
                        src = tile[:, b, :] if comp is None else tile[:, b, comp::3]
                        last = pe.transpose(ps[k][:, b * Q:(b + 1) * Q], src, m.ident[0:Q, 0:Q])
                    last.then_inc(s_tr, 1)

        with ExitStack() as c1:
            sem1 = Sems(nc, c1)
            ps_hist = c1.enter_context(nc.psum_tensor("ps_hist", [P, 512], F32))
            ps_sum = c1.enter_context(nc.psum_tensor("ps_sum", [P, 512], F32))
            ps_pre = c1.enter_context(nc.psum_tensor("ps_pre", [P, 512], F32))
            hist = c1.enter_context(nc.sbuf_tensor("hist", [P, NT], F32))
            tiles_f = c1.enter_context(nc.sbuf_tensor("tiles_f", [P, NT], F32))
            tiles_i = c1.enter_context(nc.sbuf_tensor("tiles_i", [P, 2, NT], I32))
            tile_end = c1.enter_context(nc.sbuf_tensor("tile_end", [P, NT], F32))
            passed = c1.enter_context(nc.sbuf_tensor("passed", [1, T, NT], F32))
            of_tile = c1.enter_context(nc.sbuf_tensor("of_tile", [1, T], F32))
            s_made = sem1("s_lo_made")
            s_used = sem1("s_lo_used")
            s_hist = sem1("s_hist")
            s_ch = sem1("s_pre_ch")
            s_sum = sem1("s_sum")
            block = c1.enter_context(nc.Block())

            @block.vector
            def _(dve):
                def hot(step, b):
                    dve.tensor_tensor(lo_hot[b][:, :, :], m.iota[0:P, None, 0:P].to_broadcast([P, U, P]),
                                      lo[:, ds(step * U, U), None].to_broadcast([P, U, P]), ALU.is_equal
                                      ).then_inc(s_made, 1)

                hot(0, 0)
                hot(1, 1)
                with dve.Fori(1, SORT_STEPS // 2) as it:
                    for b in range(2):
                        dve.wait_ge(s_used, 2 * it + b - 1)
                        hot(2 * it + b, b)
                ch = Chain(dve, s_ch)
                dve.wait_ge(s_hist, 1)
                ch(dve.tensor_copy(hist[:, :], ps_hist[:, 0:NT]))
                dve.wait_ge(s_sum, 1)
                ch(dve.tensor_scalar(tiles_f[:, :], ps_sum[:, 0:NT], float(EP - 1), None, ALU.add))
                ch(dve.tensor_copy(tiles_i[:, 0, :], tiles_f[:, :]))
                ch(dve.tensor_scalar(tiles_i[:, 1, :], tiles_i[:, 0, :], EP.bit_length() - 1, None,
                                     ALU.arith_shift_right))
                ch(dve.tensor_copy(tiles_f[:, :], tiles_i[:, 1, :]))
                ch(dve.tensor_tensor_scan(tile_end[:, :], m.ones[0:P, 0:NT], tiles_f[:, :], 0.0, ALU.mult, ALU.add))
                ch(dve.tensor_tensor(tiles_f[:, :], tile_end[:, :], tiles_f[:, :], ALU.subtract))
                ch(dve.scalar_tensor_tensor(start[:, :], tiles_f[:, :], float(EP), ps_pre[:, 0:NT],
                                            ALU.mult, ALU.add))
                ch(dve.tensor_tensor(passed[:, :, :], m.iota[0:1, 0:T, None].to_broadcast([1, T, NT]),
                                     tile_end[0:1, None, :].to_broadcast([1, T, NT]), ALU.is_ge))
                ch(dve.tensor_reduce(of_tile[:, :], passed[:, :, :], AX.X, ALU.add))
                ch(dve.tensor_scalar(of_tile[:, :], of_tile[:, :], float(NT - 1), None, ALU.min))
                ch(dve.tensor_copy(m.node_tile[0:1, 0:T], of_tile[:, :]))

            @block.tensor
            def _(pe):
                def count(step, b, start_, stop_):
                    for u in range(U):
                        last = pe.matmul(ps_hist[:, 0:NT], lo_hot[b][:, u, :], hi_hot[:, step * U + u, :],
                                         start=start_ and u == 0, stop=stop_ and u == U - 1,
                                         skip_group_check=True)
                    last.then_inc(s_used, 1)
                    return last

                pe.wait_ge(s_made, 1)
                count(0, 0, True, False)
                pe.wait_ge(s_made, 2)
                count(1, 1, False, False)
                with pe.Fori(1, SORT_STEPS // 2) as it:
                    for b in range(2):
                        pe.wait_ge(s_made, 2 * it + b + 1)
                        count(2 * it + b, b, False, False)
                pe.wait_ge(s_used, SORT_STEPS)
                pe.sem_inc(s_hist, 1)
                pe.wait_ge(s_ch, 1)
                pe.matmul(ps_sum[:, 0:NT], m.ones[0:P, 0:P], hist[:, :], start=True, stop=True)
                pe.matmul(ps_pre[:, 0:NT], m.after[0:P, 0:P], hist[:, :], start=True, stop=True).then_inc(s_sum, 1)

        with ExitStack() as c1:
            sem1 = Sems(nc, c1)

            def sb1(name, shape, dt=F32):
                return c1.enter_context(nc.sbuf_tensor(name, shape, dt))

            row = [sb1(f"row{b}", [1, 2, CH]) for b in range(2)]
            lo_hot_t = [sb1(f"lo_hot_t{b}", [P, U, P]) for b in range(2)]
            earlier = [sb1(f"earlier{b}", [P, U]) for b in range(2)]
            junk = sb1("junk", [P, U, CH], BF16)
            mask = sb1("mask", [P, U, CH], BF16)
            picked = [sb1(f"picked{b}", [P, U, NT]) for b in range(2)]
            base = [sb1(f"base{b}", [P, U]) for b in range(2)]
            place = [sb1(f"place{b}", [P, U], U32) for b in range(2)]
            rec_s = [sb1(f"rec_s{b}", [P, U, REC]) for b in range(2)]
            ps_dst = [c1.enter_context(nc.psum_tensor(f"ps_dst{b}", [P, 512], F32)) for b in range(2)]
            ps_lo = [c1.enter_context(nc.psum_tensor(f"ps_lo{b}", [P, 512], F32)) for b in range(2)]
            ps_base = [c1.enter_context(nc.psum_tensor(f"ps_base{b}", [P, 512], F32)) for b in range(2)]
            ps_cnt = [c1.enter_context(nc.psum_tensor(f"ps_cnt{b}", [P, 512], F32)) for b in range(2)]
            s_mask = sem1("s_mask")
            s_rowl = [sem1(f"s_rowl{b}") for b in range(2)]
            s_rows = sem1("s_rows")
            s_hot = sem1("s_hot2")
            s_rank = sem1("s_rank")
            s_look = sem1("s_look")
            s_pick = sem1("s_pick")
            s_base = sem1("s_base")
            s_run = sem1("s_run")
            s_place = sem1("s_place")
            s_recs = sem1("s_recs")
            s_sent = [sem1(f"s_sent{b}") for b in range(2)]
            s_go = sem1("s_go")
            block = c1.enter_context(nc.Block())

            @block.sync
            def _(sp):
                sp.sem_inc(s_rows, 2)
                with sp.Fori(0, SORT_STEPS // 2) as it:
                    for b in range(2):
                        s = 2 * it + b
                        sp.wait_ge(s_rows, s + 1)
                        sp.dma_start(row[b][:, :, :], row_d[None, :, ds(s * CH, CH)]).then_inc(s_rowl[b], 16)

            @block.tensor
            def _(pe):
                def spread(s, it, b):
                    pe.wait_ge(s_rowl[b], 16 * it + 16)
                    if not (known(s) and s < 2):
                        pe.wait_ge(s_rank, s - 1)
                    pe.matmul(ps_dst[b][:, 0:CH], m.ones[0:1, 0:P], row[b][:, 0, :], start=True, stop=True)
                    pe.matmul(ps_lo[b][:, 0:CH], m.ones[0:1, 0:P], row[b][:, 1, :], start=True, stop=True
                              ).then_inc(s_rows, 1)

                def look(s, b):
                    pe.wait_ge(s_hot, s + 1)
                    pe.wait_ge(s_run, s + 1)
                    for u in range(U):
                        pe.matmul(ps_base[b][:, u * NT:(u + 1) * NT], lo_hot_t[b][:, u, :], start[:, :],
                                  start=True, stop=True)
                    for u in range(U):
                        last = pe.matmul(ps_cnt[b][:, 0:NT], lo_hot[b][:, u, :], hi_hot[:, s * U + u, :],
                                         start=u == 0, stop=u == U - 1)
                    last.then_inc(s_look, 1)

                spread(0, 0, 0)
                spread(1, 0, 1)
                with pe.Fori(0, SORT_STEPS // 2 - 1) as it:
                    for b in range(2):
                        look(2 * it + b, b)
                        spread(2 * it + 2 + b, it + 1, b)
                look(SORT_STEPS - 2, 0)
                look(SORT_STEPS - 1, 1)

            @block.vector
            def _(dve):
                dve.memset(mask[:, :, :], 0.0).then_inc(s_mask, 1)
                dve.wait_ge(s_mask, 1)
                for u in range(U):
                    if u:
                        dve.memset(mask[:, u, 0:u * P], 1.0)
                    dve.tensor_copy(mask[:, u, u * P:(u + 1) * P], m.before[0:P, 0:P]).then_inc(s_mask, 1)
                dve.sem_inc(s_run, 1)
                dve.sem_inc(s_place, 1)
                dve.wait_ge(s_mask, 5)

                def prepare(s, b):
                    dve.wait_ge(s_rows, s + 3)
                    if not (known(s) and s < 1):
                        dve.wait_ge(s_rank, s)
                        dve.wait_ge(s_place, s)
                    dve.tensor_scalar(lo_hot_t[b].rearrange("p u q -> p (u q)"), ps_lo[b][:, 0:CH],
                                      m.part[0:P, 0:1], None, ALU.is_equal)
                    dve.tensor_tensor(lo_hot[b][:, :, :], m.iota[0:P, None, 0:P].to_broadcast([P, U, P]),
                                      lo[:, ds(s * U, U), None].to_broadcast([P, U, P]), ALU.is_equal
                                      ).then_inc(s_hot, 1)
                    for u in range(U):
                        n = (u + 1) * P
                        last = dve.scalar_tensor_tensor(junk[:, u, 0:n], ps_dst[b][:, 0:n],
                                                        rec_in[:, s * U + u, R_DST:R_DST + 1], mask[:, u, 0:n],
                                                        ALU.is_equal, ALU.mult, accum_out=earlier[b][:, u:u + 1])
                    last.then_inc(s_rank, 1)

                def settle(s, it, b):
                    dve.wait_ge(s_look, s + 1)
                    dve.tensor_tensor(start[:, :], start[:, :], ps_cnt[b][:, 0:NT], ALU.add)
                    dve.tensor_tensor(picked[b][:, :, :], ps_base[b][:, 0:U * NT].rearrange("p (u n) -> p u n", u=U),
                                      hi_hot[:, ds(s * U, U), :], ALU.mult).then_inc(s_run, 1)
                    dve.wait_ge(s_run, s + 2)
                    dve.tensor_reduce(base[b][:, :], picked[b][:, :, :], AX.X, ALU.add).then_inc(s_base, 1)
                    dve.wait_ge(s_base, s + 1)
                    dve.wait_ge(s_rank, s + 1)
                    if not (known(it) and it < 1):
                        dve.wait_ge(s_sent[b], 16 * U * it)
                    dve.tensor_tensor(place[b][:, :], base[b][:, :], earlier[b][:, :], ALU.add).then_inc(s_place, 1)

                prepare(0, 0)
                for b in range(2):
                    prepare(b + 1, 1 - b)
                    settle(b, 0, b)
                with dve.Fori(1, SORT_STEPS // 2 - 1) as it:
                    for b in range(2):
                        prepare(2 * it + b + 1, 1 - b)
                        settle(2 * it + b, it, b)
                prepare(SORT_STEPS - 1, 1)
                for b in range(2):
                    settle(SORT_STEPS - 2 + b, SORT_STEPS // 2 - 1, b)

            @block.scalar
            def _(act):
                def pack(s, it, b):
                    if not known(it):
                        act.wait_ge(s_sent[b], 16 * U * it)
                    act.activation(rec_s[b][:, :, :], rec_in[:, ds(s * U, U), :], ACT.Copy).then_inc(s_recs, 1)

                pack(0, 0, 0)
                pack(1, 0, 1)
                with act.Fori(1, SORT_STEPS // 2) as it:
                    for b in range(2):
                        pack(2 * it + b, it, b)

            @block.gpsimd
            def _(pool):
                with pool.Fori(0, SORT_STEPS // 2) as it:
                    for b in range(2):
                        s = 2 * it + b
                        pool.wait_ge(s_place, s + 2)
                        pool.sem_inc(s_go, 1)
                        pool.wait_ge(s_recs, s + 1)
                        pool.sem_inc(s_go, 1)
                        for u in range(U):
                            pool.indirect_dma_start(
                                out=m.rec_d[:, :], out_offset=bass.IndirectOffsetOnAxis(ap=place[b][:, u:u + 1], axis=0),
                                in_=rec_s[b][:, u, :], in_offset=None).then_inc(s_sent[b], 16)
                for b in range(2):
                    pool.wait_ge(s_sent[b], 16 * U * SORT_STEPS // 2)


@stage
def build_reload(nc, m):
    with ExitStack() as ctx:
        sem = Sems(nc, ctx)
        s_rec = [sem(f"s_recl{i}") for i in range(4)]
        s_ch = sem("s_vec")
        s_sq = sem("s_sq")
        sq = ctx.enter_context(nc.sbuf_tensor("vsq", [EP, TX, 3], F32))
        n2 = ctx.enter_context(nc.sbuf_tensor("vn2", [EP, TX], F32))
        block = ctx.enter_context(nc.Block())
        cut = [0, TX // 4, TX // 2, 3 * TX // 4, TX]
        view = m.rec_d.rearrange("(t p) c -> p t c", p=EP)

        @block.sync
        def _(sp):
            for i in range(0, 4, 2):
                sp.dma_start(m.rec[:, cut[i]:cut[i + 1], :], view[:, cut[i]:cut[i + 1], :]).then_inc(s_rec[i], 16)

        @block.scalar
        def _(act):
            for i in range(1, 4, 2):
                act.dma_start(m.rec[:, cut[i]:cut[i + 1], :], view[:, cut[i]:cut[i + 1], :]).then_inc(s_rec[i], 16)
            act.wait_ge(s_ch, 3)
            act.activation(n2[:, :], n2[:, :], ACT.Sqrt).then_inc(s_sq, 1)

        @block.vector
        def _(dve):
            for i in range(4):
                dve.wait_ge(s_rec[i], 16)
            ch = Chain(dve, s_ch)
            vec = m.rec[:, :, R_VEC:R_VEC + 3]
            ch(dve.tensor_copy(m.src[:, :], m.rec[:, :, R_SRC]))
            ch(dve.tensor_tensor(sq[:, :, :], vec, vec, ALU.mult))
            ch(dve.tensor_reduce(n2[:, :], sq[:, :, :], AX.X, ALU.add))
            dve.wait_ge(s_sq, 1)
            ch(dve.tensor_scalar(n2[:, :], n2[:, :], 1e-12, None, ALU.add))
            ch(dve.reciprocal(n2[:, :], n2[:, :]))
            ch(dve.tensor_tensor(m.unit[:, :, :], vec, n2[:, :, None].to_broadcast([EP, TX, 3]), ALU.mult))
            ch(dve.tensor_tensor(sq[:, :, :], m.unit[:, :, :], m.unit[:, :, :], ALU.mult))
            ch(dve.tensor_reduce(m.unit2[:, :], sq[:, :, :], AX.X, ALU.add))


@stage
def layer_norm(nc, m, tag, x, y, gamma=None, beta=None):
    with ExitStack() as ctx:
        sem = Sems(nc, ctx)
        st = ctx.enter_context(nc.sbuf_tensor(f"st_{tag}", [P, NT, 6], F32))
        mv = ctx.enter_context(nc.sbuf_tensor(f"mv_{tag}", [P, NT, 2], F32))
        rs = ctx.enter_context(nc.sbuf_tensor(f"rs_{tag}", [P, NT], F32))
        s_st = sem(f"s_st_{tag}")
        s_sq = sem(f"s_sq_{tag}")
        s_ch = sem(f"s_ch_{tag}")
        block = ctx.enter_context(nc.Block())

        @block.vector
        def _(dve):
            with dve.Fori(0, NG) as g:
                for u in range(G):
                    dve.bn_stats(st[:, G * g + u, :], x[:, G * g + u, :]).then_inc(s_st, 1)
            dve.wait_ge(s_st, NT)
            ch = Chain(dve, s_ch)
            ch(dve.tensor_tensor(mv[:, :, 0], st[:, :, 1], st[:, :, 4], ALU.subtract))
            ch(dve.tensor_tensor(mv[:, :, 0], mv[:, :, 0], mv[:, :, 0], ALU.mult))
            ch(dve.tensor_tensor(rs[:, :], st[:, :, 2], st[:, :, 5], ALU.add))
            ch(dve.tensor_scalar(rs[:, :], rs[:, :], 1.0 / D, EPS, ALU.mult, ALU.add))
            ch(dve.scalar_tensor_tensor(rs[:, :], mv[:, :, 0], 0.25, rs[:, :], ALU.mult, ALU.add))
            ch(dve.tensor_tensor(mv[:, :, 0], st[:, :, 1], st[:, :, 4], ALU.add))
            ch(dve.tensor_scalar(mv[:, :, 0], mv[:, :, 0], 0.5, None, ALU.mult))
            dve.wait_ge(s_sq, 1)
            ch(dve.reciprocal(rs[:, :], rs[:, :]))
            ch(dve.tensor_tensor(y[:, :, :], x[:, :, :], mv[:, :, 0:1].to_broadcast([P, NT, D]), ALU.subtract))
            ch(dve.tensor_tensor(y[:, :, :], y[:, :, :], rs[:, :, None].to_broadcast([P, NT, D]), ALU.mult))
            if gamma is not None:
                ch(dve.tensor_tensor(y[:, :, :], y[:, :, :], gamma[:, None, :].to_broadcast([P, NT, D]), ALU.mult))
                ch(dve.tensor_tensor(y[:, :, :], y[:, :, :], beta[:, None, :].to_broadcast([P, NT, D]), ALU.add))

        @block.scalar
        def _(act):
            act.wait_ge(s_ch, 5)
            act.activation(rs[:, :], rs[:, :], ACT.Sqrt).then_inc(s_sq, 1)


@stage
def add_all(nc, tag, pairs):
    with ExitStack() as ctx:
        s_ch = Sems(nc, ctx)(f"s_add_{tag}")
        block = ctx.enter_context(nc.Block())

        @block.vector
        def _(dve):
            ch = Chain(dve, s_ch)
            for out, x, y in pairs:
                ch(dve.tensor_tensor(out, x, y, ALU.add))


@stage
def project(nc, m, tag, prepare, weights, width, finish, keep=None, halves=2, own=0):
    NW = len(weights)
    with ExitStack() as ctx:
        sem = Sems(nc, ctx)
        rows = ctx.enter_context(nc.sbuf_tensor(f"rows_{tag}", [P, G, 256], F32))
        rows_t = ctx.enter_context(nc.sbuf_tensor(f"rows_t_{tag}", [128, G, 2, P], F32))
        ps_t = ctx.enter_context(nc.psum_tensor(f"ps_t_{tag}", [128, 6, 256], F32))
        ps_o = ctx.enter_context(nc.psum_tensor(f"ps_o_{tag}", [128, 6, 256], F32))
        s_prep = sem(f"s_prep_{tag}")
        s_tr = sem(f"s_tr_{tag}")
        s_evac = sem(f"s_evac_{tag}")
        s_mm = sem(f"s_mm_{tag}")
        s_fin = sem(f"s_fin_{tag}")
        s_own = sem(f"s_own_{tag}")
        block = ctx.enter_context(nc.Block())

        @block.vector
        def _(dve):
            dve.sem_inc(s_tr, 1)
            with dve.Fori(0, NG) as g:
                count = [0]

                def ch(ins):
                    count[0] += 1
                    ins.then_inc(s_own, 1)
                    dve.wait_ge(s_own, g * own + count[0])

                dve.wait_ge(s_tr, g + 1)
                prepare(dve, g, rows, ch).then_inc(s_prep, 1)
                for c in range(NW):
                    dve.wait_ge(s_mm, NW * g + c + 1)
                    finish(dve, g, c, ps_o[0:P, 0:G, 0:width], ch).then_inc(s_fin, 1)
                assert count[0] == own

        @block.tensor
        def _(pe):
            pe.sem_inc(s_evac, 1)
            pe.sem_inc(s_fin, 1)
            with pe.Fori(0, NG) as g:
                pe.wait_ge(s_prep, g + 1)
                pe.wait_ge(s_evac, g + 1)
                for u in range(G):
                    for k in range(halves):
                        last = pe.transpose(ps_t[:, u, k * 128:k * 128 + P], rows[:, u, k * 128:(k + 1) * 128],
                                            m.ident[0:P, 0:P])
                last.then_inc(s_tr, 1)
                pe.wait_ge(s_evac, g + 2)
                for c, w in enumerate(weights):
                    pe.wait_ge(s_fin, NW * g + c + 1)
                    for u in range(G):
                        for k in range(halves):
                            last = pe.matmul(ps_o[0:P, u, 0:width], rows_t[:, u, k, :], w[:, k, :],
                                             start=k == 0, stop=k == halves - 1)
                    last.then_inc(s_mm, 1)

        @block.scalar
        def _(act):
            with act.Fori(0, NG) as g:
                act.wait_ge(s_tr, g + 2)
                act.wait_ge(s_fin, NW * g + 1)
                view = ps_t[:, 0:G, :].rearrange("p u (k n) -> p u k n", k=2)[:, :, 0:halves, 0:P]
                if keep is not None:
                    for k in range(halves):
                        act.activation(keep(g, k), view[:, :, k, :], ACT.Copy)
                act.activation(rows_t[:, :, 0:halves, :], view, ACT.Copy).then_inc(s_evac, 1)


def known(s):
    return isinstance(s, int)


@stage
def build_scores(nc, m):
    with ExitStack() as ctx:
        sem = Sems(nc, ctx)

        def sb(name, shape, dt=F32):
            return ctx.enter_context(nc.sbuf_tensor(name, shape, dt))

        R = 4
        idx = [sb(f"a_idx{r}", [EP, U], U32) for r in range(R)]
        k_rows = [m.spare[:, r * U * D:(r + 1) * U * D].rearrange("p (u d) -> p u d", u=U) for r in range(R)]
        hot = [sb(f"a_hot{b}", [EP, U, P], BF16) for b in range(2)]
        rel_hot = [sb(f"a_rhot{b}", [EP, U, NREL], BF16) for b in range(2)]
        hot_t = [sb(f"a_hott{b}", [P, U, EP]) for b in range(2)]
        rel_t = [sb(f"a_rhott{b}", [NREL, U, EP]) for b in range(2)]
        kmod = [sb("a_kmod", [EP, U, D])] * 2
        prod = kmod
        ps_q = [ctx.enter_context(nc.psum_tensor(f"a_psq{b}", [EP, U, D], F32)) for b in range(2)]
        ps_t = [ctx.enter_context(nc.psum_tensor(f"a_pst{b}", [128, 2, U, EP], BF16)) for b in range(2)]
        ps_r = [ctx.enter_context(nc.psum_tensor(f"a_psr{b}", [EP, 2 * U, HD], F32)) for b in range(2)]
        s_idx = sem("a_idx")
        s_k = [sem(f"a_k_{r}") for r in range(R)]
        s_go = sem("a_go")
        s_hot = sem("a_hot")
        s_tr = sem("a_tr")
        s_ev = sem("a_ev")
        s_exp = sem("a_exp")
        s_kmod = sem("a_kmod")
        s_prod = sem("a_prod")
        s_sum = sem("a_sum")
        block = ctx.enter_context(nc.Block())

        @block.gpsimd
        def _(pool):
            def gather(s, r):
                pool.wait_ge(s_idx, s + 1)
                pool.sem_inc(s_go, 1)
                if not (known(s) and s < R):
                    pool.wait_ge(s_kmod, s - R + 1)
                    pool.sem_inc(s_go, 1)
                for u in range(U):
                    pool.indirect_dma_start(out=k_rows[r][:, u, :], out_offset=None, in_=m.k_d[:, :],
                                            in_offset=bass.IndirectOffsetOnAxis(ap=idx[r][:, u:u + 1], axis=0)
                                            ).then_inc(s_k[r], 16)

            for s in range(R):
                gather(s, s)
            with pool.Fori(1, STEPS // R) as it:
                for r in range(R):
                    gather(R * it + r, r)

        @block.scalar
        def _(act):
            def index(s, r):
                act.activation(idx[r][:, :], m.src[:, ds(s * U, U)], ACT.Copy).then_inc(s_idx, 1)

            def turned(s, b):
                act.wait_ge(s_tr, s + 1)
                if not (known(s) and s < 2):
                    act.wait_ge(s_exp, s - 1)
                act.activation(hot_t[b][:, :, :], ps_t[b][0:P, 0, :, :], ACT.Copy)
                act.activation(rel_t[b][:, :, :], ps_t[b][0:NREL, 1, :, :], ACT.Copy).then_inc(s_ev, 1)

            for s in range(R):
                index(s, s)
            for s in range(R):
                turned(s, s % 2)
            with act.Fori(1, STEPS // R) as it:
                for r in range(R):
                    act.wait_ge(s_kmod, R * it + r - R + 1)
                    index(R * it + r, r)
                    turned(R * it + r, r % 2)

        @block.tensor
        def _(pe):
            def turn(s, b):
                pe.wait_ge(s_hot, s + 1)
                if not (known(s) and s < 2):
                    pe.wait_ge(s_ev, s - 1)
                for u in range(U):
                    pe.transpose(ps_t[b][0:P, 0, u, :], hot[b][:, u, :], m.ident_b[:, :])
                    last = pe.transpose(ps_t[b][0:NREL, 1, u, :], rel_hot[b][:, u, :], m.ident_b[:, :])
                last.then_inc(s_tr, 1)

            def expand(s, b):
                pe.wait_ge(s_ev, s + 1)
                if not (known(s) and s < 2):
                    pe.wait_ge(s_prod, s - 1)
                for u in range(U):
                    j = pe.value_load(m.node_tile[0:1, ds(s * U + u, 1)], min_val=0, max_val=NT - 1)
                    pe.matmul(ps_q[b][:, u, :], hot_t[b][:, u, :], m.q[:, j, :], start=True, stop=True)
                    last = pe.matmul(ps_r[b][:, u, :], rel_t[b][:, u, :], m.rel[:, :], start=True, stop=True)
                last.then_inc(s_exp, 1)

            turn(0, 0)
            turn(1, 1)
            expand(0, 0)
            with pe.Fori(0, (STEPS - 2) // 2) as it:
                for b in range(2):
                    turn(2 * it + 2 + b, b)
                    expand(2 * it + 1 + b, 1 - b)
            expand(STEPS - 1, 1)

        @block.vector
        def _(dve):
            def make(s, b):
                if not (known(s) and s < 2):
                    dve.wait_ge(s_tr, s - 1)
                dve.tensor_tensor(hot[b][:, :, :], m.iota[:, None, 0:P].to_broadcast([EP, U, P]),
                                  m.rec[:, ds(s * U, U), R_LO:R_LO + 1].to_broadcast([EP, U, P]), ALU.is_equal)
                dve.tensor_tensor(rel_hot[b][:, :, :], m.iota[:, None, 0:NREL].to_broadcast([EP, U, NREL]),
                                  m.rec[:, ds(s * U, U), R_TYPE:R_TYPE + 1].to_broadcast([EP, U, NREL]),
                                  ALU.is_equal).then_inc(s_hot, 1)

            def score(s, it, r):
                b = r % 2
                dve.wait_ge(s_k[r], 16 * U * it + 16 * U)
                dve.wait_ge(s_exp, s + 1)
                dve.wait_ge(s_sum, s + 1)
                dve.tensor_tensor(kmod[b].rearrange("p u (h d) -> p u h d", h=H),
                                  k_rows[r].rearrange("p u (h d) -> p u h d", h=H),
                                  ps_r[b][:, 0:U, None, :].to_broadcast([EP, U, H, HD]), ALU.add).then_inc(s_kmod, 1)
                dve.wait_ge(s_kmod, s + 1)
                dve.tensor_tensor(prod[b][:, :, :], kmod[b][:, :, :], ps_q[b][:, :, :], ALU.mult).then_inc(s_prod, 1)
                dve.wait_ge(s_prod, s + 1)
                dve.tensor_reduce(m.s[:, ds(s * U, U), :].rearrange("p u h -> p (u h)"),
                                  prod[b].rearrange("p u (h d) -> p (u h) d", h=H), AX.X, ALU.add).then_inc(s_sum, 1)

            dve.sem_inc(s_sum, 1)
            make(0, 0)
            make(1, 1)
            with dve.Fori(0, STEPS // R - 1) as it:
                for r in range(R):
                    make(R * it + r + 2, r % 2)
                    score(R * it + r, it, r)
            for r in range(R):
                if r < R - 2:
                    make(STEPS - R + r + 2, r % 2)
                score(STEPS - R + r, STEPS // R - 1, r)


@stage
def build_weights(nc, m):
    with ExitStack() as ctx:
        sem = Sems(nc, ctx)

        def sb(name, shape, dt=F32):
            return ctx.enter_context(nc.sbuf_tensor(name, shape, dt))

        W = NBLK * 128
        st = sb("x_st", [128, W])
        dt = sb("x_dt", [128, W])
        cut = sb("x_cut", [128, W + 1])
        dst4 = cut[:, 0:W].rearrange("p (t h) -> p t h", h=H)
        fwd = sb("x_fwd", [128, W])
        bwd = sb("x_bwd", [128, W])
        ends = sb("x_ends", [128, 4, NBLK])
        ends_t = sb("x_ends_t", [4 * NBLK, 128])
        spare = m.agg[0:1, :, :].rearrange("p j c -> p (j c)")
        er = spare[:, 0:4 * W].rearrange("p (c w) -> p c w", c=4)
        link = sb("x_link", [1, W + H])
        both = spare[:, 4 * W:6 * W].rearrange("p (c w) -> p c w", c=2)
        run = sb("x_run", [1, 2, W + 2 * H])
        carry = er[:, 0:2, :]
        carry_t = sb("x_carry_t", [2 * NBLK, 128])
        cc = sb("x_cc", [128, 2, NBLK])
        tmp = bwd[:, :].rearrange("p (b e) -> p b e", e=128)
        NBK = -(-W // 512)
        ps_a = ctx.enter_context(nc.psum_tensor("x_psa", [128, NBK * 512], F32))
        ps_b = ctx.enter_context(nc.psum_tensor("x_psb", [128, NBK * 512], F32))
        s_ch = sem("x_ch")
        s_pe = sem("x_pe")
        s_d = [sem(f"x_d{i}") for i in range(4)]
        s_fin = sem("x_fin")
        block = ctx.enter_context(nc.Block())
        marks = {}

        @block.vector
        def _(dve):
            ch = Chain(dve, s_ch)
            b3 = lambda t: t.rearrange("p (b e) -> p b e", e=128)
            ch(dve.tensor_copy(dst4[:, :, :], m.rec[:, 0:T, R_DST:R_DST + 1].to_broadcast([EP, T, H])))
            marks["dst4"] = ch.n
            dve.wait_ge(s_pe, 1)
            ch(dve.tensor_copy(st[:, :], ps_a[:, 0:W]))
            ch(dve.tensor_copy(dt[:, :], ps_b[:, 0:W]))
            ch(dve.tensor_tensor(cut[:, 1:W], dt[:, 1:W], dt[:, 0:W - 1], ALU.not_equal))
            ch(dve.tensor_scalar(cut[:, 1:W], cut[:, 1:W], -BIG, None, ALU.mult))
            ch(dve.memset(cut[:, 0:W].rearrange("p (b e) -> p b e", e=128)[:, :, 0:1], -BIG))
            ch(dve.memset(cut[:, W:W + 1], -BIG))
            ch(dve.tensor_tensor_scan(fwd[:, :], cut[:, 0:W], st[:, :], -BIG, ALU.add, ALU.max))
            ch(dve.tensor_tensor_scan(bwd[:, ::-1], cut[:, 1:W + 1][:, ::-1], st[:, ::-1], -BIG, ALU.add, ALU.max))
            ch(dve.tensor_tensor(fwd[:, :], fwd[:, :], bwd[:, :], ALU.max))
            ch(dve.tensor_copy(ends[:, 0, :], b3(fwd)[:, :, 0]))
            ch(dve.tensor_copy(ends[:, 1, :], b3(fwd)[:, :, 127]))
            ch(dve.tensor_copy(ends[:, 2, :], b3(dt)[:, :, 0]))
            ch(dve.tensor_copy(ends[:, 3, :], b3(dt)[:, :, 127]))
            marks["ends"] = ch.n
            dve.wait_ge(s_pe, 2)
            ch(dve.tensor_copy(ends_t[:, :], ps_a[0:4 * NBLK, 0:128]))
            marks["ends_t"] = ch.n
            dve.wait_ge(s_d[1], 16)
            ch(dve.memset(link[:, :], -BIG))
            ch(dve.tensor_tensor(link[:, H:W], er[:, 2, H:W], er[:, 3, 0:W - H], ALU.not_equal))
            ch(dve.tensor_scalar(link[:, H:W], link[:, H:W], -BIG, None, ALU.mult))
            ch(dve.tensor_tensor(both[:, 0, :], er[:, 2, :], er[:, 3, :], ALU.not_equal))
            ch(dve.scalar_tensor_tensor(both[:, 1, :], both[:, 0, :], -BIG, link[:, H:W + H], ALU.mult, ALU.add))
            ch(dve.scalar_tensor_tensor(both[:, 0, :], both[:, 0, :], -BIG, link[:, 0:W], ALU.mult, ALU.add))
            ch(dve.memset(run[:, :, :], -BIG))
            for h in range(H):
                ch(dve.tensor_tensor_scan(run[:, 0, H + h:W + H:H], both[:, 0, h::H], er[:, 1, h::H], -BIG,
                                          ALU.add, ALU.max))
                ch(dve.tensor_tensor_scan(run[:, 1, h:W:H][:, ::-1], both[:, 1, h::H][:, ::-1],
                                          er[:, 0, h::H][:, ::-1], -BIG, ALU.add, ALU.max))
            ch(dve.tensor_tensor(carry[:, 0, :], run[:, 0, 0:W], link[:, 0:W], ALU.add))
            ch(dve.tensor_tensor(carry[:, 1, :], run[:, 1, H:W + H], link[:, H:W + H], ALU.add))
            marks["carry"] = ch.n
            dve.wait_ge(s_pe, 3)
            ch(dve.tensor_copy(cc.rearrange("p c b -> p (c b)"), ps_a[:, 0:2 * NBLK]))
            for side, at in ((0, 2), (1, 3)):
                ch(dve.tensor_tensor(tmp[:, :, :], b3(dt), ends[:, at, :, None].to_broadcast([128, NBLK, 128]),
                                     ALU.not_equal))
                ch(dve.scalar_tensor_tensor(tmp[:, :, :], tmp[:, :, :], -BIG,
                                            cc[:, side, :, None].to_broadcast([128, NBLK, 128]), ALU.mult, ALU.add))
                ch(dve.tensor_tensor(b3(fwd), b3(fwd), tmp[:, :, :], ALU.max))
            marks["max"] = ch.n
            dve.wait_ge(s_pe, 4)
            flat = m.s[:, 0:T, :].rearrange("p t h -> p (t h)")
            ch(dve.tensor_tensor(flat, flat, ps_b[:, 0:W], ALU.subtract))
            marks["sub"] = ch.n

        @block.tensor
        def _(pe):
            flat = m.s[:, 0:T, :].rearrange("p t h -> p (t h)")
            dflat = dst4.rearrange("p t h -> p (t h)")
            pe.wait_ge(s_ch, marks["dst4"])
            for b in range(NBLK):
                c = slice(b * 128, (b + 1) * 128)
                pe.transpose(ps_a[:, c], flat[:, c], m.ident[:, :])
                last = pe.transpose(ps_b[:, c], dflat[:, c], m.ident[:, :])
            last.then_inc(s_pe, 1)
            pe.wait_ge(s_ch, marks["ends"])
            pe.transpose(ps_a[0:4 * NBLK, 0:128], ends.rearrange("p c b -> p (c b)"), m.ident[:, :]).then_inc(s_pe, 1)
            pe.wait_ge(s_d[3], 16)
            pe.transpose(ps_a[:, 0:2 * NBLK], carry_t[:, :], m.ident[0:2 * NBLK, 0:2 * NBLK]).then_inc(s_pe, 1)
            pe.wait_ge(s_ch, marks["max"])
            for b in range(NBLK):
                c = slice(b * 128, (b + 1) * 128)
                last = pe.transpose(ps_b[:, c], fwd[:, c], m.ident[:, :])
            last.then_inc(s_pe, 1)

        @block.sync
        def _(sp):
            sp.wait_ge(s_ch, marks["ends_t"])
            sp.dma_start(m.ends_d[:, :], ends_t[:, :]).then_inc(s_d[0], 16)
            sp.wait_ge(s_d[0], 16)
            sp.dma_start(er[:, :, :], m.ends_d.rearrange("(a c b) e -> a c (b e)", a=1, c=4)).then_inc(s_d[1], 16)
            sp.wait_ge(s_ch, marks["carry"])
            sp.dma_start(m.carry_d.rearrange("(a c b) e -> a c (b e)", a=1, c=2), carry).then_inc(s_d[2], 16)
            sp.wait_ge(s_d[2], 16)
            sp.dma_start(carry_t[:, :], m.carry_d[:, :]).then_inc(s_d[3], 16)

        @block.scalar
        def _(act):
            act.wait_ge(s_ch, marks["sub"])
            act.activation(m.s[:, 0:T, :], m.s[:, 0:T, :], ACT.Exp).then_inc(s_fin, 1)


@stage
def build_values(nc, m):
    WD = D + H
    with ExitStack() as ctx:
        sem = Sems(nc, ctx)

        def sb(name, shape, dt=F32):
            return ctx.enter_context(nc.sbuf_tensor(name, shape, dt))

        R = 4
        idx = [sb(f"b_idx{r}", [EP, U], U32) for r in range(R)]
        v_rows = [sb(f"b_v{r}", [EP, U, D]) for r in range(R)]
        hot = [sb(f"b_hot{b}", [EP, U, P]) for b in range(2)]
        msg = [sb(f"b_msg{b}", [EP, U, WD]) for b in range(2)]
        ps = [ctx.enter_context(nc.psum_tensor(f"b_ps{i}", [P, 512], F32)) for i in range(2 * U)]
        s_idx = sem("b_idx")
        s_v = [sem(f"b_v_{r}") for r in range(R)]
        s_go = sem("b_go")
        s_msg = sem("b_msg")
        s_mm = sem("b_mm")
        s_add = sem("b_add")
        s_zero = sem("b_zero")
        block = ctx.enter_context(nc.Block())

        @block.gpsimd
        def _(pool):
            def gather(s, r):
                pool.wait_ge(s_idx, s + 1)
                pool.sem_inc(s_go, 1)
                if not (known(s) and s < R):
                    pool.wait_ge(s_msg, s - R + 1)
                    pool.sem_inc(s_go, 1)
                for u in range(U):
                    pool.indirect_dma_start(out=v_rows[r][:, u, :], out_offset=None, in_=m.v_d[:, :],
                                            in_offset=bass.IndirectOffsetOnAxis(ap=idx[r][:, u:u + 1], axis=0)
                                            ).then_inc(s_v[r], 16)

            for s in range(R):
                gather(s, s)
            with pool.Fori(1, STEPS // R) as it:
                for r in range(R):
                    gather(R * it + r, r)

        @block.scalar
        def _(act):
            def index(s, r):
                act.activation(idx[r][:, :], m.src[:, ds(s * U, U)], ACT.Copy).then_inc(s_idx, 1)

            for s in range(R):
                index(s, s)
            with act.Fori(1, STEPS // R) as it:
                for r in range(R):
                    act.wait_ge(s_msg, R * it + r - R + 1)
                    index(R * it + r, r)

        @block.tensor
        def _(pe):
            def body(s, b):
                pe.wait_ge(s_msg, s + 1)
                if not (known(s) and s < 2):
                    pe.wait_ge(s_add, s - 1)
                for u in range(U):
                    last = pe.matmul(ps[b * U + u][:, 0:WD], hot[b][:, u, :], msg[b][:, u, :], start=True, stop=True)
                last.then_inc(s_mm, 1)

            body(0, 0)
            body(1, 1)
            with pe.Fori(1, STEPS // 2) as it:
                for b in range(2):
                    body(2 * it + b, b)

        @block.vector
        def _(dve):
            def make(s, it, r):
                b = r % 2
                if not (known(s) and s < 2):
                    dve.wait_ge(s_mm, s - 1)
                dve.tensor_tensor(hot[b][:, :, :], m.iota[:, None, 0:P].to_broadcast([EP, U, P]),
                                  m.rec[:, ds(s * U, U), R_LO:R_LO + 1].to_broadcast([EP, U, P]), ALU.is_equal)
                dve.tensor_copy(msg[b][:, :, D:WD], m.s[:, ds(s * U, U), :])
                dve.wait_ge(s_v[r], 16 * U * it + 16 * U)
                dve.tensor_tensor(msg[b][:, :, 0:D].rearrange("p u (h d) -> p u h d", h=H),
                                  v_rows[r].rearrange("p u (h d) -> p u h d", h=H),
                                  m.s[:, ds(s * U, U), :, None].to_broadcast([EP, U, H, HD]), ALU.mult
                                  ).then_inc(s_msg, 1)

            def add(s, b):
                dve.wait_ge(s_mm, s + 1)
                for u in range(U):
                    j = dve.value_load(m.node_tile[0:1, ds(s * U + u, 1)], min_val=0, max_val=NT - 1)
                    if not (known(s) and s == 0 and u == 0):
                        dve.wait_ge(s_zero, s * U + u + 1)
                    last = dve.tensor_tensor(m.agg[:, j, 0:WD], m.agg[:, j, 0:WD], ps[b * U + u][:, 0:WD], ALU.add)
                    last.then_inc(s_zero, 1)
                dve.wait_ge(s_zero, s * U + U + 1)
                dve.sem_inc(s_add, 1)

            dve.memset(m.agg[:, :, :], 0.0).then_inc(s_zero, 1)
            make(0, 0, 0)
            dve.wait_ge(s_zero, 1)
            for r in range(1, R):
                make(r, 0, r)
                add(r - 1, (r - 1) % 2)
            with dve.Fori(1, STEPS // R) as it:
                for r in range(R):
                    make(R * it + r, it, r)
                    add(R * it + r - 1, (r - 1) % 2)
            add(STEPS - 1, 1)


@stage
def build_geometric(nc, m):
    MW = 64 + 192 + 192
    OWN = 8
    R = 8
    with ExitStack() as ctx:
        sem = Sems(nc, ctx)

        def sb(name, shape, dt=F32):
            return ctx.enter_context(nc.sbuf_tensor(name, shape, dt))

        idx = [sb(f"g_idx{r}", [EP, U], U32) for r in range(R)]
        rows = [sb(f"g_rows{r}", [EP, U, 64 + D]) for r in range(R)]
        xr = sb("g_xr", [EP, U, 64, 3])
        ut = [sb(f"g_ut{b}", [128, U, EP]) for b in range(2)]
        lk = [sb(f"g_lk{b}", [64, U, EP]) for b in range(2)]
        mx = sb("g_mx", [EP, U])
        nm = sb("g_nm", [EP, U])
        ex = sb("g_ex", [EP, U, 64])
        z = sb("g_z", [EP, U])
        en = sb("g_en", [EP, U])
        rz = sb("g_rz", [EP, U])
        al = sb("g_al", [EP, U])
        ar = sb("g_ar", [EP, U, 3])
        t1 = sb("g_t1", [EP, U, 64])
        o = [sb(f"g_o{b}", [EP, U, 192]) for b in range(2)]
        hot = [sb(f"g_hot{b}", [EP, U, P]) for b in range(2)]
        msg = [sb(f"g_msg{b}", [EP, U, MW]) for b in range(2)]
        ps_t = ctx.enter_context(nc.psum_tensor("g_pst", [128, U, EP], F32))
        ps_h = ctx.enter_context(nc.psum_tensor("g_psh", [64, U, EP], F32))
        ps_s = [ctx.enter_context(nc.psum_tensor(f"g_pss{b}", [EP, 2 * U, 64], F32)) for b in range(2)]
        ps_o = ctx.enter_context(nc.psum_tensor("g_pso", [EP, U, 256], F32))
        ps_a = [ctx.enter_context(nc.psum_tensor(f"g_psa{i}", [P, 512], F32)) for i in range(2)]
        s_idx = sem("g_idx")
        s_x = [sem(f"g_x_{r}") for r in range(R)]
        s_go = sem("g_go")
        s_xr = sem("g_xr")
        s_y = sem("g_y")
        s_tr = sem("g_tr")
        s_ut = sem("g_ut")
        s_h = sem("g_h")
        s_lk = sem("g_lk")
        s_out = sem("g_out")
        s_o = sem("g_o")
        s_nm = sem("g_nm")
        s_ex = sem("g_ex")
        s_al = sem("g_al")
        s_xm = sem("g_xm")
        s_hot = sem("g_hot")
        s_msg = sem("g_msg")
        s_prod = sem("g_prod")
        s_sum = sem("g_sum")
        s_ch = sem("g_ch")
        block = ctx.enter_context(nc.Block())

        @block.gpsimd
        def _(pool):
            def gather(s, r):
                pool.wait_ge(s_idx, s + 1)
                pool.sem_inc(s_go, 1)
                if not (known(s) and s < R):
                    pool.wait_ge(s_xm, s - R + 1)
                    pool.sem_inc(s_go, 1)
                for u in range(U):
                    pool.indirect_dma_start(out=rows[r][:, u, 64:64 + D], out_offset=None, in_=m.h_d[:, :],
                                            in_offset=bass.IndirectOffsetOnAxis(ap=idx[r][:, u:u + 1], axis=0)
                                            ).then_inc(s_x[r], 16)

            for s in range(R):
                gather(s, s)
            with pool.Fori(1, STEPS // R) as it:
                for r in range(R):
                    gather(R * it + r, r)
            for r in range(3):
                gather(STEPS + r, r)
            for r in range(3):
                pool.wait_ge(s_x[r], 16 * U * (STEPS // R + 1))

        @block.scalar
        def _(act):
            def index(s, r):
                act.activation(idx[r][:, :], m.src[:, ds(s * U, U)], ACT.Copy).then_inc(s_idx, 1)

            def turned(s, b):
                act.wait_ge(s_tr, s + 1)
                act.activation(ut[b][:, :, :], ps_t[:, :, :], ACT.Copy).then_inc(s_ut, 1)

            def relu(s, b):
                act.wait_ge(s_h, s + 1)
                act.activation(lk[b][:, :, :], ps_h[:, :, :], ACT.Relu).then_inc(s_lk, 1)

            def take(s, b):
                act.wait_ge(s_out, s + 1)
                act.activation(o[b][:, :, :], ps_o[:, :, 0:192], ACT.Copy).then_inc(s_o, 1)

            def exps(s, b):
                act.wait_ge(s_nm, s + 1)
                act.activation(en[:, :], nm[:, :], ACT.Exp)
                for u in range(U):
                    last = act.activation(ex[:, u, :], ps_s[b][:, u, :], ACT.Exp, bias=nm[:, u:u + 1],
                                          accum_out=z[:, u:u + 1])
                last.then_inc(s_ex, 1)

            for s in range(R):
                index(s, s)
            turned(0, 0)
            relu(0, 0)
            take(0, 0)
            turned(1, 1)
            relu(1, 1)
            exps(0, 0)
            with act.Fori(0, STEPS // R) as it:
                for r in range(R):
                    s, b = R * it + r, r % 2
                    turned(s + 2, b)
                    act.wait_ge(s_al, s + 1)
                    act.wait_ge(s_prod, s * U + U)
                    for u in range(U):
                        last = act.activation(msg[b][:, u, 64:256], rows[r][:, u, 128:320], ACT.Copy,
                                              scale=al[:, u:u + 1])
                    last.then_inc(s_xm, 1)
                    take(s + 1, 1 - b)
                    exps(s + 1, 1 - b)
                    relu(s + 2, b)
                    act.wait_ge(s_x[r], 16 * U * it + 16 * U)
                    index(s + R, r)

        @block.tensor
        def _(pe):
            def turn(s, r):
                pe.wait_ge(s_y, s + 2)
                for u in range(U):
                    last = pe.transpose(ps_t[:, u, :], rows[r][:, u, 0:128], m.ident[:, :])
                last.then_inc(s_tr, 1)

            def hidden(s, b):
                pe.wait_ge(s_ut, s + 1)
                pe.matmul(ps_h.rearrange("p u e -> p (u e)"), m.w_h[:, :],
                          ut[b].rearrange("p u e -> p (u e)"), start=True, stop=True).then_inc(s_h, 1)

            def out(s, b):
                if not known(s):
                    pe.wait_ge(s_o, s)
                for u in range(U):
                    pe.matmul(ps_o[:, u, 0:192], ut[b][:, u, :], m.w_o[:, :], start=True, stop=True)
                pe.wait_ge(s_lk, s + 1)
                for u in range(U):
                    pe.matmul(ps_s[b][:, u, :], ut[b][:, u, :], m.w_l[:, :], start=True, stop=False)
                    last = pe.matmul(ps_s[b][:, u, :], lk[b][:, u, :], m.w_s[:, :], start=False, stop=True)
                last.then_inc(s_out, 1)

            pe.sem_inc(s_prod, 2 * U)
            turn(0, 0)
            hidden(0, 0)
            out(0, 0)
            turn(1, 1)
            hidden(1, 1)
            with pe.Fori(0, STEPS // R) as it:
                for r in range(R):
                    s, b = R * it + r, r % 2
                    turn(s + 2, (r + 2) % R)
                    out(s + 1, 1 - b)
                    pe.wait_ge(s_hot, s + 1)
                    pe.wait_ge(s_xm, s + 1)
                    pe.wait_ge(s_msg, s + 1)
                    for u in range(U):
                        pe.wait_ge(s_sum, s * U + u + 1)
                        pe.matmul(ps_a[u % 2][:, 0:MW], hot[b][:, u, :], msg[b][:, u, :], start=True, stop=True
                                  ).then_inc(s_prod, 1)
                    hidden(s + 2, b)

        @block.vector
        def _(dve):
            def lead(s, it, r):
                dve.wait_ge(s_x[r], 16 * U * it + 16 * U)
                dve.wait_ge(s_y, s + 1)
                dve.tensor_tensor(xr[:, :, :, :], rows[r][:, :, 128:320].rearrange("p u (c k) -> p u c k", k=3),
                                  m.unit[:, ds(s * U, U), None, :].to_broadcast([EP, U, 64, 3]), ALU.mult
                                  ).then_inc(s_xr, 1)
                dve.wait_ge(s_xr, s + 1)
                dve.tensor_reduce(rows[r][:, :, 0:64], xr[:, :, :, :], AX.X, ALU.add).then_inc(s_y, 1)

            def largest(s, b, ch):
                dve.wait_ge(s_out, s + 1)
                ch(dve.tensor_reduce(mx[:, :], ps_s[b][:, 0:U, :], AX.X, ALU.max))
                dve.tensor_scalar(nm[:, :], mx[:, :], 0.0, -1.0, ALU.max, ALU.mult).then_inc(s_nm, 1)

            def one_hot(s, b):
                dve.tensor_tensor(hot[b][:, :, :], m.iota[:, None, 0:P].to_broadcast([EP, U, P]),
                                  m.rec[:, ds(s * U, U), R_LO:R_LO + 1].to_broadcast([EP, U, P]), ALU.is_equal
                                  ).then_inc(s_hot, 1)

            dve.memset(m.agg[:, :, :], 0.0).then_inc(s_sum, 2)
            dve.sem_inc(s_y, 1)
            for s in range(3):
                lead(s, 0, s)
            first = Chain(dve, s_ch)
            largest(0, 0, first)
            one_hot(0, 0)
            with dve.Fori(0, STEPS // R) as it:
                for r in range(R):
                    s, b = R * it + r, r % 2
                    count = [0]

                    def ch(ins):
                        count[0] += 1
                        ins.then_inc(s_ch, 1)
                        dve.wait_ge(s_ch, s * OWN + count[0] + 1)

                    dve.wait_ge(s_ex, s + 1)
                    ch(dve.scalar_tensor_tensor(rz[:, :], en[:, :], 192.0, z[:, :], ALU.mult, ALU.add))
                    ch(dve.reciprocal(rz[:, :], rz[:, :]))
                    dve.tensor_tensor(al[:, :], en[:, :], rz[:, :], ALU.mult).then_inc(s_al, 1)
                    dve.wait_ge(s_o, s + 1)
                    ch(dve.tensor_tensor(t1[:, :, :], o[b][:, :, 128:192],
                                         m.unit2[:, ds(s * U, U), None].to_broadcast([EP, U, 64]), ALU.mult))
                    dve.wait_ge(s_al, s + 1)
                    dve.tensor_tensor(ar[:, :, :], m.unit[:, ds(s * U, U), :],
                                      al[:, :, None].to_broadcast([EP, U, 3]), ALU.mult)
                    ch(dve.tensor_tensor(t1[:, :, :], t1[:, :, :], o[b][:, :, 0:64], ALU.add))
                    ch(dve.tensor_tensor(t1[:, :, :], t1[:, :, :], rz[:, :, None].to_broadcast([EP, U, 64]), ALU.mult))
                    dve.wait_ge(s_prod, s * U + U)
                    ch(dve.tensor_tensor(msg[b][:, :, 0:64], t1[:, :, :], ex[:, :, :], ALU.mult))
                    for u in range(U):
                        last = dve.tensor_tensor(msg[b][:, u, 256:448].rearrange("p (k c) -> p k c", k=3),
                                                 o[b][:, u, None, 64:128].to_broadcast([EP, 3, 64]),
                                                 ar[:, u, :, None].to_broadcast([EP, 3, 64]), ALU.mult)
                    ch(last)
                    dve.sem_inc(s_msg, 1)
                    largest(s + 1, 1 - b, ch)
                    assert count[0] == OWN
                    lead(s + 3, it if r < R - 3 else it + 1, (r + 3) % R)
                    dve.wait_ge(s_prod, s * U + 2 * U)
                    one_hot(s + 1, 1 - b)
                    for u in range(U):
                        j = dve.value_load(m.node_tile[0:1, ds(s * U + u, 1)], min_val=0, max_val=NT - 1)
                        dve.wait_ge(s_prod, s * U + u + 1 + 2 * U)
                        dve.wait_ge(s_sum, s * U + u + 2)
                        dve.tensor_tensor(m.agg[:, j, 0:MW], m.agg[:, j, 0:MW], ps_a[u % 2][:, 0:MW], ALU.add
                                          ).then_inc(s_sum, 1)


@stage
def build_geometric_weights(nc, m, a):
    c8 = 1.0 / 8.0
    ctp = float(1.0 / np.sqrt(128.0))
    kap = c8 * ctp * c8
    sq3 = float(np.sqrt(3.0))
    names = ["lin_src_w0", "lin_src_w1", "tp1_w00", "tp1_w11", "tp1_w01", "tp1_w10", "tp2_w00", "tp2_w11",
             "tp2_w01", "tp2_w10", "lin_hidden_w0", "lin_hidden_w1"]
    with ExitStack() as ctx:
        sem = Sems(nc, ctx)
        w = ctx.enter_context(nc.sbuf_tensor("gw_w", [64, 12, 64], F32))
        wt = ctx.enter_context(nc.sbuf_tensor("gw_wt", [64, 6, 64], F32))
        pr = ctx.enter_context(nc.sbuf_tensor("gw_pr", [64, 4, 64], F32))
        abt = ctx.enter_context(nc.sbuf_tensor("gw_abt", [64, 4, 64], F32))
        ab = ctx.enter_context(nc.sbuf_tensor("gw_ab", [64, 2, 64], F32))
        up = ctx.enter_context(nc.sbuf_tensor("gw_up", [64, 5, 64], F32))
        ps = [ctx.enter_context(nc.psum_tensor(f"gw_ps{i}", [64, 8, 64], F32)) for i in range(3)]
        s_in = sem("gw_in")
        s_tr = sem("gw_tr")
        s_ev = sem("gw_ev")
        s_z = sem("gw_z")
        s_mv = sem("gw_mv")
        block = ctx.enter_context(nc.Block())
        LS0, LS1, T00, T11, T01, T10, U00, U11, U01, U10, LH0, LH1 = range(12)

        @block.sync
        def _(sp):
            for i, n in enumerate(names):
                sp.dma_start(w[:, i, :], a["L1_gnn_" + n]).then_inc(s_in, 16)
            sp.wait_ge(s_ev, 7)
            sp.dma_start(m.w_h[64:128, :], up[:, 0, :]).then_inc(s_mv, 16)
            sp.dma_start(m.w_o[64:128, :], up[:, 1:4, :].rearrange("p c d -> p (c d)")).then_inc(s_mv, 16)
            sp.dma_start(m.w_d[64:128, 0, 64:128], m.w_d[0:64, 0, 0:64]).then_inc(s_mv, 16)
            sp.dma_start(m.w_l[64:128, :], up[:, 4, :]).then_inc(s_mv, 16)
            sp.wait_ge(s_mv, 64)

        @block.tensor
        def _(pe):
            i64 = m.ident[0:64, 0:64]
            pe.wait_ge(s_in, 16 * 12)
            for k, i in enumerate((LS0, LS1, T00, T11, T01, T10)):
                last = pe.transpose(ps[0][:, k, :], w[:, i, :], i64)
            last.then_inc(s_tr, 1)
            pe.wait_ge(s_ev, 1)
            for k, h in enumerate((LH0, LH0, LH1, LH1)):
                last = pe.matmul(ps[1][:, k, :], wt[:, 2 + k, :], w[:, h, :], start=True, stop=True)
            last.then_inc(s_tr, 1)
            pe.wait_ge(s_ev, 2)
            for k, l in enumerate((0, 1, 0, 1)):
                pe.matmul(ps[2][:, k, :], pr[:, k, :], wt[:, l, :], start=True, stop=True)
            for k in range(2):
                last = pe.matmul(ps[2][:, 4 + k, :], wt[:, k, :], pr[:, k, :], start=True, stop=True)
            last.then_inc(s_tr, 1)
            pe.wait_ge(s_ev, 4)
            prods = [(0, [(0, U00)]), (1, [(1, U00), (3, U11)]), (2, [(0, U01), (2, U10)]), (3, [(1, U01)]),
                     (4, [(2, U11)]), (5, [(3, U10)])]
            for slot, terms in prods:
                for n, (k, u) in enumerate(terms):
                    pe.matmul(ps[1][:, slot, :], abt[:, k, :], w[:, u, :], start=n == 0,
                              stop=n == len(terms) - 1)
            for k in range(2):
                last = pe.matmul(ps[1][:, 6 + k, :], abt[:, k, :], m.w_s[:, :], start=True, stop=True)
            last.then_inc(s_tr, 1)

        @block.vector
        def _(dve):
            dve.wait_ge(s_tr, 1)
            dve.tensor_copy(wt[:, :, :], ps[0][:, 0:6, :]).then_inc(s_ev, 1)
            dve.wait_ge(s_tr, 2)
            dve.tensor_copy(pr[:, :, :], ps[1][:, 0:4, :]).then_inc(s_ev, 1)
            dve.wait_ge(s_tr, 3)
            dve.tensor_scalar(abt[:, :, :], ps[2][:, 0:4, :], kap, None, ALU.mult).then_inc(s_ev, 1)
            dve.tensor_scalar(ab[:, :, :], ps[2][:, 4:6, :], kap, None, ALU.mult).then_inc(s_ev, 1)
            dve.memset(m.w_d[:, :, :], 0.0).then_inc(s_z, 1)
            dve.wait_ge(s_tr, 4)
            dve.wait_ge(s_ev, 4)
            dve.wait_ge(s_z, 1)
            dve.tensor_copy(up[:, 0, :], ab[:, 0, :])
            dve.tensor_scalar(up[:, 1, :], ps[1][:, 0, :], ctp, None, ALU.mult)
            dve.tensor_scalar(up[:, 2, :], ps[1][:, 2, :], sq3 * ctp, None, ALU.mult)
            dve.tensor_scalar(up[:, 4, :], ps[1][:, 6, :], 0.01, None, ALU.mult)
            dve.tensor_scalar(m.w_s[:, :], m.w_s[:, :], 0.99, None, ALU.mult)
            dve.tensor_scalar(up[:, 3, :], ps[1][:, 4, :], sq3 * ctp, None, ALU.mult).then_inc(s_ev, 1)
            dve.tensor_copy(m.w_h[0:64, :], ab[:, 1, :])
            dve.tensor_scalar(m.w_o[0:64, 0:64], ps[1][:, 1, :], ctp, None, ALU.mult)
            dve.tensor_scalar(m.w_o[0:64, 64:128], ps[1][:, 3, :], sq3 * ctp, None, ALU.mult)
            dve.memset(m.w_o[0:64, 128:192], 0.0).then_inc(s_ev, 1)
            dve.tensor_scalar(m.w_l[0:64, :], ps[1][:, 7, :], 0.01, None, ALU.mult)
            dve.tensor_scalar(m.w_d[0:64, 0, 0:64], ps[1][:, 5, :], ctp, None, ALU.mult)
            dve.tensor_scalar(m.w_d[0:64, 1, 128:192], ps[1][:, 5, :], ctp, None, ALU.mult).then_inc(s_ev, 1)


@stage
def feed_forward(nc, m, tag, act_func, first, rest, gate):
    n_rest = 0 if rest is None else rest[0].shape[0]
    with ExitStack() as ctx:
        sem = Sems(nc, ctx)

        def sb(name, shape, dt=F32):
            return ctx.enter_context(nc.sbuf_tensor(f"{name}_{tag}", shape, dt))

        w1 = [sb(f"w1{b}", [128, 2, FF]) for b in range(2)]
        w2 = [sb(f"w2{b}", [128, NF, D]) for b in range(2)]
        b1 = [sb(f"b1{b}", [128, NF]) for b in range(2)]
        b2 = [sb(f"b2{b}", [P, D]) for b in range(2)]
        hs = sb("hs", [128, NF, G * P])
        t = sb("t", [P, G, D])
        ps_h = [ctx.enter_context(nc.psum_tensor(f"ps_h{b}_{tag}", [128, 1024], F32)) for b in range(2)]
        ps_y = ctx.enter_context(nc.psum_tensor(f"ps_y_{tag}", [128, 6, 256], F32))
        s_w = [sem(f"s_w{b}_{tag}") for b in range(2)]
        s_h = sem(f"s_h_{tag}")
        s_g = sem(f"s_g_{tag}")
        s_y = sem(f"s_y_{tag}")
        s_t = sem(f"s_t_{tag}")
        s_ch = sem(f"s_ch_{tag}")
        s_exp = sem(f"s_exp_{tag}")
        block = ctx.enter_context(nc.Block())

        @block.sync
        def _(sp):
            def load(w, b):
                for dst, src in zip((w1[b][:, :, :], w2[b][:, :, :], b1[b][:, :], b2[b][:, :]), w):
                    sp.dma_start(dst, src).then_inc(s_w[b], 16)

            with nc.allow_non_contiguous_dma(reason="biases down the partitions, 4 KB each"):
                load([first[0].rearrange("(k p) f -> p k f", p=128), first[2].rearrange("(c p) d -> p c d", p=128),
                      first[1].rearrange("(c p) -> p c", p=128),
                      first[3].rearrange("(o d) -> o d", o=1).to_broadcast([P, D])], 0)
                if rest is not None:
                    def load_rest(e, b):
                        load([rest[0][ds(e, 1)].rearrange("o (k p) f -> p (o k) f", p=128),
                              rest[2][ds(e, 1)].rearrange("o (c p) d -> p (o c) d", p=128),
                              rest[1][ds(e, 1)].rearrange("o (c p) -> p (o c)", p=128),
                              rest[3][ds(e, 1)].to_broadcast([P, D])], b)

                    load_rest(0, 1)
                    with sp.Fori(1, n_rest // 2) as it:
                        sp.wait_ge(s_exp, 2 * it - 1)
                        load_rest(2 * it - 1, 0)
                        sp.wait_ge(s_exp, 2 * it)
                        load_rest(2 * it, 1)
                    sp.wait_ge(s_exp, n_rest - 1)
                    load_rest(n_rest - 1, 0)

        def networks(eng, body):
            with eng.Fori(0, NG) as g:
                body(0, 0, 0, g)
            if rest is not None:
                with eng.Fori(0, n_rest // 2) as it:
                    with eng.Fori(0, NG) as g:
                        body(2 * it + 1, it, 1, g)
                    with eng.Fori(0, NG) as g:
                        body(2 * it + 2, it + 1, 0, g)

        @block.tensor
        def _(pe):
            pe.sem_inc(s_g, 2)

            def body(e, it, b, g):
                n = e * NG + g
                pe.wait_ge(s_w[b], 64 * it + 64)
                for c in range(NF):
                    pe.wait_ge(s_g, n * NF + c + 1)
                    for i in range(2):
                        for k in range(2):
                            last = pe.matmul(ps_h[c % 2][:, 512 * i:512 * i + SPLIT[i + 1] - SPLIT[i]],
                                             w1[b][:, k, c * 128:(c + 1) * 128],
                                             m.h_t[:, k, ds(g * G * P + SPLIT[i], SPLIT[i + 1] - SPLIT[i])],
                                             start=k == 0, stop=k == 1)
                    last.then_inc(s_h, 1)
                pe.wait_ge(s_t, n + 1)
                pe.wait_ge(s_g, n * NF + NF + 2)
                for u in range(G):
                    for c in range(NF):
                        last = pe.matmul(ps_y[0:P, u, :], hs[:, c, u * P:(u + 1) * P], w2[b][:, c, :],
                                         start=c == 0, stop=c == NF - 1)
                last.then_inc(s_y, 1)

            networks(pe, body)

        @block.scalar
        def _(act):
            act.sem_inc(s_y, 1)

            def body(e, it, b, g):
                n = e * NG + g
                act.wait_ge(s_w[b], 64 * it + 64)
                act.wait_ge(s_y, n + 1)
                for c in range(NF):
                    act.wait_ge(s_h, n * NF + c + 1)
                    for i in range(2):
                        last = act.activation(hs[:, c, SPLIT[i]:SPLIT[i + 1]],
                                              ps_h[c % 2][:, 512 * i:512 * i + SPLIT[i + 1] - SPLIT[i]],
                                              act_func, bias=b1[b][:, c:c + 1])
                    last.then_inc(s_g, 1)

            networks(act, body)

        @block.vector
        def _(dve):
            dve.sem_inc(s_t, 1)

            def body(e, it, b, g):
                n = e * NG + g
                dve.wait_ge(s_w[b], 64 * it + 64)
                dve.wait_ge(s_y, n + 2)
                dve.tensor_tensor(t[:, :, :], ps_y[0:P, 0:G, :], b2[b][:, None, :].to_broadcast([P, G, D]), ALU.add
                                  ).then_inc(s_t, 1)
                dve.wait_ge(s_t, n + 2)
                f = gate(e, g)
                if f is not None:
                    dve.tensor_tensor(t[:, :, :], t[:, :, :], f.to_broadcast([P, G, D]), ALU.mult).then_inc(s_ch, 1)
                else:
                    dve.sem_inc(s_ch, 1)
                dve.wait_ge(s_ch, 2 * n + 1)
                x = m.x[:, ds(g * G, G), :]
                dve.tensor_tensor(x, x, t[:, :, :], ALU.add).then_inc(s_ch, 1)
                dve.wait_ge(s_ch, 2 * n + 2)

            with dve.Fori(0, NG) as g:
                body(0, 0, 0, g)
            dve.sem_inc(s_exp, 1)
            if rest is not None:
                with dve.Fori(0, n_rest // 2) as it:
                    with dve.Fori(0, NG) as g:
                        body(2 * it + 1, it, 1, g)
                    dve.sem_inc(s_exp, 1)
                    with dve.Fori(0, NG) as g:
                        body(2 * it + 2, it + 1, 0, g)
                    dve.sem_inc(s_exp, 1)


@stage
def build_top(nc, m):
    with ExitStack() as ctx:
        sem = Sems(nc, ctx)
        ps = ctx.enter_context(nc.psum_tensor("t_ps", [NT, 512], F32))
        wt = ctx.enter_context(nc.sbuf_tensor("t_wt", [NT, P], F32))
        row = ctx.enter_context(nc.sbuf_tensor("t_row", [P, N], F32))
        junk = ctx.enter_context(nc.sbuf_tensor("t_junk", [P, 4, N], BF16))
        part = ctx.enter_context(nc.sbuf_tensor("t_part", [P, NT, 4], F32))
        rank = ctx.enter_context(nc.sbuf_tensor("t_rank", [P, NT], F32))
        s_pe = sem("t_pe")
        s_wt = sem("t_wt")
        s_d = sem("t_d")
        s_r = sem("t_r")
        s_part = sem("t_part")
        s_ch = sem("t_ch")
        block = ctx.enter_context(nc.Block())

        @block.tensor
        def _(pe):
            pe.transpose(ps[:, 0:P], m.w[:, :], m.ident[0:P, 0:P]).then_inc(s_pe, 1)

        @block.sync
        def _(sp):
            sp.wait_ge(s_wt, 1)
            sp.dma_start(m.wrow_d.rearrange("(j p) -> j p", p=P), wt[:, :]).then_inc(s_d, 16)
            sp.wait_ge(s_d, 16)
            sp.dma_start(row[:, :], m.wrow_d.rearrange("(o n) -> o n", o=1).to_broadcast([P, N])).then_inc(s_r, 16)

        @block.vector
        def _(dve):
            dve.wait_ge(s_pe, 1)
            dve.tensor_copy(wt[:, :], ps[:, 0:P]).then_inc(s_wt, 1)
            dve.memset(part[:, :, :], 0.0).then_inc(s_part, 1)
            dve.wait_ge(s_part, 1)
            dve.wait_ge(s_r, 16)
            for j in range(NT):
                a, b = j * P, (j + 1) * P
                mine = m.w[:, j:j + 1]
                dve.wait_ge(s_part, j + 1)
                if j:
                    dve.tensor_scalar(junk[:, 0, 0:a], row[:, 0:a], mine, None, ALU.is_ge, ALU.add,
                                      accum_out=part[:, j, 0:1])
                if j < NT - 1:
                    dve.tensor_scalar(junk[:, 1, b:N], row[:, b:N], mine, None, ALU.is_gt, ALU.add,
                                      accum_out=part[:, j, 1:2])
                dve.tensor_scalar(junk[:, 2, a:b], row[:, a:b], mine, None, ALU.is_gt, ALU.add,
                                  accum_out=part[:, j, 2:3])
                dve.scalar_tensor_tensor(junk[:, 3, 0:P], row[:, a:b], mine,
                                         m.before[0:P, 0:P], ALU.is_equal, ALU.mult, accum_out=part[:, j, 3:4]
                                         ).then_inc(s_part, 1)
            dve.wait_ge(s_part, NT + 1)
            ch = Chain(dve, s_ch)
            ch(dve.tensor_reduce(rank[:, :], part[:, :, :], AX.X, ALU.add))
            ch(dve.tensor_scalar(rank[:, :], rank[:, :], float(KEPT), None, ALU.is_lt))
            ch(dve.tensor_tensor(m.w[:, :], m.w[:, :], rank[:, :], ALU.mult))


@stage
def build_router(nc, m):
    with ExitStack() as ctx:
        sem = Sems(nc, ctx)

        def sb(name, shape, dt=F32):
            return ctx.enter_context(nc.sbuf_tensor(f"r_{name}", shape, dt))

        mx = sb("mx", [P, NT])
        p = sb("p", [P, NT, NE])
        sm = sb("sm", [P, NT])
        cmp_ = sb("cmp", [P, NT, NE])
        rank = sb("rank", [P, NT, NE])
        sel = sb("sel", [P, NT, NE])
        tot = sb("tot", [P, NT, NE])
        upto = sb("upto", [P, NT, NE])
        cnt = sb("cnt", [P, NE])
        cnt_i = sb("cnt_i", [P, 2, NE], I32)
        end = sb("end", [P, NE])
        place = sb("place", [P, NT, NE])
        passed = sb("passed", [1, ETX, NE])
        of_tile = sb("of_tile", [1, ETX])
        ps = ctx.enter_context(nc.psum_tensor("r_ps", [P, 2, 512], F32))
        s_ch = sem("r_ch")
        s_ex = sem("r_ex")
        s_pe = sem("r_pe")
        block = ctx.enter_context(nc.Block())
        shape = [P, NT, NE]
        marks = {}

        @block.scalar
        def _(act):
            act.wait_ge(s_ch, 2)
            act.activation(p[:, :, :], m.mask[:, :, :], ACT.Exp).then_inc(s_ex, 1)

        @block.vector
        def _(dve):
            ch = Chain(dve, s_ch)
            ch(dve.tensor_reduce(mx[:, :], m.mask[:, :, :], AX.X, ALU.max))
            ch(dve.tensor_tensor(m.mask[:, :, :], m.mask[:, :, :], mx[:, :, None].to_broadcast(shape), ALU.subtract))
            dve.wait_ge(s_ex, 1)
            ch(dve.tensor_reduce(sm[:, :], p[:, :, :], AX.X, ALU.add))
            ch(dve.reciprocal(sm[:, :], sm[:, :]))
            ch(dve.tensor_tensor(p[:, :, :], p[:, :, :], sm[:, :, None].to_broadcast(shape), ALU.mult))
            for e in range(NE):
                if e:
                    ch(dve.tensor_tensor(cmp_[:, :, 0:e], p[:, :, 0:e], p[:, :, e:e + 1].to_broadcast([P, NT, e]),
                                         ALU.is_ge))
                ch(dve.tensor_tensor(cmp_[:, :, e:NE], p[:, :, e:NE], p[:, :, e:e + 1].to_broadcast([P, NT, NE - e]),
                                     ALU.is_gt))
                ch(dve.tensor_reduce(rank[:, :, e], cmp_[:, :, :], AX.X, ALU.add))
            ch(dve.tensor_scalar(sel[:, :, :], rank[:, :, :], float(TOP), None, ALU.is_lt))
            marks["sel"] = ch.n
            ch(dve.tensor_tensor(p[:, :, :], p[:, :, :], sel[:, :, :], ALU.mult))
            ch(dve.tensor_reduce(sm[:, :], p[:, :, :], AX.X, ALU.add))
            ch(dve.reciprocal(sm[:, :], sm[:, :]))
            ch(dve.tensor_tensor(p[:, :, :], p[:, :, :], sm[:, :, None].to_broadcast(shape), ALU.mult))
            dve.wait_ge(s_pe, 1)
            ch(dve.tensor_copy(tot.rearrange("p j e -> p (j e)"), ps[:, 0, 0:NT * NE]))
            for e in range(NE):
                dve.tensor_tensor_scan(upto[:, :, e], m.ones[0:P, 0:NT], tot[:, :, e], 0.0, ALU.mult, ALU.add
                                       ).then_inc(s_ch, 1)
                ch.n += 1
            dve.wait_ge(s_ch, ch.n)
            ch(dve.tensor_scalar(cnt[:, :], upto[:, NT - 1, :], float(EP - 1), None, ALU.add))
            ch(dve.tensor_copy(cnt_i[:, 0, :], cnt[:, :]))
            ch(dve.tensor_scalar(cnt_i[:, 1, :], cnt_i[:, 0, :], EP.bit_length() - 1, None, ALU.arith_shift_right))
            ch(dve.tensor_copy(cnt[:, :], cnt_i[:, 1, :]))
            ch(dve.tensor_tensor_scan(end[:, :], m.ones[0:P, 0:NE], cnt[:, :], 0.0, ALU.mult, ALU.add))
            ch(dve.tensor_tensor(cnt[:, :], end[:, :], cnt[:, :], ALU.subtract))
            ch(dve.tensor_tensor(place[:, :, :], upto[:, :, :], tot[:, :, :], ALU.subtract))
            ch(dve.tensor_tensor(place[:, :, :], place[:, :, :],
                                 ps[:, 1, 0:NT * NE].rearrange("p (j e) -> p j e", e=NE), ALU.add))
            ch(dve.scalar_tensor_tensor(place[:, :, :], cnt[:, None, :].to_broadcast(shape), float(EP),
                                        place[:, :, :], ALU.mult, ALU.add))
            for k in range(TOP):
                ch(dve.tensor_scalar(sel[:, :, :], rank[:, :, :], float(k), None, ALU.is_equal))
                ch(dve.tensor_tensor(cmp_[:, :, :], sel[:, :, :], p[:, :, :], ALU.mult))
                ch(dve.tensor_reduce(m.gate[:, :, k], cmp_[:, :, :], AX.X, ALU.add))
                ch(dve.tensor_tensor(cmp_[:, :, :], sel[:, :, :], place[:, :, :], ALU.mult))
                ch(dve.tensor_reduce(sm[:, :], cmp_[:, :, :], AX.X, ALU.add))
                ch(dve.tensor_copy(m.place[:, :, k], sm[:, :]))
            ch(dve.tensor_tensor(passed[:, :, :], m.iota[0:1, 0:ETX, None].to_broadcast([1, ETX, NE]),
                                 end[0:1, None, :].to_broadcast([1, ETX, NE]), ALU.is_ge))
            ch(dve.tensor_reduce(of_tile[:, :], passed[:, :, :], AX.X, ALU.add))
            ch(dve.tensor_scalar(of_tile[:, :], of_tile[:, :], float(NE - 1), None, ALU.min))
            ch(dve.tensor_copy(m.expert[:, :], of_tile[:, :]))
            ch(dve.tensor_scalar(mx[:, :], m.iota[0:P, 0:NT], float(P), m.part[0:P, 0:1], ALU.mult, ALU.add))
            ch(dve.tensor_copy(m.number[:, :], mx[:, :]))

        @block.tensor
        def _(pe):
            flat = sel.rearrange("p j e -> p (j e)")
            pe.wait_ge(s_ch, marks["sel"])
            pe.matmul(ps[:, 0, 0:NT * NE], m.ones[0:P, 0:P], flat, start=True, stop=True)
            pe.matmul(ps[:, 1, 0:NT * NE], m.after[0:P, 0:P], flat, start=True, stop=True).then_inc(s_pe, 1)


@stage
def send_rows(nc, m):
    with ExitStack() as ctx:
        sem = Sems(nc, ctx)
        place = ctx.enter_context(nc.sbuf_tensor("n_place", [P, G, TOP], U32))
        number = ctx.enter_context(nc.sbuf_tensor("n_number", [P, G], U32))
        none = ctx.enter_context(nc.sbuf_tensor("n_none", [EP, ETX], U32))
        s_zero = sem("n_zero")
        s_fill = sem("n_fill")
        s_slot = sem("n_slot")
        s_go = sem("n_go")
        s_sent = sem("n_sent")
        s_back = sem("n_back")
        block = ctx.enter_context(nc.Block())

        @block.vector
        def _(dve):
            dve.memset(none[:, :], 0).then_inc(s_zero, 1)
            dve.tensor_copy(place[:, :, :], m.place[:, 0:G, :])
            dve.tensor_copy(number[:, :], m.number[:, 0:G]).then_inc(s_slot, 1)
            with dve.Fori(1, NG) as g:
                dve.wait_ge(s_sent, 16 * G * TOP * g)
                dve.tensor_copy(place[:, :, :], m.place[:, ds(g * G, G), :])
                dve.tensor_copy(number[:, :], m.number[:, ds(g * G, G)]).then_inc(s_slot, 1)

        @block.gpsimd
        def _(pool):
            pool.wait_ge(s_fill, 16)
            with pool.Fori(0, NG) as g:
                pool.wait_ge(s_slot, g + 1)
                pool.sem_inc(s_go, 1)
                for u in range(G):
                    for k in range(TOP):
                        pool.indirect_dma_start(
                            out=m.list_d[:, :],
                            out_offset=bass.IndirectOffsetOnAxis(ap=place[:, u, k:k + 1], axis=0),
                            in_=number[:, u:u + 1], in_offset=None).then_inc(s_sent, 16)
            pool.wait_ge(s_sent, 16 * NT * TOP)

        @block.sync
        def _(sp):
            sp.wait_ge(s_zero, 1)
            with nc.allow_non_contiguous_dma(reason="one word a row, once"):
                sp.dma_start(m.list_d.rearrange("(p t) o -> p (t o)", p=EP), none[:, :]).then_inc(s_fill, 16)
                sp.wait_ge(s_fill, 16)
                sp.wait_ge(s_sent, 16 * NT * TOP)
                sp.dma_start(m.rows_of[:, :], m.list_d.rearrange("(t p) o -> p (t o)", p=EP)).then_inc(s_back, 16)
                sp.wait_ge(s_back, 16)


@stage
def build_experts(nc, m, a):
    with ExitStack() as ctx:
        sem = Sems(nc, ctx)

        def sb(name, shape, dt=F32):
            return ctx.enter_context(nc.sbuf_tensor(f"e_{name}", shape, dt))

        w1 = sb("w1", [128, NE, 2, FF])
        w2 = sb("w2", [128, NE, NF, D])
        b1 = sb("b1", [128, NE, NF])
        b2 = sb("b2", [128, NE, D])
        idx = [sb(f"idx{r}", [EP, 1], U32) for r in range(ER)]
        rows = [sb(f"rows{r}", [EP, D]) for r in range(ER)]
        xt = [sb(f"xt{b}", [128, 2, EP]) for b in range(2)]
        h = sb("h", [EP, FF])
        ht = sb("ht", [128, NF, EP])
        y = [sb(f"y{b}", [EP, D]) for b in range(2)]
        ps_x = ctx.enter_context(nc.psum_tensor("e_psx", [128, 4, EP], F32))
        ps_h = ctx.enter_context(nc.psum_tensor("e_psh", [EP, FF], F32))
        ps_t = ctx.enter_context(nc.psum_tensor("e_pst", [128, NF, EP], F32))
        ps_y = [ctx.enter_context(nc.psum_tensor(f"e_psy{b}", [EP, 512], F32)) for b in range(2)]
        s_w1 = sem("e_w1")
        s_w2 = sem("e_w2")
        s_b = sem("e_b")
        s_idx = sem("e_idx")
        s_go = sem("e_go")
        s_x = [sem(f"e_x{r}") for r in range(ER)]
        s_tr = sem("e_tr")
        s_xt = sem("e_xt")
        s_h = sem("e_h")
        s_hs = sem("e_hs")
        s_ht = sem("e_ht")
        s_g = sem("e_g")
        s_y = sem("e_y")
        s_ys = sem("e_ys")
        s_out = [sem(f"e_out{b}") for b in range(2)]
        block = ctx.enter_context(nc.Block())

        @block.sync
        def _(sp):
            with nc.allow_non_contiguous_dma(reason="biases down the partitions"):
                sp.dma_start(b1[:, :, :], a["L1_ffn_b1p"].rearrange("e (c p) -> p e c", p=128)).then_inc(s_b, 16)
            for e in range(NE):
                sp.dma_start(w1[:, e, :, :], a["L1_ffn_W1p"][e].rearrange("(k p) f -> p k f", p=128)
                             ).then_inc(s_w1, 16)

            def store(t, b):
                sp.wait_ge(s_ys, t + 1)
                sp.dma_start(m.y_d[ds(t * EP, EP), :], y[b][:, :]).then_inc(s_out[b], 16)

            with sp.Fori(0, ET // 2) as it:
                for b in range(2):
                    store(2 * it + b, b)
            for b in range(2):
                sp.wait_ge(s_out[b], 16 * ET // 2)

        @block.gpsimd
        def _(pool):
            def gather(t, r):
                pool.wait_ge(s_idx, t + 1)
                pool.sem_inc(s_go, 1)
                if not (known(t) and t < ER):
                    pool.wait_ge(s_tr, t - ER + 1)
                    pool.sem_inc(s_go, 1)
                pool.indirect_dma_start(out=rows[r][:, :], out_offset=None, in_=m.h_d[:, :],
                                        in_offset=bass.IndirectOffsetOnAxis(ap=idx[r][:, :], axis=0)
                                        ).then_inc(s_x[r], 16)

            for t in range(ER):
                gather(t, t)
            with pool.Fori(1, ET // ER) as it:
                for r in range(ER):
                    gather(ER * it + r, r)
            for r in range(2):
                gather(ET + r, r)
            for r in range(2):
                pool.wait_ge(s_x[r], 16 * (ET // ER + 1))

        @block.tensor
        def _(pe):
            def turn(t, it, r):
                pe.wait_ge(s_x[r], 16 * it + 16)
                if not (known(t) and t < 1):
                    pe.wait_ge(s_xt, t)
                for k in range(2):
                    last = pe.transpose(ps_x[:, k, :], rows[r][:, k * 128:(k + 1) * 128], m.ident[:, :])
                last.then_inc(s_tr, 1)

            def layer1(t, b):
                e = pe.value_load(m.expert[0:1, ds(t, 1)], min_val=0, max_val=NE - 1)
                pe.wait_ge(s_xt, t + 1)
                if not (known(t) and t < 1):
                    pe.wait_ge(s_hs, t)
                for i in range(2):
                    for k in range(2):
                        last = pe.matmul(ps_h[:, i * 512:(i + 1) * 512], xt[b][:, k, :],
                                         w1[:, e, k, i * 512:(i + 1) * 512], start=k == 0, stop=k == 1)
                last.then_inc(s_h, 1)

            def turn_h(t):
                pe.wait_ge(s_hs, t + 1)
                for c in range(NF):
                    last = pe.transpose(ps_t[:, c, :], h[:, c * 128:(c + 1) * 128], m.ident[:, :])
                last.then_inc(s_ht, 1)

            def layer2(t, b):
                e = pe.value_load(m.expert[0:1, ds(t, 1)], min_val=0, max_val=NE - 1)
                pe.wait_ge(s_g, t + 1)
                for c in range(NF):
                    last = pe.matmul(ps_y[b][:, 0:D], ht[:, c, :], w2[:, e, c, :], start=c == 0, stop=c == NF - 1)
                last.then_inc(s_y, 1)

            turn(0, 0, 0)
            turn(1, 0, 1)
            pe.wait_ge(s_w1, 16 * NE)
            layer1(0, 0)
            turn_h(0)
            pe.wait_ge(s_w2, 16 * NE)
            with pe.Fori(0, ET // ER) as it:
                for r in range(ER):
                    t, b = ER * it + r, r % 2
                    turn(t + 2, it if r < ER - 2 else it + 1, (r + 2) % ER)
                    layer1(t + 1, 1 - b)
                    layer2(t, b)
                    turn_h(t + 1)

        @block.scalar
        def _(act):
            def index(t, r):
                act.activation(idx[r][:, :], m.rows_of[:, ds(t, 1)], ACT.Copy).then_inc(s_idx, 1)

            def turned(t, b):
                act.wait_ge(s_tr, t + 1)
                act.activation(xt[b][:, :, :], ps_x[:, 0:2, :], ACT.Copy).then_inc(s_xt, 1)

            def gelu(t):
                e = act.value_load(m.expert[0:1, ds(t, 1)], min_val=0, max_val=NE - 1)
                act.wait_ge(s_ht, t + 1)
                for c in range(NF):
                    last = act.activation(ht[:, c, :], ps_t[:, c, :], ACT.Gelu, bias=b1[:, e, c:c + 1])
                last.then_inc(s_g, 1)

            for e in range(NE):
                act.dma_start(w2[:, e, :, :], a["L1_ffn_W2p"][e].rearrange("(c p) d -> p c d", p=128)
                              ).then_inc(s_w2, 16)
                act.dma_start(b2[:, e, :], a["L1_ffn_b2p"][e].rearrange("(o d) -> o d", o=1).to_broadcast([128, D])
                              ).then_inc(s_b, 16)
            for t in range(ER):
                index(t, t)
            turned(0, 0)
            turned(1, 1)
            act.wait_ge(s_b, 16 * NE + 16)
            gelu(0)
            with act.Fori(0, ET // ER) as it:
                for r in range(ER):
                    t, b = ER * it + r, r % 2
                    act.wait_ge(s_h, t + 2)
                    turned(t + 2, b)
                    act.wait_ge(s_x[r], 16 * it + 16)
                    index(t + ER, r)
                    gelu(t + 1)

        @block.vector
        def _(dve):
            def first(t):
                dve.wait_ge(s_h, t + 1)
                if not (known(t) and t < 1):
                    dve.wait_ge(s_ht, t)
                dve.tensor_copy(h[:, :], ps_h[:, :]).then_inc(s_hs, 1)

            dve.wait_ge(s_b, 16 * NE + 16)
            first(0)
            dve.wait_ge(s_ht, 1)

            def second(t, it, b):
                e = dve.value_load(m.expert[0:1, ds(t, 1)], min_val=0, max_val=NE - 1)
                dve.wait_ge(s_y, t + 1)
                if not known(it):
                    dve.wait_ge(s_out[b], 16 * it)
                dve.tensor_tensor(y[b][:, :], ps_y[b][:, 0:D], b2[:, e, :], ALU.add).then_inc(s_ys, 1)

            for t in range(2):
                first(t + 1)
                second(t, 0, t)
            with dve.Fori(1, ET // 2) as it:
                for b in range(2):
                    first(2 * it + b + 1)
                    second(2 * it + b, it, b)


@stage
def combine_experts(nc, m):
    with ExitStack() as ctx:
        sem = Sems(nc, ctx)
        place = [ctx.enter_context(nc.sbuf_tensor(f"c_place{k}", [P, G], U32)) for k in range(TOP)]
        y = [[ctx.enter_context(nc.sbuf_tensor(f"c_y{u}{k}", [P, D], F32)) for k in range(TOP)] for u in range(G)]
        s_slot = sem("c_slot")
        s_go = sem("c_go")
        s_y = [sem(f"c_y{u}") for u in range(G)]
        s_add = sem("c_add")
        s_done = sem("c_done")
        block = ctx.enter_context(nc.Block())

        @block.scalar
        def _(act):
            def slots(g):
                for k in range(TOP):
                    act.activation(place[k][:, :], m.place[:, ds(g * G, G), k], ACT.Copy).then_inc(s_slot, 1)

            slots(0)
            with act.Fori(1, NG) as g:
                for u in range(G):
                    act.wait_ge(s_y[u], 16 * TOP * g)
                slots(g)

        @block.gpsimd
        def _(pool):
            def gather(g):
                pool.wait_ge(s_slot, TOP * g + TOP)
                pool.sem_inc(s_go, 1)
                if not known(g):
                    pool.wait_ge(s_done, g)
                    pool.sem_inc(s_go, 1)
                for u in range(G):
                    for k in range(TOP):
                        pool.indirect_dma_start(out=y[u][k][:, :], out_offset=None, in_=m.y_d[:, :],
                                                in_offset=bass.IndirectOffsetOnAxis(ap=place[k][:, u:u + 1], axis=0)
                                                ).then_inc(s_y[u], 16)

            gather(0)
            with pool.Fori(1, NG) as g:
                gather(g)

        @block.vector
        def _(dve):
            with dve.Fori(0, NG) as g:
                for u in range(G):
                    dve.wait_ge(s_y[u], 16 * TOP * g + 16 * TOP)
                    x = m.x[:, g * G + u, :]
                    for k in range(TOP):
                        if u or k:
                            dve.wait_ge(s_add, g * G * TOP + u * TOP + k)
                        dve.scalar_tensor_tensor(x, y[u][k][:, :], m.gate[:, g * G + u, k:k + 1], x,
                                                 ALU.mult, ALU.add).then_inc(s_add, 1)
                dve.wait_ge(s_add, (g + 1) * G * TOP)
                dve.sem_inc(s_done, 1)


@stage
def move(nc, tag, loads):
    with ExitStack() as ctx:
        sem = Sems(nc, ctx)
        s = [sem(f"mv_{tag}{i}") for i in range(2)]
        block = ctx.enter_context(nc.Block())

        def issue(eng, mine, s_mine):
            for dst, src in mine:
                eng.dma_start(dst, src).then_inc(s_mine, 16)
            if mine:
                eng.wait_ge(s_mine, 16 * len(mine))

        @block.sync
        def _(sp):
            issue(sp, loads[0::2], s[0])

        @block.scalar
        def _(act):
            issue(act, loads[1::2], s[1])


class Memory:
    pass


def build(nc, a, out):
    m = Memory()
    with ExitStack() as top:
        def sb(name, shape, dt=F32, to=top):
            return to.enter_context(nc.sbuf_tensor(name, shape, dt))

        def dram(name, shape, dt=F32):
            return nc.dram_tensor(name, shape, dt, kind="Internal").ap()

        m.rec_d = dram("rec_d", [TX * EP, REC])
        m.row_d = dram("row_d", [2, E])
        m.k_d = dram("k_d", [N, D])
        m.v_d = dram("v_d", [N, D])
        m.h_d = dram("h_d", [N, D])
        m.ends_d = dram("ends_d", [4 * NBLK, 128])
        m.carry_d = dram("carry_d", [2 * NBLK, 128])
        m.list_d = dram("list_d", [ETX * EP, 1], U32)
        m.y_d = dram("y_d", [ET * EP, D])
        m.wrow_d = dram("wrow_d", [N])

        m.ident = sb("ident", [128, 128])
        m.ident_b = sb("ident_b", [128, 128], BF16)
        m.ones = sb("ones", [128, 128])
        m.before = sb("before", [128, 128])
        m.after = sb("after", [128, 128])
        m.iota = sb("iota", [128, T])
        m.part = sb("part", [128, 1])
        m.x = sb("x", [P, NT, D])
        edges = top.enter_context(ExitStack())
        m.node_tile = sb("node_tile", [1, T], I32, to=edges)
        m.h = sb("h", [P, NT, D], to=edges)
        agg_full = sb("agg", [128, NT, 448], to=edges)
        m.agg = agg_full[0:P, :, :]
        m.spare = agg_full[:, :, :].rearrange("p j c -> p (j c)")
        m.rec = sb("rec", [EP, TX, REC], to=edges)
        m.src = sb("src", [EP, TX], U32, to=edges)
        m.unit = sb("unit", [EP, TX, 3], to=edges)
        m.unit2 = sb("unit2", [EP, TX], to=edges)
        rows = lambda ap: ap.rearrange("(j p) d -> p j d", p=P)
        vec = lambda ap, n=P: ap.rearrange("(o d) -> o d", o=1).to_broadcast([n, ap.shape[0]])
        half = lambda ap: ap.rearrange("(k p) n -> p k n", p=128)

        build_constants(nc, m)
        build_sort(nc, m, a)
        build_reload(nc, m)

        with ExitStack() as l0:
            m.v = sb("v", [P, NT, D], to=l0)
            m.s = sb("s", [EP, T, H], to=l0)
            m.rel = sb("rel", [NREL, HD], to=l0)
            l0q = l0.enter_context(ExitStack())
            m.q = sb("q", [P, NT, D], to=l0q)
            move(nc, "x", [(m.x[:, :, :], rows(a["x"])), (m.rel[:, :], a["L0_gnn_rel_w"])])
            layer_norm(nc, m, "n0", m.x, m.h)
            with ExitStack() as c1:
                qe = sb("qe", [P, D], to=c1)
                bias = [sb(f"bias{i}", [P, D], to=c1) for i in range(3)]
                wqkv = [sb(f"wqkv{i}", [128, 2, D], to=c1) for i in range(3)]
                move(nc, "qkv", [(qe[:, :], vec(a["L0_gnn_query_emb"]))]
                     + [(bias[i][:, :], vec(a["L0_gnn_b" + c])) for i, c in enumerate("qkv")]
                     + [(wqkv[i][:, :, :], half(a["L0_gnn_W" + c])) for i, c in enumerate("qkv")])
                scale_qkv(nc, m, qe, bias[0])

                def enhance(dve, g, slot, ch):
                    return dve.tensor_tensor(slot[:, :, :], m.h[:, ds(g * G, G), :],
                                             qe[:, None, :].to_broadcast([P, G, D]), ALU.add)

                def take(dve, g, c, ps, ch):
                    b = bias[c][:, None, :].to_broadcast([P, G, D])
                    if c == 0:
                        return dve.scalar_tensor_tensor(m.q[:, ds(g * G, G), :], ps, 0.125, b, ALU.mult, ALU.add)
                    to = m.agg[:, ds(g * G, G), 0:D] if c == 1 else m.v[:, ds(g * G, G), :]
                    return dve.tensor_tensor(to, ps, b, ALU.add)

                project(nc, m, "qkv", enhance, wqkv, D, take)
            move(nc, "kv", [(rows(m.k_d), m.agg[:, :, 0:D]), (rows(m.v_d), m.v[:, :, :])])
            build_scores(nc, m)
            l0q.close()
            build_weights(nc, m)
            build_values(nc, m)
            m.q = sb("y", [P, NT, D], to=l0)
            with ExitStack() as c1:
                rd = sb("rd", [P, NT, H], to=c1)
                dz = sb("dz", [P, NT, H], to=c1)
                bo = sb("bo", [P, D], to=c1)
                wo = sb("wo", [128, 2, D], to=c1)
                tmp = sb("tmp", [P, G, D], to=c1)
                move(nc, "wo", [(bo[:, :], vec(a["L0_gnn_bo"])), (wo[:, :, :], half(a["L0_gnn_Wo"]))])
                divide_sums(nc, m, rd, dz)
                hd = lambda ap: ap.rearrange("p u (h d) -> p u h d", h=H)

                def normalise(dve, g, slot, ch):
                    gs = ds(g * G, G)
                    shape = [P, G, H, HD]
                    ch(dve.tensor_tensor(hd(slot[:, :, :]), hd(m.agg[:, gs, 0:D]),
                                         rd[:, gs, :, None].to_broadcast(shape), ALU.mult))
                    ch(dve.tensor_tensor(hd(tmp[:, :, :]), hd(m.v[:, gs, :]), dz[:, gs, :, None].to_broadcast(shape),
                                         ALU.mult))
                    return dve.tensor_tensor(slot[:, :, :], slot[:, :, :], tmp[:, :, :], ALU.add)

                def residual(dve, g, c, ps, ch):
                    ch(dve.tensor_tensor(tmp[:, :, :], ps, bo[:, None, :].to_broadcast([P, G, D]), ALU.add))
                    return dve.tensor_tensor(m.q[:, ds(g * G, G), :], tmp[:, :, :], m.h[:, ds(g * G, G), :], ALU.add)

                project(nc, m, "wo", normalise, [wo], D, residual, own=3)
            with ExitStack() as c1:
                gb = [sb(f"gb{i}", [P, D], to=c1) for i in range(2)]
                move(nc, "gb", [(gb[0][:, :], vec(a["L0_gnn_gamma"])), (gb[1][:, :], vec(a["L0_gnn_beta"]))])
                layer_norm(nc, m, "n1", m.q, m.v, gb[0], gb[1])
            add_all(nc, "l0", [(m.x[:, :, :], m.x[:, :, :], m.v[:, :, :])])

        layer_norm(nc, m, "n2", m.x, m.h)
        with ExitStack() as c0:
            m.h_t = sb("h_t0", [128, 2, N], to=c0)
            m.w = sb("w", [P, NT], to=c0)
            with ExitStack() as c1:
                wr = sb("wr", [128, 2, 1], to=c1)
                br = sb("br", [P, 1], to=c1)
                with nc.allow_non_contiguous_dma(reason="256 words, once"):
                    move(nc, "wr", [(wr[:, :, :], half(a["L0_ffn_wr"])), (br[:, :], vec(a["L0_ffn_br"]))])

                def copy_rows(dve, g, slot, ch):
                    return dve.tensor_copy(slot[:, :, :], m.h[:, ds(g * G, G), :])

                def keep(g, k):
                    return m.h_t[:, k, ds(g * G * P, G * P)].rearrange("p (u n) -> p u n", u=G)

                def take_w(dve, g, c, ps, ch):
                    return dve.tensor_scalar(m.w[:, ds(g * G, G)], ps[:, :, 0], br[:, 0:1], None, ALU.add)

                project(nc, m, "wr", copy_rows, [wr], 1, take_w, keep=keep)
            build_top(nc, m)
            add_all(nc, "f0", [(m.x[:, :, :], m.x[:, :, :], m.h[:, :, :])])
            feed_forward(nc, m, "f0", ACT.Gelu_apprx_tanh,
                         [a["L0_ffn_w1"], a["L0_ffn_b1"], a["L0_ffn_w2"], a["L0_ffn_b2"]], None,
                         lambda e, g: m.w[:, ds(g * G, G), None])

        layer_norm(nc, m, "n3", m.x, m.h)
        with ExitStack() as c0:
            m.w_h = sb("w_h", [128, 64], to=c0)
            m.w_o = sb("w_o", [128, 192], to=c0)
            m.w_d = sb("w_d", [128, 2, 192], to=c0)
            m.w_s = sb("w_s", [64, 64], to=c0)
            m.w_l = sb("w_l", [128, 64], to=c0)
            move(nc, "h", [(rows(m.h_d), m.h[:, :, :]), (m.w_s[:, :], a["L1_gnn_lin_scalar_w"])])
            scale_logits(nc, m)
            build_geometric_weights(nc, m, a)
            build_geometric(nc, m)
            with ExitStack() as c1:
                tmp = sb("tmp1", [P, G, D], to=c1)

                def vectors(dve, g, slot, ch):
                    ch(dve.memset(slot[:, :, 192:256], 0.0))
                    return dve.tensor_copy(slot[:, :, 0:192].rearrange("p u (k c) -> p u k c", k=3),
                                           m.agg[:, ds(g * G, G), 64:256].rearrange("p u (c k) -> p u k c", k=3))

                def joined(dve, g, c, ps, ch):
                    gs = ds(g * G, G)
                    ch(dve.tensor_copy(tmp[:, :, 0:64], m.agg[:, gs, 0:64]))
                    ch(dve.tensor_tensor(tmp[:, :, 64:256].rearrange("p u (c k) -> p u k c", k=3),
                                         ps.rearrange("p u (k c) -> p u k c", k=3),
                                         m.agg[:, gs, 256:448].rearrange("p u (k c) -> p u k c", k=3), ALU.add))
                    ch(dve.tensor_tensor(tmp[:, :, :], tmp[:, :, :], m.h[:, gs, :], ALU.add))
                    return dve.tensor_tensor(m.x[:, gs, :], m.x[:, gs, :], tmp[:, :, :], ALU.add)

                project(nc, m, "wd", vectors, [m.w_d], 192, joined, own=4)

        edges.close()
        m.mask = sb("mask1", [P, NT, NE])
        m.gate = sb("gate", [P, NT, TOP])
        m.place = sb("place", [P, NT, TOP], U32)
        m.number = sb("number", [P, NT], U32)
        m.expert = sb("expert", [1, ETX], I32)
        m.rows_of = sb("rows_of", [EP, ETX], U32)
        with ExitStack() as c0:
            m.h_t = sb("h_t1", [128, 2, N], to=c0)
            with ExitStack() as c1:
                m.h = sb("h1", [P, NT, D], to=c1)
                wr = sb("wr1", [128, 2, NE], to=c1)
                layer_norm(nc, m, "n4", m.x, m.h)
                move(nc, "wr1", [(rows(m.h_d), m.h[:, :, :]), (wr[:, :, :], half(a["L1_ffn_Wr"]))])

                def take_l(dve, g, c, ps, ch):
                    return dve.tensor_copy(m.mask[:, ds(g * G, G), :], ps)

                def keep1(g, k):
                    return m.h_t[:, k, ds(g * G * P, G * P)].rearrange("p (u n) -> p u n", u=G)

                project(nc, m, "wr1", lambda dve, g, slot, ch: dve.tensor_copy(slot[:, :, :], m.h[:, ds(g * G, G), :]),
                        [wr], NE, take_l, keep=keep1)
            build_router(nc, m)
            send_rows(nc, m)
            feed_forward(nc, m, "f1", ACT.Gelu,
                         [a["L1_ffn_W1s"], a["L1_ffn_b1s"], a["L1_ffn_W2s"], a["L1_ffn_b2s"]], None,
                         lambda e, g: None)
        build_experts(nc, m, a)
        combine_experts(nc, m)
        move(nc, "out", [(rows(out), m.x[:, :, :])])


@stage
def scale_qkv(nc, m, qe, bq):
    with ExitStack() as ctx:
        s = Sems(nc, ctx)("sc_qkv")
        block = ctx.enter_context(nc.Block())

        @block.vector
        def _(dve):
            ch = Chain(dve, s)
            ch(dve.tensor_scalar(qe[:, :], qe[:, :], 0.1, None, ALU.mult))
            ch(dve.tensor_scalar(bq[:, :], bq[:, :], 0.125, None, ALU.mult))
            ch(dve.tensor_scalar(m.rel[:, :], m.rel[:, :], 0.2, None, ALU.mult))


@stage
def scale_logits(nc, m):
    with ExitStack() as ctx:
        s = Sems(nc, ctx)("sc_log")
        block = ctx.enter_context(nc.Block())

        @block.vector
        def _(dve):
            Chain(dve, s)(dve.tensor_scalar(m.w_s[:, :], m.w_s[:, :], 0.125, None, ALU.mult))


@stage
def divide_sums(nc, m, rd, dz):
    with ExitStack() as ctx:
        s = Sems(nc, ctx)("sc_div")
        block = ctx.enter_context(nc.Block())

        @block.vector
        def _(dve):
            ch = Chain(dve, s)
            ch(dve.tensor_scalar(dz[:, :, :], m.agg[:, :, D:D + H], 0.0, None, ALU.is_equal))
            ch(dve.tensor_tensor(rd[:, :, :], m.agg[:, :, D:D + H], dz[:, :, :], ALU.add))
            ch(dve.reciprocal(rd[:, :, :], rd[:, :, :]))


_INS = ["x", "src", "dst", "edge_attr_3", "edge_type_64", "L0_gnn_query_emb", "L0_gnn_Wq", "L0_gnn_bq", "L0_gnn_Wk",
        "L0_gnn_bk", "L0_gnn_Wv", "L0_gnn_bv", "L0_gnn_rel_w", "L0_gnn_Wo", "L0_gnn_bo", "L0_gnn_gamma",
        "L0_gnn_beta", "L0_ffn_wr", "L0_ffn_br", "L0_ffn_w1", "L0_ffn_b1", "L0_ffn_w2", "L0_ffn_b2",
        "L1_gnn_lin_src_w0", "L1_gnn_lin_src_w1", "L1_gnn_tp1_w00", "L1_gnn_tp1_w11", "L1_gnn_tp1_w01",
        "L1_gnn_tp1_w10", "L1_gnn_tp2_w00", "L1_gnn_tp2_w11", "L1_gnn_tp2_w01", "L1_gnn_tp2_w10",
        "L1_gnn_lin_hidden_w0", "L1_gnn_lin_hidden_w1", "L1_gnn_lin_scalar_w", "L1_ffn_Wr", "L1_ffn_W1s",
        "L1_ffn_b1s", "L1_ffn_W2s", "L1_ffn_b2s", "L1_ffn_W1p", "L1_ffn_b1p", "L1_ffn_W2p", "L1_ffn_b2p"]


def kernel(**inputs):
    import numpy as _np
    import concourse.bacc as _bacc
    from concourse import mybir as _mybir
    from concourse.bass_utils import run_bass_kernel_spmd as _run

    nc = _bacc.Bacc("TRN2", target_bir_lowering=False, num_devices=1)
    arrays, args = {}, {}
    for name in _INS:
        x = _np.ascontiguousarray(inputs[name])
        arrays[f"in_{name}"] = x
        args[name] = nc.dram_tensor(f"in_{name}", x.shape, _mybir.dt.from_np(x.dtype), kind="ExternalInput").ap()
    out = nc.dram_tensor("out_0", (N, D), _mybir.dt.float32, kind="ExternalOutput").ap()
    build(nc, args, out)
    r = _run(nc, [arrays], core_ids=[0])
    return r.results[0]["out_0"]
```

```python
from contextlib import ExitStack

import numpy as np
import concourse.bass as bass
from concourse import mybir

ALU = mybir.AluOpType
ACT = mybir.ActivationFunctionType
F32 = mybir.dt.float32
BF16 = mybir.dt.bfloat16
I32 = mybir.dt.int32
U32 = mybir.dt.uint32
AX = mybir.AxisListType
ENGINE = mybir.EngineType
ds = bass.ds

N = 3125
E = 50000
D = 256
P = 125
NT = N // P
G = 5
NG = NT // G
H, HD = 4, 64
NREL = 64
EP = 128
U = 4
CH = U * P
SORT_STEPS = E // CH
T = -(-((E + NT * (EP - 1)) // EP) // (2 * U)) * 2 * U
STEPS = T // U
TX = T + 8 * U
REC = 8
R_SRC, R_LO, R_TYPE, R_VEC, R_DST = 0, 1, 2, 3, 6
BIG = 1.0e30
FF = 1024
NF = FF // 128
NE = 8
KEPT = max(1, N // 2) - 1
EPS = 1e-5
EARLY = NE - -(-NF * G * P // (NF * D))
TOP = 2
ER = 4
ET = -(-((N * TOP + NE * (EP - 1)) // EP) // ER) * ER
ETX = ET + 2 * ER
NBLK = T * H // 128
SPLIT = (0, 320, G * P)


class Sems:

    def __init__(self, nc, ctx):
        self.nc, self.ctx = nc, ctx

    def __call__(self, name):
        return self.nc.alloc_semaphore(name)


def stage(build_stage):
    def staged(nc, *args, **kw):
        with nc.cleanup_on_exit():
            build_stage(nc, *args, **kw)
    return staged


class Chain:

    def __init__(self, eng, sem):
        self.eng, self.sem, self.n = eng, sem, 0

    def __call__(self, ins):
        self.n += 1
        ins.then_inc(self.sem, 1)
        self.eng.wait_ge(self.sem, self.n)


@stage
def build_constants(nc, m):
    with ExitStack() as ctx:
        sem = Sems(nc, ctx)
        iota_i = ctx.enter_context(nc.sbuf_tensor("iota_i", [128, T], I32))
        part_i = ctx.enter_context(nc.sbuf_tensor("part_i", [128, 1], I32))
        s_made = sem("c_made")
        s_cast = sem("c_cast")
        block = ctx.enter_context(nc.Block())

        @block.gpsimd
        def _(pool):
            ch = Chain(pool, s_made)
            ch(pool.memset(m.ones[:, :], 1.0))
            ch(pool.iota(iota_i[:, :], pattern=[[1, T]], base=0, channel_multiplier=0))
            ch(pool.iota(part_i[:, :], pattern=[[0, 1]], base=0, channel_multiplier=1))
            ch(pool.memset(m.ident[:, :], 0.0))
            ch(pool.affine_select(out=m.ident[:, :], in_=m.ident[:, :], compare_op=ALU.not_equal, fill=1.0,
                                  base=0, pattern=[[-1, 128]], channel_multiplier=1))
            ch(pool.affine_select(out=m.before[:, :], in_=m.ones[:, :], compare_op=ALU.is_gt, fill=0.0,
                                  base=0, pattern=[[-1, 128]], channel_multiplier=1))
            ch(pool.affine_select(out=m.after[:, :], in_=m.ones[:, :], compare_op=ALU.is_gt, fill=0.0,
                                  base=0, pattern=[[1, 128]], channel_multiplier=-1))

        @block.vector
        def _(dve):
            ch = Chain(dve, s_cast)
            dve.wait_ge(s_made, 7)
            ch(dve.tensor_copy(m.iota[:, :], iota_i[:, :]))
            ch(dve.tensor_copy(m.part[:, :], part_i[:, :]))
            ch(dve.tensor_copy(m.ident_b[:, :], m.ident[:, :]))


@stage
def build_sort(nc, m, a):
    with ExitStack() as ctx:
        sem = Sems(nc, ctx)

        def sb(name, shape, dt=F32):
            return ctx.enter_context(nc.sbuf_tensor(name, shape, dt))

        Q = 100
        NB = E // (Q * P)
        rec_in = sb("rec_in", [P, SORT_STEPS * U, REC])
        hi = sb("hi", [P, SORT_STEPS * U])
        lo = sb("lo", [P, SORT_STEPS * U])
        hi_hot = sb("hi_hot", [P, SORT_STEPS * U, NT], BF16)
        lo_hot = [sb(f"lo_hot{i}", [P, U, P], BF16) for i in range(2)]
        start = sb("start", [P, NT])
        row_d = m.row_d

        with ExitStack() as c1:
            def sb1(name, shape, dt=F32):
                return c1.enter_context(nc.sbuf_tensor(name, shape, dt))

            sem1 = Sems(nc, c1)
            nat_i = [sb1(f"nat_i{i}", [Q, NB, P], I32) for i in range(3)]
            nat_v = sb1("nat_v", [Q, NB, 3 * P])
            nat_f = [sb1(f"nat_f{i}", [Q, NB, P]) for i in range(3)]
            nat_hi = [sb1(f"nat_hi{i}", [Q, NB, P]) for i in range(2)]
            nat_lo = sb1("nat_lo", [Q, NB, P])
            nat_b = sb1("nat_b", [Q, 2, NB, P], BF16)
            empty = sb1("empty", [EP, TX, REC])
            ps = [c1.enter_context(nc.psum_tensor(f"ps_f{i}", [P, 512], F32)) for i in range(8)]
            s_in = [sem1(f"s_in{i}") for i in range(4)]
            s_flt = sem1("s_flt")
            s_lo = sem1("s_lo")
            s_tr = sem1("s_tr")
            s_empty = sem1("s_empty")
            s_row = sem1("s_row")
            s_fill = sem1("s_fill")
            s_rec = sem1("s_rec")
            s_hot = sem1("s_hot")
            block = c1.enter_context(nc.Block())
            cols = [(nat_f[1], None, R_SRC), (nat_lo, None, R_LO), (nat_f[2], None, R_TYPE),
                    (nat_v, 0, R_VEC), (nat_v, 1, R_VEC + 1), (nat_v, 2, R_VEC + 2), (nat_f[0], None, R_DST),
                    (nat_hi[0], None, None)]

            @block.sync
            def _(sp):
                for i, x in enumerate((a["dst"], a["src"], a["edge_type_64"])):
                    sp.dma_start(nat_i[i][:, :, :], x.rearrange("(b q p) -> q b p", b=NB, q=Q)).then_inc(s_in[i], 16)
                sp.dma_start(nat_v[:, :, :], a["edge_attr_3"].rearrange("(b q p) c -> q b (p c)", b=NB, q=Q)
                             ).then_inc(s_in[3], 16)
                sp.wait_ge(s_empty, 3)
                sp.dma_start(m.rec_d.rearrange("(p t) c -> p t c", p=EP), empty[:, :, :]).then_inc(s_fill, 16)
                sp.wait_ge(s_lo, 28)
                for i in range(2):
                    sp.dma_start(row_d[i, :].rearrange("(b q p) -> q b p", b=NB, q=Q), nat_b[:, i, :, :]
                                 ).then_inc(s_row, 16)
                sp.wait_ge(s_row, 32)
                sp.wait_ge(s_fill, 16)

            @block.gpsimd
            def _(pool):
                ch = Chain(pool, s_empty)
                ch(pool.memset(empty[:, :, :], 0.0))
                ch(pool.memset(empty[:, :, R_LO:R_LO + 1], -1.0))
                ch(pool.memset(empty[:, :, R_DST:R_DST + 1], -1.0))

            @block.vector
            def _(dve):
                for i in range(3):
                    dve.wait_ge(s_in[i], 16)
                    dve.tensor_copy(nat_f[i][:, :, :], nat_i[i][:, :, :]).then_inc(s_flt, 1)
                dve.wait_ge(s_flt, 3)
                ch = Chain(dve, s_lo)
                ch(dve.memset(nat_hi[0][:, :, :], 0.0))
                for k in range(1, NT):
                    ch(dve.scalar_tensor_tensor(nat_hi[k % 2][:, :, :], nat_f[0][:, :, :], float(k * P),
                                                nat_hi[(k + 1) % 2][:, :, :], ALU.is_ge, ALU.add))
                ch(dve.scalar_tensor_tensor(nat_lo[:, :, :], nat_hi[0][:, :, :], -float(P), nat_f[0][:, :, :],
                                            ALU.mult, ALU.add))
                ch(dve.tensor_copy(nat_b[:, 0, :, :], nat_lo[:, :, :]))
                ch(dve.tensor_copy(nat_b[:, 1, :, :], nat_hi[0][:, :, :]))
                dve.memset(rec_in[:, :, :], 0.0).then_inc(s_rec, 1)
                dve.wait_ge(s_rec, 1)
                for k, (_, _, field) in enumerate(cols):
                    dve.wait_ge(s_tr, k + 1)
                    to = hi[:, :] if field is None else rec_in[:, :, field]
                    dve.tensor_copy(to, ps[k][:, 0:NB * Q]).then_inc(s_rec, 1)
                dve.wait_ge(s_rec, 9)
                dve.tensor_copy(lo[:, :], rec_in[:, :, R_LO]).then_inc(s_hot, 1)
                dve.tensor_tensor(hi_hot[:, :, :], m.iota[0:P, None, 0:NT].to_broadcast([P, SORT_STEPS * U, NT]),
                                  hi[:, :, None].to_broadcast([P, SORT_STEPS * U, NT]), ALU.is_equal
                                  ).then_inc(s_hot, 1)

            @block.tensor
            def _(pe):
                pe.wait_ge(s_lo, 26)
                pe.wait_ge(s_in[3], 16)
                for k, (tile, comp, _) in enumerate(cols):
                    for b in range(NB):
                        src = tile[:, b, :] if comp is None else tile[:, b, comp::3]
                        last = pe.transpose(ps[k][:, b * Q:(b + 1) * Q], src, m.ident[0:Q, 0:Q])
                    last.then_inc(s_tr, 1)

        with ExitStack() as c1:
            sem1 = Sems(nc, c1)
            ps_hist = c1.enter_context(nc.psum_tensor("ps_hist", [P, 512], F32))
            ps_sum = c1.enter_context(nc.psum_tensor("ps_sum", [P, 512], F32))
            ps_pre = c1.enter_context(nc.psum_tensor("ps_pre", [P, 512], F32))
            hist = c1.enter_context(nc.sbuf_tensor("hist", [P, NT], F32))
            tiles_f = c1.enter_context(nc.sbuf_tensor("tiles_f", [P, NT], F32))
            tiles_i = c1.enter_context(nc.sbuf_tensor("tiles_i", [P, 2, NT], I32))
            tile_end = c1.enter_context(nc.sbuf_tensor("tile_end", [P, NT], F32))
            passed = c1.enter_context(nc.sbuf_tensor("passed", [1, T, NT], F32))
            of_tile = c1.enter_context(nc.sbuf_tensor("of_tile", [1, T], F32))
            s_made = sem1("s_lo_made")
            s_used = sem1("s_lo_used")
            s_hist = sem1("s_hist")
            s_ch = sem1("s_pre_ch")
            s_sum = sem1("s_sum")
            block = c1.enter_context(nc.Block())

            @block.vector
            def _(dve):
                def hot(step, b):
                    dve.tensor_tensor(lo_hot[b][:, :, :], m.iota[0:P, None, 0:P].to_broadcast([P, U, P]),
                                      lo[:, ds(step * U, U), None].to_broadcast([P, U, P]), ALU.is_equal
                                      ).then_inc(s_made, 1)

                hot(0, 0)
                hot(1, 1)
                with dve.Fori(1, SORT_STEPS // 2) as it:
                    for b in range(2):
                        dve.wait_ge(s_used, 2 * it + b - 1)
                        hot(2 * it + b, b)
                ch = Chain(dve, s_ch)
                dve.wait_ge(s_hist, 1)
                ch(dve.tensor_copy(hist[:, :], ps_hist[:, 0:NT]))
                dve.wait_ge(s_sum, 1)
                ch(dve.tensor_scalar(tiles_f[:, :], ps_sum[:, 0:NT], float(EP - 1), None, ALU.add))
                ch(dve.tensor_copy(tiles_i[:, 0, :], tiles_f[:, :]))
                ch(dve.tensor_scalar(tiles_i[:, 1, :], tiles_i[:, 0, :], EP.bit_length() - 1, None,
                                     ALU.arith_shift_right))
                ch(dve.tensor_copy(tiles_f[:, :], tiles_i[:, 1, :]))
                ch(dve.tensor_tensor_scan(tile_end[:, :], m.ones[0:P, 0:NT], tiles_f[:, :], 0.0, ALU.mult, ALU.add))
                ch(dve.tensor_tensor(tiles_f[:, :], tile_end[:, :], tiles_f[:, :], ALU.subtract))
                ch(dve.scalar_tensor_tensor(start[:, :], tiles_f[:, :], float(EP), ps_pre[:, 0:NT],
                                            ALU.mult, ALU.add))
                ch(dve.tensor_tensor(passed[:, :, :], m.iota[0:1, 0:T, None].to_broadcast([1, T, NT]),
                                     tile_end[0:1, None, :].to_broadcast([1, T, NT]), ALU.is_ge))
                ch(dve.tensor_reduce(of_tile[:, :], passed[:, :, :], AX.X, ALU.add))
                ch(dve.tensor_scalar(of_tile[:, :], of_tile[:, :], float(NT - 1), None, ALU.min))
                ch(dve.tensor_copy(m.node_tile[0:1, 0:T], of_tile[:, :]))

            @block.tensor
            def _(pe):
                def count(step, b, start_, stop_):
                    for u in range(U):
                        last = pe.matmul(ps_hist[:, 0:NT], lo_hot[b][:, u, :], hi_hot[:, step * U + u, :],
                                         start=start_ and u == 0, stop=stop_ and u == U - 1,
                                         skip_group_check=True)
                    last.then_inc(s_used, 1)
                    return last

                pe.wait_ge(s_made, 1)
                count(0, 0, True, False)
                pe.wait_ge(s_made, 2)
                count(1, 1, False, False)
                with pe.Fori(1, SORT_STEPS // 2) as it:
                    for b in range(2):
                        pe.wait_ge(s_made, 2 * it + b + 1)
                        count(2 * it + b, b, False, False)
                pe.wait_ge(s_used, SORT_STEPS)
                pe.sem_inc(s_hist, 1)
                pe.wait_ge(s_ch, 1)
                pe.matmul(ps_sum[:, 0:NT], m.ones[0:P, 0:P], hist[:, :], start=True, stop=True)
                pe.matmul(ps_pre[:, 0:NT], m.after[0:P, 0:P], hist[:, :], start=True, stop=True).then_inc(s_sum, 1)

        with ExitStack() as c1:
            sem1 = Sems(nc, c1)

            def sb1(name, shape, dt=F32):
                return c1.enter_context(nc.sbuf_tensor(name, shape, dt))

            row = [sb1(f"row{b}", [2, CH], BF16) for b in range(2)]
            combine = sb1("combine", [2, 2, P], BF16)
            lo_hot_t = [sb1(f"lo_hot_t{b}", [P, U, P]) for b in range(2)]
            earlier = [sb1(f"earlier{b}", [P, U]) for b in range(2)]
            junk = sb1("junk", [P, U, CH], BF16)
            mask = sb1("mask", [P, U, CH], BF16)
            picked = [sb1(f"picked{b}", [P, U, NT]) for b in range(2)]
            base = [sb1(f"base{b}", [P, U]) for b in range(2)]
            place = [sb1(f"place{b}", [P, U], U32) for b in range(2)]
            rec_s = [sb1(f"rec_s{b}", [P, U, REC]) for b in range(2)]
            ps_dst = [c1.enter_context(nc.psum_tensor(f"ps_dst{b}", [P, 512], F32)) for b in range(2)]
            ps_lo = [c1.enter_context(nc.psum_tensor(f"ps_lo{b}", [P, 512], F32)) for b in range(2)]
            ps_base = [c1.enter_context(nc.psum_tensor(f"ps_base{b}", [P, 512], F32)) for b in range(2)]
            ps_cnt = [c1.enter_context(nc.psum_tensor(f"ps_cnt{b}", [P, 512], F32)) for b in range(2)]
            s_mask = sem1("s_mask")
            s_comb = sem1("s_comb")
            s_rowl = [sem1(f"s_rowl{b}") for b in range(2)]
            s_rows = sem1("s_rows")
            s_hot = sem1("s_hot2")
            s_rank = sem1("s_rank")
            s_look = sem1("s_look")
            s_pick = sem1("s_pick")
            s_base = sem1("s_base")
            s_run = sem1("s_run")
            s_place = sem1("s_place")
            s_recs = sem1("s_recs")
            s_sent = [sem1(f"s_sent{b}") for b in range(2)]
            s_go = sem1("s_go")
            block = c1.enter_context(nc.Block())

            @block.sync
            def _(sp):
                sp.sem_inc(s_rows, 2)
                with sp.Fori(0, SORT_STEPS // 2) as it:
                    for b in range(2):
                        s = 2 * it + b
                        sp.wait_ge(s_rows, s + 1)
                        sp.dma_start(row[b][:, :], row_d[:, ds(s * CH, CH)]).then_inc(s_rowl[b], 16)

            @block.tensor
            def _(pe):
                def spread(s, it, b):
                    pe.wait_ge(s_rowl[b], 16 * it + 16)
                    if not (known(s) and s < 2):
                        pe.wait_ge(s_rank, s - 1)
                    pe.matmul(ps_dst[b][:, 0:CH], combine[:, 0, :], row[b][:, :], start=True, stop=True)
                    pe.matmul(ps_lo[b][:, 0:CH], combine[:, 1, :], row[b][:, :], start=True, stop=True
                              ).then_inc(s_rows, 1)

                def look(s, b):
                    pe.wait_ge(s_hot, s + 1)
                    pe.wait_ge(s_run, s + 1)
                    for u in range(U):
                        pe.matmul(ps_base[b][:, u * NT:(u + 1) * NT], lo_hot_t[b][:, u, :], start[:, :],
                                  start=True, stop=True)
                    for u in range(U):
                        last = pe.matmul(ps_cnt[b][:, 0:NT], lo_hot[b][:, u, :], hi_hot[:, s * U + u, :],
                                         start=u == 0, stop=u == U - 1)
                    last.then_inc(s_look, 1)

                pe.wait_ge(s_comb, 2)
                spread(0, 0, 0)
                spread(1, 0, 1)
                with pe.Fori(0, SORT_STEPS // 2 - 1) as it:
                    for b in range(2):
                        look(2 * it + b, b)
                        spread(2 * it + 2 + b, it + 1, b)
                look(SORT_STEPS - 2, 0)
                look(SORT_STEPS - 1, 1)

            @block.vector
            def _(dve):
                column = m.part[0:2, 0:1].to_broadcast([2, P])
                dve.tensor_scalar(combine[:, 0, :], column, float(P - 1), 1.0, ALU.mult, ALU.add).then_inc(s_comb, 1)
                dve.tensor_scalar(combine[:, 1, :], column, -1.0, 1.0, ALU.mult, ALU.add).then_inc(s_comb, 1)
                dve.memset(mask[:, :, :], 0.0).then_inc(s_mask, 1)
                dve.wait_ge(s_mask, 1)
                for u in range(U):
                    if u:
                        dve.memset(mask[:, u, 0:u * P], 1.0)
                    dve.tensor_copy(mask[:, u, u * P:(u + 1) * P], m.before[0:P, 0:P]).then_inc(s_mask, 1)
                dve.sem_inc(s_run, 1)
                dve.sem_inc(s_place, 1)
                dve.wait_ge(s_mask, 5)

                def prepare(s, b):
                    dve.wait_ge(s_rows, s + 3)
                    if not (known(s) and s < 1):
                        dve.wait_ge(s_rank, s)
                        dve.wait_ge(s_place, s)
                    dve.tensor_scalar(lo_hot_t[b].rearrange("p u q -> p (u q)"), ps_lo[b][:, 0:CH],
                                      m.part[0:P, 0:1], None, ALU.is_equal)
                    dve.tensor_tensor(lo_hot[b][:, :, :], m.iota[0:P, None, 0:P].to_broadcast([P, U, P]),
                                      lo[:, ds(s * U, U), None].to_broadcast([P, U, P]), ALU.is_equal
                                      ).then_inc(s_hot, 1)
                    for u in range(U):
                        n = (u + 1) * P
                        last = dve.scalar_tensor_tensor(junk[:, u, 0:n], ps_dst[b][:, 0:n],
                                                        rec_in[:, s * U + u, R_DST:R_DST + 1], mask[:, u, 0:n],
                                                        ALU.is_equal, ALU.mult, accum_out=earlier[b][:, u:u + 1])
                    last.then_inc(s_rank, 1)

                def settle(s, it, b):
                    dve.wait_ge(s_look, s + 1)
                    dve.tensor_tensor(start[:, :], start[:, :], ps_cnt[b][:, 0:NT], ALU.add)
                    dve.tensor_tensor(picked[b][:, :, :], ps_base[b][:, 0:U * NT].rearrange("p (u n) -> p u n", u=U),
                                      hi_hot[:, ds(s * U, U), :], ALU.mult).then_inc(s_run, 1)
                    dve.wait_ge(s_run, s + 2)
                    dve.tensor_reduce(base[b][:, :], picked[b][:, :, :], AX.X, ALU.add).then_inc(s_base, 1)
                    dve.wait_ge(s_base, s + 1)
                    dve.wait_ge(s_rank, s + 1)
                    if not (known(it) and it < 1):
                        dve.wait_ge(s_sent[b], 16 * U * it)
                    dve.tensor_tensor(place[b][:, :], base[b][:, :], earlier[b][:, :], ALU.add).then_inc(s_place, 1)

                prepare(0, 0)
                for b in range(2):
                    prepare(b + 1, 1 - b)
                    settle(b, 0, b)
                with dve.Fori(1, SORT_STEPS // 2 - 1) as it:
                    for b in range(2):
                        prepare(2 * it + b + 1, 1 - b)
                        settle(2 * it + b, it, b)
                prepare(SORT_STEPS - 1, 1)
                for b in range(2):
                    settle(SORT_STEPS - 2 + b, SORT_STEPS // 2 - 1, b)

            @block.scalar
            def _(act):
                def pack(s, it, b):
                    if not known(it):
                        act.wait_ge(s_sent[b], 16 * U * it)
                    act.activation(rec_s[b][:, :, :], rec_in[:, ds(s * U, U), :], ACT.Copy).then_inc(s_recs, 1)

                pack(0, 0, 0)
                pack(1, 0, 1)
                with act.Fori(1, SORT_STEPS // 2) as it:
                    for b in range(2):
                        pack(2 * it + b, it, b)

            @block.gpsimd
            def _(pool):
                with pool.Fori(0, SORT_STEPS // 2) as it:
                    for b in range(2):
                        s = 2 * it + b
                        pool.wait_ge(s_place, s + 2)
                        pool.sem_inc(s_go, 1)
                        pool.wait_ge(s_recs, s + 1)
                        pool.sem_inc(s_go, 1)
                        for u in range(U):
                            pool.indirect_dma_start(
                                out=m.rec_d[:, :], out_offset=bass.IndirectOffsetOnAxis(ap=place[b][:, u:u + 1], axis=0),
                                in_=rec_s[b][:, u, :], in_offset=None).then_inc(s_sent[b], 16)
                for b in range(2):
                    pool.wait_ge(s_sent[b], 16 * U * SORT_STEPS // 2)


@stage
def build_reload(nc, m):
    with ExitStack() as ctx:
        sem = Sems(nc, ctx)
        s_rec = [sem(f"s_recl{i}") for i in range(4)]
        s_ch = sem("s_vec")
        s_sq = sem("s_sq")
        sq = ctx.enter_context(nc.sbuf_tensor("vsq", [EP, TX, 3], F32))
        n2 = ctx.enter_context(nc.sbuf_tensor("vn2", [EP, TX], F32))
        block = ctx.enter_context(nc.Block())
        cut = [0, TX // 4, TX // 2, 3 * TX // 4, TX]
        view = m.rec_d.rearrange("(t p) c -> p t c", p=EP)

        @block.sync
        def _(sp):
            for i in range(0, 4, 2):
                sp.dma_start(m.rec[:, cut[i]:cut[i + 1], :], view[:, cut[i]:cut[i + 1], :]).then_inc(s_rec[i], 16)

        @block.scalar
        def _(act):
            for i in range(1, 4, 2):
                act.dma_start(m.rec[:, cut[i]:cut[i + 1], :], view[:, cut[i]:cut[i + 1], :]).then_inc(s_rec[i], 16)
            act.wait_ge(s_ch, 3)
            act.activation(n2[:, :], n2[:, :], ACT.Sqrt).then_inc(s_sq, 1)

        @block.vector
        def _(dve):
            for i in range(4):
                dve.wait_ge(s_rec[i], 16)
            ch = Chain(dve, s_ch)
            vec = m.rec[:, :, R_VEC:R_VEC + 3]
            ch(dve.tensor_copy(m.src[:, :], m.rec[:, :, R_SRC]))
            ch(dve.tensor_tensor(sq[:, :, :], vec, vec, ALU.mult))
            ch(dve.tensor_reduce(n2[:, :], sq[:, :, :], AX.X, ALU.add))
            dve.wait_ge(s_sq, 1)
            ch(dve.tensor_scalar(n2[:, :], n2[:, :], 1e-12, None, ALU.add))
            ch(dve.reciprocal(n2[:, :], n2[:, :]))
            ch(dve.tensor_tensor(m.unit[:, :, :], vec, n2[:, :, None].to_broadcast([EP, TX, 3]), ALU.mult))
            ch(dve.tensor_tensor(sq[:, :, :], m.unit[:, :, :], m.unit[:, :, :], ALU.mult))
            ch(dve.tensor_reduce(m.unit2[:, :], sq[:, :, :], AX.X, ALU.add))


@stage
def layer_norm(nc, m, tag, x, y, gamma=None, beta=None):
    with ExitStack() as ctx:
        sem = Sems(nc, ctx)
        st = ctx.enter_context(nc.sbuf_tensor(f"st_{tag}", [P, NT, 6], F32))
        mv = ctx.enter_context(nc.sbuf_tensor(f"mv_{tag}", [P, NT, 2], F32))
        rs = ctx.enter_context(nc.sbuf_tensor(f"rs_{tag}", [P, NT], F32))
        s_st = sem(f"s_st_{tag}")
        s_sq = sem(f"s_sq_{tag}")
        s_ch = sem(f"s_ch_{tag}")
        block = ctx.enter_context(nc.Block())

        @block.vector
        def _(dve):
            with dve.Fori(0, NG) as g:
                for u in range(G):
                    dve.bn_stats(st[:, G * g + u, :], x[:, G * g + u, :]).then_inc(s_st, 1)
            dve.wait_ge(s_st, NT)
            ch = Chain(dve, s_ch)
            ch(dve.tensor_tensor(mv[:, :, 0], st[:, :, 1], st[:, :, 4], ALU.subtract))
            ch(dve.tensor_tensor(mv[:, :, 0], mv[:, :, 0], mv[:, :, 0], ALU.mult))
            ch(dve.tensor_tensor(rs[:, :], st[:, :, 2], st[:, :, 5], ALU.add))
            ch(dve.tensor_scalar(rs[:, :], rs[:, :], 1.0 / D, EPS, ALU.mult, ALU.add))
            ch(dve.scalar_tensor_tensor(rs[:, :], mv[:, :, 0], 0.25, rs[:, :], ALU.mult, ALU.add))
            ch(dve.tensor_tensor(mv[:, :, 0], st[:, :, 1], st[:, :, 4], ALU.add))
            ch(dve.tensor_scalar(mv[:, :, 0], mv[:, :, 0], 0.5, None, ALU.mult))
            dve.wait_ge(s_sq, 1)
            ch(dve.reciprocal(rs[:, :], rs[:, :]))
            for j in range(NT):
                last = dve.tensor_scalar(y[:, j, :], x[:, j, :], mv[:, j, 0:1], rs[:, j:j + 1],
                                         ALU.subtract, ALU.mult)
            ch(last)
            if gamma is not None:
                ch(dve.tensor_tensor(y[:, :, :], y[:, :, :], gamma[:, None, :].to_broadcast([P, NT, D]), ALU.mult))
                ch(dve.tensor_tensor(y[:, :, :], y[:, :, :], beta[:, None, :].to_broadcast([P, NT, D]), ALU.add))

        @block.scalar
        def _(act):
            act.wait_ge(s_ch, 5)
            act.activation(rs[:, :], rs[:, :], ACT.Sqrt).then_inc(s_sq, 1)


@stage
def add_all(nc, tag, pairs):
    with ExitStack() as ctx:
        s_ch = Sems(nc, ctx)(f"s_add_{tag}")
        block = ctx.enter_context(nc.Block())

        @block.vector
        def _(dve):
            ch = Chain(dve, s_ch)
            for out, x, y in pairs:
                ch(dve.tensor_tensor(out, x, y, ALU.add))


@stage
def project(nc, m, tag, prepare, weights, width, finish, keep=None, halves=2, own=0):
    NW = len(weights)
    with ExitStack() as ctx:
        sem = Sems(nc, ctx)
        rows = [ctx.enter_context(nc.sbuf_tensor(f"rows{b}_{tag}", [P, G, 256], F32)) for b in range(2)]
        rows_t = [ctx.enter_context(nc.sbuf_tensor(f"rows_t{b}_{tag}", [128, G, 2, P], F32)) for b in range(2)]
        ps_t = ctx.enter_context(nc.psum_tensor(f"ps_t_{tag}", [128, 6, 256], F32))
        ps_o = ctx.enter_context(nc.psum_tensor(f"ps_o_{tag}", [128, 6, 256], F32))
        s_prep = sem(f"s_prep_{tag}")
        s_tr = sem(f"s_tr_{tag}")
        s_evac = sem(f"s_evac_{tag}")
        s_mm = sem(f"s_mm_{tag}")
        s_fin = sem(f"s_fin_{tag}")
        s_own = sem(f"s_own_{tag}")
        block = ctx.enter_context(nc.Block())

        def groups(eng, body):
            with eng.Fori(0, (NG - 1) // 2) as it:
                for b in range(2):
                    body(2 * it + b, b)

        @block.vector
        def _(dve):
            count = [0]
            base = [0]

            def ch(ins):
                count[0] += 1
                ins.then_inc(s_own, 1)
                dve.wait_ge(s_own, base[0] + count[0])

            def make(g, b):
                dve.wait_ge(s_tr, g + 1)
                prepare(dve, g, rows[b], ch).then_inc(s_prep, 1)

            def finish_all(g):
                for c in range(NW):
                    dve.wait_ge(s_mm, NW * g + c + 1)
                    finish(dve, g, c, ps_o[0:P, 0:G, 0:width], ch).then_inc(s_fin, 1)

            dve.sem_inc(s_tr, 2)
            make(0, 0)
            first = count[0]

            def body(g, b):
                base[0] = g * own + first
                count[0] = 0
                make(g + 1, 1 - b)
                finish_all(g)
                assert count[0] == own

            groups(dve, body)
            base[0] = (NG - 1) * own + first
            count[0] = 0
            finish_all(NG - 1)

        @block.tensor
        def _(pe):
            def transposes(g, b):
                pe.wait_ge(s_prep, g + 1)
                pe.wait_ge(s_evac, g + 1)
                for u in range(G):
                    for k in range(halves):
                        last = pe.transpose(ps_t[:, u, k * 128:k * 128 + P], rows[b][:, u, k * 128:(k + 1) * 128],
                                            m.ident[0:P, 0:P])
                last.then_inc(s_tr, 1)

            def products(g, b):
                pe.wait_ge(s_evac, g + 2)
                for c, w in enumerate(weights):
                    pe.wait_ge(s_fin, NW * g + c + 1 + NW)
                    for u in range(G):
                        for k in range(halves):
                            last = pe.matmul(ps_o[0:P, u, 0:width], rows_t[b][:, u, k, :], w[:, k, :],
                                             start=k == 0, stop=k == halves - 1)
                    last.then_inc(s_mm, 1)

            pe.sem_inc(s_evac, 1)
            pe.sem_inc(s_fin, NW + 1)
            transposes(0, 0)

            def body(g, b):
                transposes(g + 1, 1 - b)
                products(g, b)

            groups(pe, body)
            products(NG - 1, (NG - 1) % 2)

        @block.scalar
        def _(act):
            def body(g, b):
                act.wait_ge(s_tr, g + 3)
                act.wait_ge(s_fin, NW * g + 1)
                view = ps_t[:, 0:G, :].rearrange("p u (k n) -> p u k n", k=2)[:, :, 0:halves, 0:P]
                if keep is not None:
                    for k in range(halves):
                        act.activation(keep(g, k), view[:, :, k, :], ACT.Copy)
                act.activation(rows_t[b][:, :, 0:halves, :], view, ACT.Copy).then_inc(s_evac, 1)

            groups(act, body)
            body(NG - 1, (NG - 1) % 2)


def known(s):
    return isinstance(s, int)


def node_tiles_of(nc, m, s, engine):
    return nc.values_load_multi_w_load_instructions(m.node_tile[0:1, ds(s * U, U)], engines=[engine],
                                                    min_val=0, max_val=NT - 1)[1]


@stage
def build_scores(nc, m):
    with ExitStack() as ctx:
        sem = Sems(nc, ctx)

        def sb(name, shape, dt=F32):
            return ctx.enter_context(nc.sbuf_tensor(name, shape, dt))

        R = 4
        idx = [sb(f"a_idx{r}", [EP, U], U32) for r in range(R)]
        k_rows = [m.spare[:, r * U * D:(r + 1) * U * D].rearrange("p (u d) -> p u d", u=U) for r in range(R)]
        hot = [sb(f"a_hot{b}", [EP, U, P], BF16) for b in range(2)]
        rel_hot = [sb(f"a_rhot{b}", [EP, U, NREL], BF16) for b in range(2)]
        hot_t = [sb(f"a_hott{b}", [P, U, EP]) for b in range(2)]
        rel_t = [sb(f"a_rhott{b}", [NREL, U, EP]) for b in range(2)]
        kmod = [sb("a_kmod", [EP, U, D])] * 2
        prod = kmod
        ps_q = [ctx.enter_context(nc.psum_tensor(f"a_psq{b}", [EP, U, D], F32)) for b in range(2)]
        ps_t = [ctx.enter_context(nc.psum_tensor(f"a_pst{b}", [128, 2, U, EP], BF16)) for b in range(2)]
        ps_r = [ctx.enter_context(nc.psum_tensor(f"a_psr{b}", [EP, 2 * U, HD], F32)) for b in range(2)]
        s_idx = sem("a_idx")
        s_k = [sem(f"a_k_{r}") for r in range(R)]
        s_go = sem("a_go")
        s_hot = sem("a_hot")
        s_tr = sem("a_tr")
        s_ev = sem("a_ev")
        s_exp = sem("a_exp")
        s_kmod = sem("a_kmod")
        s_prod = sem("a_prod")
        s_sum = sem("a_sum")
        block = ctx.enter_context(nc.Block())

        @block.gpsimd
        def _(pool):
            def gather(s, r):
                pool.wait_ge(s_idx, s + 1)
                pool.sem_inc(s_go, 1)
                if not (known(s) and s < R):
                    pool.wait_ge(s_kmod, s - R + 1)
                    pool.sem_inc(s_go, 1)
                for u in range(U):
                    pool.indirect_dma_start(out=k_rows[r][:, u, :], out_offset=None, in_=m.k_d[:, :],
                                            in_offset=bass.IndirectOffsetOnAxis(ap=idx[r][:, u:u + 1], axis=0)
                                            ).then_inc(s_k[r], 16)

            for s in range(R):
                gather(s, s)
            with pool.Fori(1, STEPS // R) as it:
                for r in range(R):
                    gather(R * it + r, r)

        @block.scalar
        def _(act):
            def index(s, r):
                act.activation(idx[r][:, :], m.src[:, ds(s * U, U)], ACT.Copy).then_inc(s_idx, 1)

            def turned(s, b):
                act.wait_ge(s_tr, s + 1)
                if not (known(s) and s < 2):
                    act.wait_ge(s_exp, s - 1)
                act.activation(hot_t[b][:, :, :], ps_t[b][0:P, 0, :, :], ACT.Copy)
                act.activation(rel_t[b][:, :, :], ps_t[b][0:NREL, 1, :, :], ACT.Copy).then_inc(s_ev, 1)

            for s in range(R):
                index(s, s)
            for s in range(R):
                turned(s, s % 2)
            with act.Fori(1, STEPS // R) as it:
                for r in range(R):
                    act.wait_ge(s_kmod, R * it + r - R + 1)
                    index(R * it + r, r)
                    turned(R * it + r, r % 2)

        @block.tensor
        def _(pe):
            def turn(s, b):
                pe.wait_ge(s_hot, s + 1)
                if not (known(s) and s < 2):
                    pe.wait_ge(s_ev, s - 1)
                for u in range(U):
                    pe.transpose(ps_t[b][0:P, 0, u, :], hot[b][:, u, :], m.ident_b[:, :])
                    last = pe.transpose(ps_t[b][0:NREL, 1, u, :], rel_hot[b][:, u, :], m.ident_b[:, :])
                last.then_inc(s_tr, 1)

            def expand(s, b):
                pe.wait_ge(s_ev, s + 1)
                if not (known(s) and s < 2):
                    pe.wait_ge(s_prod, s - 1)
                for u in range(U):
                    j = pe.value_load(m.node_tile[0:1, ds(s * U + u, 1)], min_val=0, max_val=NT - 1)
                    pe.matmul(ps_q[b][:, u, :], hot_t[b][:, u, :], m.q[:, j, :], start=True, stop=True)
                    last = pe.matmul(ps_r[b][:, u, :], rel_t[b][:, u, :], m.rel[:, :], start=True, stop=True)
                last.then_inc(s_exp, 1)

            turn(0, 0)
            turn(1, 1)
            expand(0, 0)
            with pe.Fori(0, (STEPS - 2) // 2) as it:
                for b in range(2):
                    turn(2 * it + 2 + b, b)
                    expand(2 * it + 1 + b, 1 - b)
            expand(STEPS - 1, 1)

        @block.vector
        def _(dve):
            def make(s, b):
                if not (known(s) and s < 2):
                    dve.wait_ge(s_tr, s - 1)
                dve.tensor_tensor(hot[b][:, :, :], m.iota[:, None, 0:P].to_broadcast([EP, U, P]),
                                  m.rec[:, ds(s * U, U), R_LO:R_LO + 1].to_broadcast([EP, U, P]), ALU.is_equal)
                dve.tensor_tensor(rel_hot[b][:, :, :], m.iota[:, None, 0:NREL].to_broadcast([EP, U, NREL]),
                                  m.rec[:, ds(s * U, U), R_TYPE:R_TYPE + 1].to_broadcast([EP, U, NREL]),
                                  ALU.is_equal).then_inc(s_hot, 1)

            def score(s, it, r):
                b = r % 2
                dve.wait_ge(s_k[r], 16 * U * it + 16 * U)
                dve.wait_ge(s_exp, s + 1)
                dve.wait_ge(s_sum, s + 1)
                dve.tensor_tensor(kmod[b].rearrange("p u (h d) -> p u h d", h=H),
                                  k_rows[r].rearrange("p u (h d) -> p u h d", h=H),
                                  ps_r[b][:, 0:U, None, :].to_broadcast([EP, U, H, HD]), ALU.add).then_inc(s_kmod, 1)
                dve.wait_ge(s_kmod, s + 1)
                dve.tensor_tensor(prod[b][:, :, :], kmod[b][:, :, :], ps_q[b][:, :, :], ALU.mult).then_inc(s_prod, 1)
                dve.wait_ge(s_prod, s + 1)
                dve.tensor_reduce(m.s[:, ds(s * U, U), :].rearrange("p u h -> p (u h)"),
                                  prod[b].rearrange("p u (h d) -> p (u h) d", h=H), AX.X, ALU.add).then_inc(s_sum, 1)

            dve.sem_inc(s_sum, 1)
            make(0, 0)
            make(1, 1)
            with dve.Fori(0, STEPS // R - 1) as it:
                for r in range(R):
                    make(R * it + r + 2, r % 2)
                    score(R * it + r, it, r)
            for r in range(R):
                if r < R - 2:
                    make(STEPS - R + r + 2, r % 2)
                score(STEPS - R + r, STEPS // R - 1, r)


@stage
def build_weights(nc, m):
    with ExitStack() as ctx:
        sem = Sems(nc, ctx)

        def sb(name, shape, dt=F32):
            return ctx.enter_context(nc.sbuf_tensor(name, shape, dt))

        W = NBLK * 128
        st = sb("x_st", [128, W])
        dt = sb("x_dt", [128, W])
        cut = sb("x_cut", [128, W + 1])
        dst4 = cut[:, 0:W].rearrange("p (t h) -> p t h", h=H)
        fwd = sb("x_fwd", [128, W])
        bwd = sb("x_bwd", [128, W])
        ends = sb("x_ends", [128, 4, NBLK])
        ends_t = sb("x_ends_t", [4 * NBLK, 128])
        spare = m.agg[0:1, :, :].rearrange("p j c -> p (j c)")
        er = spare[:, 0:4 * W].rearrange("p (c w) -> p c w", c=4)
        link = sb("x_link", [1, W + H])
        both = spare[:, 4 * W:6 * W].rearrange("p (c w) -> p c w", c=2)
        run = sb("x_run", [1, 2, W + 2 * H])
        carry = er[:, 0:2, :]
        carry_t = sb("x_carry_t", [2 * NBLK, 128])
        cc = sb("x_cc", [128, 2, NBLK])
        tmp = bwd[:, :].rearrange("p (b e) -> p b e", e=128)
        NBK = -(-W // 512)
        ps_a = ctx.enter_context(nc.psum_tensor("x_psa", [128, NBK * 512], F32))
        ps_b = ctx.enter_context(nc.psum_tensor("x_psb", [128, NBK * 512], F32))
        s_ch = sem("x_ch")
        s_pe = sem("x_pe")
        s_d = [sem(f"x_d{i}") for i in range(4)]
        s_fin = sem("x_fin")
        block = ctx.enter_context(nc.Block())
        marks = {}

        @block.vector
        def _(dve):
            ch = Chain(dve, s_ch)
            b3 = lambda t: t.rearrange("p (b e) -> p b e", e=128)
            ch(dve.tensor_copy(dst4[:, :, :], m.rec[:, 0:T, R_DST:R_DST + 1].to_broadcast([EP, T, H])))
            marks["dst4"] = ch.n
            dve.wait_ge(s_pe, 1)
            ch(dve.tensor_copy(st[:, :], ps_a[:, 0:W]))
            ch(dve.tensor_copy(dt[:, :], ps_b[:, 0:W]))
            ch(dve.tensor_tensor(cut[:, 1:W], dt[:, 1:W], dt[:, 0:W - 1], ALU.not_equal))
            ch(dve.tensor_scalar(cut[:, 1:W], cut[:, 1:W], -BIG, None, ALU.mult))
            ch(dve.memset(cut[:, 0:W].rearrange("p (b e) -> p b e", e=128)[:, :, 0:1], -BIG))
            ch(dve.memset(cut[:, W:W + 1], -BIG))
            ch(dve.tensor_tensor_scan(fwd[:, :], cut[:, 0:W], st[:, :], -BIG, ALU.add, ALU.max))
            ch(dve.tensor_tensor_scan(bwd[:, ::-1], cut[:, 1:W + 1][:, ::-1], st[:, ::-1], -BIG, ALU.add, ALU.max))
            ch(dve.tensor_tensor(fwd[:, :], fwd[:, :], bwd[:, :], ALU.max))
            ch(dve.tensor_copy(ends[:, 0, :], b3(fwd)[:, :, 0]))
            ch(dve.tensor_copy(ends[:, 1, :], b3(fwd)[:, :, 127]))
            ch(dve.tensor_copy(ends[:, 2, :], b3(dt)[:, :, 0]))
            ch(dve.tensor_copy(ends[:, 3, :], b3(dt)[:, :, 127]))
            marks["ends"] = ch.n
            dve.wait_ge(s_pe, 2)
            ch(dve.tensor_copy(ends_t[:, :], ps_a[0:4 * NBLK, 0:128]))
            marks["ends_t"] = ch.n
            dve.wait_ge(s_d[1], 16)
            ch(dve.memset(link[:, :], -BIG))
            ch(dve.tensor_tensor(link[:, H:W], er[:, 2, H:W], er[:, 3, 0:W - H], ALU.not_equal))
            ch(dve.tensor_scalar(link[:, H:W], link[:, H:W], -BIG, None, ALU.mult))
            ch(dve.tensor_tensor(both[:, 0, :], er[:, 2, :], er[:, 3, :], ALU.not_equal))
            ch(dve.scalar_tensor_tensor(both[:, 1, :], both[:, 0, :], -BIG, link[:, H:W + H], ALU.mult, ALU.add))
            ch(dve.scalar_tensor_tensor(both[:, 0, :], both[:, 0, :], -BIG, link[:, 0:W], ALU.mult, ALU.add))
            ch(dve.memset(run[:, :, :], -BIG))
            for h in range(H):
                ch(dve.tensor_tensor_scan(run[:, 0, H + h:W + H:H], both[:, 0, h::H], er[:, 1, h::H], -BIG,
                                          ALU.add, ALU.max))
                ch(dve.tensor_tensor_scan(run[:, 1, h:W:H][:, ::-1], both[:, 1, h::H][:, ::-1],
                                          er[:, 0, h::H][:, ::-1], -BIG, ALU.add, ALU.max))
            ch(dve.tensor_tensor(carry[:, 0, :], run[:, 0, 0:W], link[:, 0:W], ALU.add))
            ch(dve.tensor_tensor(carry[:, 1, :], run[:, 1, H:W + H], link[:, H:W + H], ALU.add))
            marks["carry"] = ch.n
            dve.wait_ge(s_pe, 3)
            ch(dve.tensor_copy(cc.rearrange("p c b -> p (c b)"), ps_a[:, 0:2 * NBLK]))
            for side, at in ((0, 2), (1, 3)):
                ch(dve.tensor_tensor(tmp[:, :, :], b3(dt), ends[:, at, :, None].to_broadcast([128, NBLK, 128]),
                                     ALU.not_equal))
                ch(dve.scalar_tensor_tensor(tmp[:, :, :], tmp[:, :, :], -BIG,
                                            cc[:, side, :, None].to_broadcast([128, NBLK, 128]), ALU.mult, ALU.add))
                ch(dve.tensor_tensor(b3(fwd), b3(fwd), tmp[:, :, :], ALU.max))
            marks["max"] = ch.n
            dve.wait_ge(s_pe, 4)
            flat = m.s[:, 0:T, :].rearrange("p t h -> p (t h)")
            ch(dve.tensor_tensor(flat, flat, ps_b[:, 0:W], ALU.subtract))
            marks["sub"] = ch.n

        @block.tensor
        def _(pe):
            flat = m.s[:, 0:T, :].rearrange("p t h -> p (t h)")
            dflat = dst4.rearrange("p t h -> p (t h)")
            pe.wait_ge(s_ch, marks["dst4"])
            for b in range(NBLK):
                c = slice(b * 128, (b + 1) * 128)
                pe.transpose(ps_a[:, c], flat[:, c], m.ident[:, :])
                last = pe.transpose(ps_b[:, c], dflat[:, c], m.ident[:, :])
            last.then_inc(s_pe, 1)
            pe.wait_ge(s_ch, marks["ends"])
            pe.transpose(ps_a[0:4 * NBLK, 0:128], ends.rearrange("p c b -> p (c b)"), m.ident[:, :]).then_inc(s_pe, 1)
            pe.wait_ge(s_d[3], 16)
            pe.transpose(ps_a[:, 0:2 * NBLK], carry_t[:, :], m.ident[0:2 * NBLK, 0:2 * NBLK]).then_inc(s_pe, 1)
            pe.wait_ge(s_ch, marks["max"])
            for b in range(NBLK):
                c = slice(b * 128, (b + 1) * 128)
                last = pe.transpose(ps_b[:, c], fwd[:, c], m.ident[:, :])
            last.then_inc(s_pe, 1)

        @block.sync
        def _(sp):
            sp.wait_ge(s_ch, marks["ends_t"])
            sp.dma_start(m.ends_d[:, :], ends_t[:, :]).then_inc(s_d[0], 16)
            sp.wait_ge(s_d[0], 16)
            sp.dma_start(er[:, :, :], m.ends_d.rearrange("(a c b) e -> a c (b e)", a=1, c=4)).then_inc(s_d[1], 16)
            sp.wait_ge(s_ch, marks["carry"])
            sp.dma_start(m.carry_d.rearrange("(a c b) e -> a c (b e)", a=1, c=2), carry).then_inc(s_d[2], 16)
            sp.wait_ge(s_d[2], 16)
            sp.dma_start(carry_t[:, :], m.carry_d[:, :]).then_inc(s_d[3], 16)

        @block.scalar
        def _(act):
            act.wait_ge(s_ch, marks["sub"])
            act.activation(m.s[:, 0:T, :], m.s[:, 0:T, :], ACT.Exp).then_inc(s_fin, 1)


@stage
def build_values(nc, m):
    WD = D + H
    with ExitStack() as ctx:
        sem = Sems(nc, ctx)

        def sb(name, shape, dt=F32):
            return ctx.enter_context(nc.sbuf_tensor(name, shape, dt))

        R = 4
        idx = [sb(f"b_idx{r}", [EP, U], U32) for r in range(R)]
        v_rows = [sb(f"b_v{r}", [EP, U, D]) for r in range(R)]
        hot = [sb(f"b_hot{b}", [EP, U, P]) for b in range(2)]
        msg = [sb(f"b_msg{b}", [EP, U, WD]) for b in range(2)]
        ps = [ctx.enter_context(nc.psum_tensor(f"b_ps{i}", [P, 512], F32)) for i in range(2 * U)]
        s_idx = sem("b_idx")
        s_v = [sem(f"b_v_{r}") for r in range(R)]
        s_go = sem("b_go")
        s_msg = sem("b_msg")
        s_mm = sem("b_mm")
        s_add = sem("b_add")
        s_zero = sem("b_zero")
        block = ctx.enter_context(nc.Block())

        @block.gpsimd
        def _(pool):
            def gather(s, r):
                pool.wait_ge(s_idx, s + 1)
                pool.sem_inc(s_go, 1)
                if not (known(s) and s < R):
                    pool.wait_ge(s_msg, s - R + 1)
                    pool.sem_inc(s_go, 1)
                for u in range(U):
                    pool.indirect_dma_start(out=v_rows[r][:, u, :], out_offset=None, in_=m.v_d[:, :],
                                            in_offset=bass.IndirectOffsetOnAxis(ap=idx[r][:, u:u + 1], axis=0)
                                            ).then_inc(s_v[r], 16)

            for s in range(R):
                gather(s, s)
            with pool.Fori(1, STEPS // R) as it:
                for r in range(R):
                    gather(R * it + r, r)

        @block.scalar
        def _(act):
            def index(s, r):
                act.activation(idx[r][:, :], m.src[:, ds(s * U, U)], ACT.Copy).then_inc(s_idx, 1)

            for s in range(R):
                index(s, s)
            with act.Fori(1, STEPS // R) as it:
                for r in range(R):
                    act.wait_ge(s_msg, R * it + r - R + 1)
                    index(R * it + r, r)

        @block.tensor
        def _(pe):
            def body(s, b):
                pe.wait_ge(s_msg, s + 1)
                if not (known(s) and s < 2):
                    pe.wait_ge(s_add, s - 1)
                for u in range(U):
                    last = pe.matmul(ps[b * U + u][:, 0:WD], hot[b][:, u, :], msg[b][:, u, :], start=True, stop=True)
                last.then_inc(s_mm, 1)

            body(0, 0)
            body(1, 1)
            with pe.Fori(1, STEPS // 2) as it:
                for b in range(2):
                    body(2 * it + b, b)

        @block.vector
        def _(dve):
            def make(s, it, r):
                b = r % 2
                if not (known(s) and s < 2):
                    dve.wait_ge(s_mm, s - 1)
                dve.tensor_tensor(hot[b][:, :, :], m.iota[:, None, 0:P].to_broadcast([EP, U, P]),
                                  m.rec[:, ds(s * U, U), R_LO:R_LO + 1].to_broadcast([EP, U, P]), ALU.is_equal)
                dve.tensor_copy(msg[b][:, :, D:WD], m.s[:, ds(s * U, U), :])
                dve.wait_ge(s_v[r], 16 * U * it + 16 * U)
                dve.tensor_tensor(msg[b][:, :, 0:D].rearrange("p u (h d) -> p u h d", h=H),
                                  v_rows[r].rearrange("p u (h d) -> p u h d", h=H),
                                  m.s[:, ds(s * U, U), :, None].to_broadcast([EP, U, H, HD]), ALU.mult
                                  ).then_inc(s_msg, 1)

            def add(s, b):
                node_tiles = node_tiles_of(nc, m, s, ENGINE.DVE)
                dve.wait_ge(s_mm, s + 1)
                for u, j in enumerate(node_tiles):
                    if not (known(s) and s == 0 and u == 0):
                        dve.wait_ge(s_zero, s * U + u + 1)
                    last = dve.tensor_tensor(m.agg[:, j, 0:WD], m.agg[:, j, 0:WD], ps[b * U + u][:, 0:WD], ALU.add)
                    last.then_inc(s_zero, 1)
                dve.wait_ge(s_zero, s * U + U + 1)
                dve.sem_inc(s_add, 1)

            dve.memset(m.agg[:, :, :], 0.0).then_inc(s_zero, 1)
            make(0, 0, 0)
            dve.wait_ge(s_zero, 1)
            for r in range(1, R):
                make(r, 0, r)
                add(r - 1, (r - 1) % 2)
            with dve.Fori(1, STEPS // R) as it:
                for r in range(R):
                    make(R * it + r, it, r)
                    add(R * it + r - 1, (r - 1) % 2)
            add(STEPS - 1, 1)


@stage
def build_geometric(nc, m):
    MW = 64 + 192 + 192
    OWN = 5
    R = 8
    with ExitStack() as ctx:
        sem = Sems(nc, ctx)

        def sb(name, shape, dt=F32):
            return ctx.enter_context(nc.sbuf_tensor(name, shape, dt))

        idx = [sb(f"g_idx{r}", [EP, U], U32) for r in range(R)]
        rows = [sb(f"g_rows{r}", [EP, U, 64 + D]) for r in range(R)]
        xr = [sb(f"g_xr{b}", [EP, U, 64, 3]) for b in range(2)]
        ut = [sb(f"g_ut{b}", [128, U, EP]) for b in range(2)]
        lk = [sb(f"g_lk{b}", [64, U, EP]) for b in range(2)]
        mx = sb("g_mx", [EP, U])
        nm = sb("g_nm", [EP, U])
        ex = sb("g_ex", [EP, U, 64])
        z = sb("g_z", [EP, U])
        en = sb("g_en", [EP, U])
        rz = sb("g_rz", [EP, U])
        al = sb("g_al", [EP, U])
        ar = sb("g_ar", [EP, U, 3])
        t1 = sb("g_t1", [EP, U, 64])
        o = [sb(f"g_o{b}", [EP, U, 192]) for b in range(2)]
        hot = [sb(f"g_hot{b}", [EP, U, P]) for b in range(2)]
        msg = [sb(f"g_msg{b}", [EP, U, MW]) for b in range(2)]
        ps_t = ctx.enter_context(nc.psum_tensor("g_pst", [128, U, EP], F32))
        ps_h = ctx.enter_context(nc.psum_tensor("g_psh", [64, U, EP], F32))
        ps_o = ctx.enter_context(nc.psum_tensor("g_pso", [EP, U, 256], F32))
        ps_a = [ctx.enter_context(nc.psum_tensor(f"g_psa{u}", [P, 512], F32)) for u in range(U)]
        s_idx = sem("g_idx")
        s_x = [sem(f"g_x_{r}") for r in range(R)]
        s_go = sem("g_go")
        s_xr = sem("g_xr")
        s_y = sem("g_y")
        s_tr = sem("g_tr")
        s_ut = sem("g_ut")
        s_h = sem("g_h")
        s_lk = sem("g_lk")
        s_out = sem("g_out")
        s_o = sem("g_o")
        s_nm = sem("g_nm")
        s_ex = sem("g_ex")
        s_al = sem("g_al")
        s_xm = sem("g_xm")
        s_hot = sem("g_hot")
        s_msg = sem("g_msg")
        s_prod = sem("g_prod")
        s_sum = sem("g_sum")
        s_ch = sem("g_ch")
        block = ctx.enter_context(nc.Block())

        @block.gpsimd
        def _(pool):
            def gather(s, r):
                pool.wait_ge(s_idx, s + 1)
                pool.sem_inc(s_go, 1)
                if not (known(s) and s < R):
                    pool.wait_ge(s_xm, s - R + 1)
                    pool.sem_inc(s_go, 1)
                for u in range(U):
                    pool.indirect_dma_start(out=rows[r][:, u, 64:64 + D], out_offset=None, in_=m.h_d[:, :],
                                            in_offset=bass.IndirectOffsetOnAxis(ap=idx[r][:, u:u + 1], axis=0)
                                            ).then_inc(s_x[r], 16)

            def lead(s, it, r, b):
                pool.wait_ge(s_x[r], 16 * U * it + 16 * U)
                pool.wait_ge(s_y, s + 1)
                pool.tensor_tensor(xr[b][:, :, :, :], rows[r][:, :, 128:320].rearrange("p u (c k) -> p u c k", k=3),
                                   m.unit[:, ds(s * U, U), None, :].to_broadcast([EP, U, 64, 3]), ALU.mult
                                   ).then_inc(s_xr, 1)
                pool.wait_ge(s_xr, 2 * s + 1)
                pool.tensor_tensor(rows[r][:, :, 0:64], xr[b][:, :, :, 0], xr[b][:, :, :, 1], ALU.add
                                   ).then_inc(s_xr, 1)

            for s in range(R):
                gather(s, s)
            pool.sem_inc(s_y, 2)
            for s in range(4):
                lead(s, 0, s, s % 2)
            with pool.Fori(0, STEPS // R) as it:
                for r in range(R):
                    s, b = R * it + r, r % 2
                    lead(s + 4, it if r < R - 4 else it + 1, (r + 4) % R, b)
                    gather(s + R, r)
            for r in range(R):
                pool.wait_ge(s_x[r], 16 * U * (STEPS // R + 1))

        @block.scalar
        def _(act):
            def index(s, r):
                act.activation(idx[r][:, :], m.src[:, ds(s * U, U)], ACT.Copy).then_inc(s_idx, 1)

            def turned(s, b):
                act.wait_ge(s_tr, s + 1)
                act.activation(ut[b][:, :, :], ps_t[:, :, :], ACT.Copy).then_inc(s_ut, 1)

            def relu(s, b):
                act.wait_ge(s_h, s + 1)
                act.activation(lk[b][:, :, :], ps_h[:, :, :], ACT.Relu).then_inc(s_lk, 1)

            def take(s, b):
                act.wait_ge(s_out, s + 1)
                act.activation(o[b][:, :, :], ps_o[:, :, 0:192], ACT.Copy).then_inc(s_o, 1)

            def exps(s, b):
                act.wait_ge(s_nm, s + 1)
                act.activation(en[:, :], nm[:, :], ACT.Exp)
                for u in range(U):
                    last = act.activation(ex[:, u, :], ps_o[:, u, 192:256], ACT.Exp, bias=nm[:, u:u + 1],
                                          accum_out=z[:, u:u + 1])
                last.then_inc(s_ex, 1)

            for s in range(R):
                index(s, s)
            turned(0, 0)
            relu(0, 0)
            take(0, 0)
            turned(1, 1)
            relu(1, 1)
            exps(0, 0)
            with act.Fori(0, STEPS // R) as it:
                for r in range(R):
                    s, b = R * it + r, r % 2
                    act.wait_ge(s_al, s + 1)
                    act.wait_ge(s_prod, s * U + U)
                    for u in range(U):
                        last = act.activation(msg[b][:, u, 64:256], rows[r][:, u, 128:320], ACT.Copy,
                                              scale=al[:, u:u + 1])
                    last.then_inc(s_xm, 1)
                    take(s + 1, 1 - b)
                    turned(s + 2, b)
                    exps(s + 1, 1 - b)
                    relu(s + 2, b)
                    act.wait_ge(s_x[r], 16 * U * it + 16 * U)
                    index(s + R, r)

        @block.tensor
        def _(pe):
            def turn(s, r):
                pe.wait_ge(s_y, s + 3)
                for u in range(U):
                    last = pe.transpose(ps_t[:, u, :], rows[r][:, u, 0:128], m.ident[:, :])
                last.then_inc(s_tr, 1)

            def hidden(s, b):
                pe.wait_ge(s_ut, s + 1)
                pe.matmul(ps_h.rearrange("p u e -> p (u e)"), m.w_h[:, :],
                          ut[b].rearrange("p u e -> p (u e)"), start=True, stop=True).then_inc(s_h, 1)

            def out(s, b):
                if not known(s):
                    pe.wait_ge(s_ex, s)
                for u in range(U):
                    pe.matmul(ps_o[:, u, 0:192], ut[b][:, u, :], m.w_o[:, :], start=True, stop=True)
                pe.wait_ge(s_lk, s + 1)
                for u in range(U):
                    pe.matmul(ps_o[:, u, 192:256], ut[b][:, u, :], m.w_l[:, :], start=True, stop=False)
                    last = pe.matmul(ps_o[:, u, 192:256], lk[b][:, u, :], m.w_s[:, :], start=False, stop=True)
                last.then_inc(s_out, 1)

            pe.sem_inc(s_prod, 2 * U)
            turn(0, 0)
            hidden(0, 0)
            out(0, 0)
            turn(1, 1)
            hidden(1, 1)
            with pe.Fori(0, STEPS // R) as it:
                for r in range(R):
                    s, b = R * it + r, r % 2
                    out(s + 1, 1 - b)
                    turn(s + 2, (r + 2) % R)
                    pe.wait_ge(s_hot, s + 1)
                    pe.wait_ge(s_xm, s + 1)
                    pe.wait_ge(s_msg, s + 1)
                    for u in range(U):
                        pe.wait_ge(s_sum, s * U + u + 1)
                        pe.matmul(ps_a[u][:, 0:MW], hot[b][:, u, :], msg[b][:, u, :], start=True, stop=True
                                  ).then_inc(s_prod, 1)
                    hidden(s + 2, b)

        @block.vector
        def _(dve):
            def lead(s, r):
                dve.wait_ge(s_xr, 2 * s + 2)
                y = rows[r][:, :, 0:64]
                dve.tensor_tensor(y, y, xr[r % 2][:, :, :, 2], ALU.add).then_inc(s_y, 1)

            def largest(s):
                dve.wait_ge(s_o, s + 1)
                return dve.tensor_reduce(mx[:, :], ps_o[:, :, 192:256], AX.X, ALU.max)

            def negate():
                dve.tensor_scalar(nm[:, :], mx[:, :], 0.0, -1.0, ALU.max, ALU.mult).then_inc(s_nm, 1)

            def one_hot(s, b):
                dve.wait_ge(s_prod, s * U + U)
                dve.tensor_tensor(hot[b][:, :, :], m.iota[:, None, 0:P].to_broadcast([EP, U, P]),
                                  m.rec[:, ds(s * U, U), R_LO:R_LO + 1].to_broadcast([EP, U, P]), ALU.is_equal
                                  ).then_inc(s_hot, 1)

            def addition(s, u, j):
                dve.wait_ge(s_prod, s * U + u + 1 + 2 * U)
                dve.wait_ge(s_sum, s * U + u + U)
                dve.tensor_tensor(m.agg[:, j, 0:MW], m.agg[:, j, 0:MW], ps_a[u][:, 0:MW], ALU.add
                                  ).then_inc(s_sum, 1)

            dve.memset(m.agg[:, :, :], 0.0).then_inc(s_sum, U)
            for s in range(3):
                lead(s, s)
            first = Chain(dve, s_ch)
            first(largest(0))
            negate()
            one_hot(0, 0)

            def step(s, r):
                b = r % 2

                def done(n):
                    dve.wait_ge(s_ch, s * OWN + n + 1)

                def scalars(us):
                    for u in us:
                        last = dve.scalar_tensor_tensor(t1[:, u, :], o[b][:, u, 128:192], m.unit2[:, ds(s * U + u, 1)],
                                                        o[b][:, u, 0:64], ALU.mult, ALU.add)
                    return last

                dve.wait_ge(s_ex, s + 1)
                dve.scalar_tensor_tensor(rz[:, :], en[:, :], 192.0, z[:, :], ALU.mult, ALU.add).then_inc(s_ch, 1)
                scalars((0, 1))
                done(1)
                dve.reciprocal(rz[:, :], rz[:, :]).then_inc(s_ch, 1)
                scalars((2, 3)).then_inc(s_ch, 1)
                done(3)
                dve.tensor_tensor(al[:, :], en[:, :], rz[:, :], ALU.mult).then_inc(s_al, 1)
                dve.wait_ge(s_prod, s * U + U)
                for u in range(U):
                    dve.scalar_tensor_tensor(msg[b][:, u, 0:64], t1[:, u, :], rz[:, u:u + 1], ex[:, u, :],
                                             ALU.mult, ALU.mult)
                dve.wait_ge(s_al, s + 1)
                dve.tensor_tensor(ar[:, :, :], m.unit[:, ds(s * U, U), :],
                                  al[:, :, None].to_broadcast([EP, U, 3]), ALU.mult).then_inc(s_ch, 1)
                done(4)
                for u in range(U):
                    last = dve.tensor_tensor(msg[b][:, u, 256:448].rearrange("p (k c) -> p k c", k=3),
                                             o[b][:, u, None, 64:128].to_broadcast([EP, 3, 64]),
                                             ar[:, u, :, None].to_broadcast([EP, 3, 64]), ALU.mult)
                last.then_inc(s_msg, 1)
                if known(s) and s == 0:
                    largest(1).then_inc(s_ch, 1)
                    done(5)
                    negate()
                else:
                    j = node_tiles_of(nc, m, s - 1, ENGINE.DVE)
                    addition(s - 1, 0, j[0])
                    addition(s - 1, 1, j[1])
                    largest(s + 1).then_inc(s_ch, 1)
                    addition(s - 1, 2, j[2])
                    done(5)
                    negate()
                    addition(s - 1, 3, j[3])
                one_hot(s + 1, 1 - b)
                lead(s + 3, (r + 3) % R)
                dve.wait_ge(s_msg, s + 1)

            for r in range(R):
                step(r, r)
            with dve.Fori(1, STEPS // R) as it:
                for r in range(R):
                    step(R * it + r, r)
            for u, j in enumerate(node_tiles_of(nc, m, STEPS - 1, ENGINE.DVE)):
                addition(STEPS - 1, u, j)


@stage
def build_geometric_weights(nc, m, a):
    c8 = 1.0 / 8.0
    ctp = float(1.0 / np.sqrt(128.0))
    kap = c8 * ctp * c8
    sq3 = float(np.sqrt(3.0))
    names = ["lin_src_w0", "lin_src_w1", "tp1_w00", "tp1_w11", "tp1_w01", "tp1_w10", "tp2_w00", "tp2_w11",
             "tp2_w01", "tp2_w10", "lin_hidden_w0", "lin_hidden_w1"]
    with ExitStack() as ctx:
        sem = Sems(nc, ctx)
        w = ctx.enter_context(nc.sbuf_tensor("gw_w", [64, 12, 64], F32))
        wt = ctx.enter_context(nc.sbuf_tensor("gw_wt", [64, 6, 64], F32))
        pr = ctx.enter_context(nc.sbuf_tensor("gw_pr", [64, 4, 64], F32))
        abt = ctx.enter_context(nc.sbuf_tensor("gw_abt", [64, 4, 64], F32))
        ab = ctx.enter_context(nc.sbuf_tensor("gw_ab", [64, 2, 64], F32))
        up = ctx.enter_context(nc.sbuf_tensor("gw_up", [64, 5, 64], F32))
        ps = [ctx.enter_context(nc.psum_tensor(f"gw_ps{i}", [64, 8, 64], F32)) for i in range(3)]
        s_in = sem("gw_in")
        s_tr = sem("gw_tr")
        s_ev = sem("gw_ev")
        s_z = sem("gw_z")
        s_mv = sem("gw_mv")
        block = ctx.enter_context(nc.Block())
        LS0, LS1, T00, T11, T01, T10, U00, U11, U01, U10, LH0, LH1 = range(12)

        @block.sync
        def _(sp):
            for i, n in enumerate(names):
                sp.dma_start(w[:, i, :], a["L1_gnn_" + n]).then_inc(s_in, 16)
            sp.wait_ge(s_ev, 7)
            sp.dma_start(m.w_h[64:128, :], up[:, 0, :]).then_inc(s_mv, 16)
            sp.dma_start(m.w_o[64:128, :], up[:, 1:4, :].rearrange("p c d -> p (c d)")).then_inc(s_mv, 16)
            sp.dma_start(m.w_d[64:128, 0, 64:128], m.w_d[0:64, 0, 0:64]).then_inc(s_mv, 16)
            sp.dma_start(m.w_l[64:128, :], up[:, 4, :]).then_inc(s_mv, 16)
            sp.wait_ge(s_mv, 64)

        @block.tensor
        def _(pe):
            i64 = m.ident[0:64, 0:64]
            pe.wait_ge(s_in, 16 * 12)
            for k, i in enumerate((LS0, LS1, T00, T11, T01, T10)):
                last = pe.transpose(ps[0][:, k, :], w[:, i, :], i64)
            last.then_inc(s_tr, 1)
            pe.wait_ge(s_ev, 1)
            for k, h in enumerate((LH0, LH0, LH1, LH1)):
                last = pe.matmul(ps[1][:, k, :], wt[:, 2 + k, :], w[:, h, :], start=True, stop=True)
            last.then_inc(s_tr, 1)
            pe.wait_ge(s_ev, 2)
            for k, l in enumerate((0, 1, 0, 1)):
                pe.matmul(ps[2][:, k, :], pr[:, k, :], wt[:, l, :], start=True, stop=True)
            for k in range(2):
                last = pe.matmul(ps[2][:, 4 + k, :], wt[:, k, :], pr[:, k, :], start=True, stop=True)
            last.then_inc(s_tr, 1)
            pe.wait_ge(s_ev, 4)
            prods = [(0, [(0, U00)]), (1, [(1, U00), (3, U11)]), (2, [(0, U01), (2, U10)]), (3, [(1, U01)]),
                     (4, [(2, U11)]), (5, [(3, U10)])]
            for slot, terms in prods:
                for n, (k, u) in enumerate(terms):
                    pe.matmul(ps[1][:, slot, :], abt[:, k, :], w[:, u, :], start=n == 0,
                              stop=n == len(terms) - 1)
            for k in range(2):
                last = pe.matmul(ps[1][:, 6 + k, :], abt[:, k, :], m.w_s[:, :], start=True, stop=True)
            last.then_inc(s_tr, 1)

        @block.vector
        def _(dve):
            dve.wait_ge(s_tr, 1)
            dve.tensor_copy(wt[:, :, :], ps[0][:, 0:6, :]).then_inc(s_ev, 1)
            dve.wait_ge(s_tr, 2)
            dve.tensor_copy(pr[:, :, :], ps[1][:, 0:4, :]).then_inc(s_ev, 1)
            dve.wait_ge(s_tr, 3)
            dve.tensor_scalar(abt[:, :, :], ps[2][:, 0:4, :], kap, None, ALU.mult).then_inc(s_ev, 1)
            dve.tensor_scalar(ab[:, :, :], ps[2][:, 4:6, :], kap, None, ALU.mult).then_inc(s_ev, 1)
            dve.memset(m.w_d[:, :, :], 0.0).then_inc(s_z, 1)
            dve.wait_ge(s_tr, 4)
            dve.wait_ge(s_ev, 4)
            dve.wait_ge(s_z, 1)
            dve.tensor_copy(up[:, 0, :], ab[:, 0, :])
            dve.tensor_scalar(up[:, 1, :], ps[1][:, 0, :], ctp, None, ALU.mult)
            dve.tensor_scalar(up[:, 2, :], ps[1][:, 2, :], sq3 * ctp, None, ALU.mult)
            dve.tensor_scalar(up[:, 4, :], ps[1][:, 6, :], 0.01, None, ALU.mult)
            dve.tensor_scalar(m.w_s[:, :], m.w_s[:, :], 0.99, None, ALU.mult)
            dve.tensor_scalar(up[:, 3, :], ps[1][:, 4, :], sq3 * ctp, None, ALU.mult).then_inc(s_ev, 1)
            dve.tensor_copy(m.w_h[0:64, :], ab[:, 1, :])
            dve.tensor_scalar(m.w_o[0:64, 0:64], ps[1][:, 1, :], ctp, None, ALU.mult)
            dve.tensor_scalar(m.w_o[0:64, 64:128], ps[1][:, 3, :], sq3 * ctp, None, ALU.mult)
            dve.memset(m.w_o[0:64, 128:192], 0.0).then_inc(s_ev, 1)
            dve.tensor_scalar(m.w_l[0:64, :], ps[1][:, 7, :], 0.01, None, ALU.mult)
            dve.tensor_scalar(m.w_d[0:64, 0, 0:64], ps[1][:, 5, :], ctp, None, ALU.mult)
            dve.tensor_scalar(m.w_d[0:64, 1, 128:192], ps[1][:, 5, :], ctp, None, ALU.mult).then_inc(s_ev, 1)


@stage
def feed_forward(nc, m, tag, act_func, net, gate=None, later=None, rows=False, room=None):
    with ExitStack() as ctx:
        sem = Sems(nc, ctx)

        def sb(name, shape, dt=F32):
            return ctx.enter_context(nc.sbuf_tensor(f"{name}_{tag}", shape, dt))

        w1 = sb("w1", [128, 2, FF])
        w2 = sb("w2", [128, NF, D])
        b1 = sb("b1", [128, NF])
        b2 = sb("b2", [P, D])
        hs = sb("hs", [128, NF, G * P]) if room is None else room
        t = sb("t", [P, G, D]) if gate is not None else None
        ps_h = [ctx.enter_context(nc.psum_tensor(f"ps_h{b}_{tag}", [128, 1024], F32)) for b in range(2)]
        ps_y = ctx.enter_context(nc.psum_tensor(f"ps_y_{tag}", [128, 6, 256], F32))
        s_w = sem(f"s_w_{tag}")
        s_h = sem(f"s_h_{tag}")
        s_g = sem(f"s_g_{tag}")
        s_y = sem(f"s_y_{tag}")
        s_t = sem(f"s_t_{tag}")
        s_ch = sem(f"s_ch_{tag}")
        s_later = sem(f"s_later_{tag}")
        if rows:
            on_pool, fill, read_back = send_rows(nc, m, ctx, sem)
        block = ctx.enter_context(nc.Block())

        @block.sync
        def _(sp):
            with nc.allow_non_contiguous_dma(reason="biases down the partitions, 4 KB each"):
                sp.dma_start(w1[:, :, :], net[0].rearrange("(k p) f -> p k f", p=128)).then_inc(s_w, 16)
                sp.dma_start(b1[:, :], net[1].rearrange("(c p) -> p c", p=128)).then_inc(s_w, 16)
                sp.dma_start(w2[:, :, :], net[2].rearrange("(c p) d -> p c d", p=128)).then_inc(s_w, 16)
                sp.dma_start(b2[:, :], net[3].rearrange("(o d) -> o d", o=1).to_broadcast([P, D])).then_inc(s_w, 16)
            if rows:
                fill(sp)
            if later is not None:
                count = later(sp, s_later)
                sp.wait_ge(s_later, count)
            if rows:
                read_back(sp)

        if rows:
            @block.gpsimd
            def _(pool):
                on_pool(pool)

        @block.tensor
        def _(pe):
            pe.sem_inc(s_g, 2)
            pe.wait_ge(s_w, 64)
            with pe.Fori(0, NG) as n:
                for c in range(NF):
                    pe.wait_ge(s_g, n * NF + c + 1)
                    for i in range(2):
                        for k in range(2):
                            last = pe.matmul(ps_h[c % 2][:, 512 * i:512 * i + SPLIT[i + 1] - SPLIT[i]],
                                             w1[:, k, c * 128:(c + 1) * 128],
                                             m.h_t[:, k, ds(n * G * P + SPLIT[i], SPLIT[i + 1] - SPLIT[i])],
                                             start=k == 0, stop=k == 1)
                    last.then_inc(s_h, 1)
                pe.wait_ge(s_t, n + 1)
                pe.wait_ge(s_g, n * NF + NF + 2)
                for u in range(G):
                    for c in range(NF):
                        last = pe.matmul(ps_y[0:P, u, :], hs[:, c, u * P:(u + 1) * P], w2[:, c, :],
                                         start=c == 0, stop=c == NF - 1)
                last.then_inc(s_y, 1)

        @block.scalar
        def _(act):
            act.sem_inc(s_y, 1)
            act.wait_ge(s_w, 64)
            with act.Fori(0, NG) as n:
                act.wait_ge(s_y, n + 1)
                for c in range(NF):
                    act.wait_ge(s_h, n * NF + c + 1)
                    for i in range(2):
                        last = act.activation(hs[:, c, SPLIT[i]:SPLIT[i + 1]],
                                              ps_h[c % 2][:, 512 * i:512 * i + SPLIT[i + 1] - SPLIT[i]],
                                              act_func, bias=b1[:, c:c + 1])
                    last.then_inc(s_g, 1)

        @block.vector
        def _(dve):
            dve.sem_inc(s_t, 1)
            dve.wait_ge(s_w, 64)
            with dve.Fori(0, NG) as n:
                x = m.x[:, ds(n * G, G), :]
                bias = b2[:, None, :].to_broadcast([P, G, D])
                if gate is None:
                    dve.tensor_tensor(x, x, bias, ALU.add).then_inc(s_ch, 1)
                    dve.wait_ge(s_ch, 2 * n + 1)
                    dve.wait_ge(s_y, n + 2)
                    dve.tensor_tensor(x, x, ps_y[0:P, 0:G, :], ALU.add).then_inc(s_t, 1)
                    dve.wait_ge(s_t, n + 2)
                    dve.sem_inc(s_ch, 1)
                else:
                    dve.wait_ge(s_y, n + 2)
                    dve.tensor_tensor(t[:, :, :], ps_y[0:P, 0:G, :], bias, ALU.add).then_inc(s_t, 1)
                    dve.wait_ge(s_t, n + 2)
                    dve.tensor_tensor(t[:, :, :], t[:, :, :], gate(n).to_broadcast([P, G, D]), ALU.mult
                                      ).then_inc(s_ch, 1)
                    dve.wait_ge(s_ch, 2 * n + 1)
                    dve.tensor_tensor(x, x, t[:, :, :], ALU.add).then_inc(s_ch, 1)
                    dve.wait_ge(s_ch, 2 * n + 2)


@stage
def build_top(nc, m):
    with ExitStack() as ctx:
        sem = Sems(nc, ctx)
        ps = ctx.enter_context(nc.psum_tensor("t_ps", [NT, 512], F32))
        wt = ctx.enter_context(nc.sbuf_tensor("t_wt", [NT, P], F32))
        row = ctx.enter_context(nc.sbuf_tensor("t_row", [P, N], F32))
        junk = ctx.enter_context(nc.sbuf_tensor("t_junk", [P, 4, N], BF16))
        part = ctx.enter_context(nc.sbuf_tensor("t_part", [P, NT, 4], F32))
        rank = ctx.enter_context(nc.sbuf_tensor("t_rank", [P, NT], F32))
        s_pe = sem("t_pe")
        s_wt = sem("t_wt")
        s_d = sem("t_d")
        s_r = sem("t_r")
        s_part = sem("t_part")
        s_ch = sem("t_ch")
        block = ctx.enter_context(nc.Block())

        @block.tensor
        def _(pe):
            pe.transpose(ps[:, 0:P], m.w[:, :], m.ident[0:P, 0:P]).then_inc(s_pe, 1)

        @block.sync
        def _(sp):
            sp.wait_ge(s_wt, 1)
            sp.dma_start(m.wrow_d.rearrange("(j p) -> j p", p=P), wt[:, :]).then_inc(s_d, 16)
            sp.wait_ge(s_d, 16)
            sp.dma_start(row[:, :], m.wrow_d.rearrange("(o n) -> o n", o=1).to_broadcast([P, N])).then_inc(s_r, 16)

        @block.vector
        def _(dve):
            dve.wait_ge(s_pe, 1)
            dve.tensor_copy(wt[:, :], ps[:, 0:P]).then_inc(s_wt, 1)
            dve.memset(part[:, :, :], 0.0).then_inc(s_part, 1)
            dve.wait_ge(s_part, 1)
            dve.wait_ge(s_r, 16)
            for j in range(NT):
                a, b = j * P, (j + 1) * P
                mine = m.w[:, j:j + 1]
                dve.wait_ge(s_part, j + 1)
                if j:
                    dve.tensor_scalar(junk[:, 0, 0:a], row[:, 0:a], mine, None, ALU.is_ge, ALU.add,
                                      accum_out=part[:, j, 0:1])
                if j < NT - 1:
                    dve.tensor_scalar(junk[:, 1, b:N], row[:, b:N], mine, None, ALU.is_gt, ALU.add,
                                      accum_out=part[:, j, 1:2])
                dve.tensor_scalar(junk[:, 2, a:b], row[:, a:b], mine, None, ALU.is_gt, ALU.add,
                                  accum_out=part[:, j, 2:3])
                dve.scalar_tensor_tensor(junk[:, 3, 0:P], row[:, a:b], mine,
                                         m.before[0:P, 0:P], ALU.is_equal, ALU.mult, accum_out=part[:, j, 3:4]
                                         ).then_inc(s_part, 1)
            dve.wait_ge(s_part, NT + 1)
            ch = Chain(dve, s_ch)
            ch(dve.tensor_reduce(rank[:, :], part[:, :, :], AX.X, ALU.add))
            ch(dve.tensor_scalar(rank[:, :], rank[:, :], float(KEPT), None, ALU.is_lt))
            ch(dve.tensor_tensor(m.w[:, :], m.w[:, :], rank[:, :], ALU.mult))


@stage
def build_router(nc, m):
    with ExitStack() as ctx:
        sem = Sems(nc, ctx)

        def sb(name, shape, dt=F32):
            return ctx.enter_context(nc.sbuf_tensor(f"r_{name}", shape, dt))

        mx = sb("mx", [P, NT])
        p = sb("p", [P, NT, NE])
        sm = sb("sm", [P, NT])
        cmp_ = sb("cmp", [P, NT, NE])
        rank = sb("rank", [P, NT, NE])
        sel = sb("sel", [P, NT, NE])
        tot = sb("tot", [P, NT, NE])
        upto = sb("upto", [P, NT, NE])
        cnt = sb("cnt", [P, NE])
        cnt_i = sb("cnt_i", [P, 2, NE], I32)
        end = sb("end", [P, NE])
        place = sb("place", [P, NT, NE])
        passed = sb("passed", [1, ETX, NE])
        of_tile = sb("of_tile", [1, ETX])
        ps = ctx.enter_context(nc.psum_tensor("r_ps", [P, 2, 512], F32))
        s_ch = sem("r_ch")
        s_ex = sem("r_ex")
        s_pe = sem("r_pe")
        block = ctx.enter_context(nc.Block())
        shape = [P, NT, NE]
        marks = {}

        @block.scalar
        def _(act):
            act.wait_ge(s_ch, 2)
            act.activation(p[:, :, :], m.mask[:, :, :], ACT.Exp).then_inc(s_ex, 1)

        @block.vector
        def _(dve):
            ch = Chain(dve, s_ch)
            ch(dve.tensor_reduce(mx[:, :], m.mask[:, :, :], AX.X, ALU.max))
            ch(dve.tensor_tensor(m.mask[:, :, :], m.mask[:, :, :], mx[:, :, None].to_broadcast(shape), ALU.subtract))
            dve.wait_ge(s_ex, 1)
            ch(dve.tensor_reduce(sm[:, :], p[:, :, :], AX.X, ALU.add))
            ch(dve.reciprocal(sm[:, :], sm[:, :]))
            ch(dve.tensor_tensor(p[:, :, :], p[:, :, :], sm[:, :, None].to_broadcast(shape), ALU.mult))
            for e in range(NE):
                if e:
                    ch(dve.tensor_tensor(cmp_[:, :, 0:e], p[:, :, 0:e], p[:, :, e:e + 1].to_broadcast([P, NT, e]),
                                         ALU.is_ge))
                ch(dve.tensor_tensor(cmp_[:, :, e:NE], p[:, :, e:NE], p[:, :, e:e + 1].to_broadcast([P, NT, NE - e]),
                                     ALU.is_gt))
                ch(dve.tensor_reduce(rank[:, :, e], cmp_[:, :, :], AX.X, ALU.add))
            ch(dve.tensor_scalar(sel[:, :, :], rank[:, :, :], float(TOP), None, ALU.is_lt))
            marks["sel"] = ch.n
            ch(dve.tensor_tensor(p[:, :, :], p[:, :, :], sel[:, :, :], ALU.mult))
            ch(dve.tensor_reduce(sm[:, :], p[:, :, :], AX.X, ALU.add))
            ch(dve.reciprocal(sm[:, :], sm[:, :]))
            ch(dve.tensor_tensor(p[:, :, :], p[:, :, :], sm[:, :, None].to_broadcast(shape), ALU.mult))
            dve.wait_ge(s_pe, 1)
            ch(dve.tensor_copy(tot.rearrange("p j e -> p (j e)"), ps[:, 0, 0:NT * NE]))
            for e in range(NE):
                dve.tensor_tensor_scan(upto[:, :, e], m.ones[0:P, 0:NT], tot[:, :, e], 0.0, ALU.mult, ALU.add
                                       ).then_inc(s_ch, 1)
                ch.n += 1
            dve.wait_ge(s_ch, ch.n)
            ch(dve.tensor_scalar(cnt[:, :], upto[:, NT - 1, :], float(EP - 1), None, ALU.add))
            ch(dve.tensor_copy(cnt_i[:, 0, :], cnt[:, :]))
            ch(dve.tensor_scalar(cnt_i[:, 1, :], cnt_i[:, 0, :], EP.bit_length() - 1, None, ALU.arith_shift_right))
            ch(dve.tensor_copy(cnt[:, :], cnt_i[:, 1, :]))
            ch(dve.tensor_tensor_scan(end[:, :], m.ones[0:P, 0:NE], cnt[:, :], 0.0, ALU.mult, ALU.add))
            ch(dve.tensor_tensor(cnt[:, :], end[:, :], cnt[:, :], ALU.subtract))
            ch(dve.tensor_tensor(place[:, :, :], upto[:, :, :], tot[:, :, :], ALU.subtract))
            ch(dve.tensor_tensor(place[:, :, :], place[:, :, :],
                                 ps[:, 1, 0:NT * NE].rearrange("p (j e) -> p j e", e=NE), ALU.add))
            ch(dve.scalar_tensor_tensor(place[:, :, :], cnt[:, None, :].to_broadcast(shape), float(EP),
                                        place[:, :, :], ALU.mult, ALU.add))
            for k in range(TOP):
                ch(dve.tensor_scalar(sel[:, :, :], rank[:, :, :], float(k), None, ALU.is_equal))
                ch(dve.tensor_tensor(cmp_[:, :, :], sel[:, :, :], p[:, :, :], ALU.mult))
                ch(dve.tensor_reduce(m.gate[:, :, k], cmp_[:, :, :], AX.X, ALU.add))
                ch(dve.tensor_tensor(cmp_[:, :, :], sel[:, :, :], place[:, :, :], ALU.mult))
                ch(dve.tensor_reduce(sm[:, :], cmp_[:, :, :], AX.X, ALU.add))
                ch(dve.tensor_copy(m.place[:, :, k], sm[:, :]))
            ch(dve.tensor_tensor(passed[:, :, :], m.iota[0:1, 0:ETX, None].to_broadcast([1, ETX, NE]),
                                 end[0:1, None, :].to_broadcast([1, ETX, NE]), ALU.is_ge))
            ch(dve.tensor_reduce(of_tile[:, :], passed[:, :, :], AX.X, ALU.add))
            ch(dve.tensor_scalar(of_tile[:, :], of_tile[:, :], float(NE - 1), None, ALU.min))
            ch(dve.tensor_copy(m.expert[:, :], of_tile[:, :]))
            ch(dve.tensor_scalar(mx[:, :], m.iota[0:P, 0:NT], float(P), m.part[0:P, 0:1], ALU.mult, ALU.add))
            ch(dve.tensor_copy(m.number[:, :], mx[:, :]))

        @block.tensor
        def _(pe):
            flat = sel.rearrange("p j e -> p (j e)")
            pe.wait_ge(s_ch, marks["sel"])
            pe.matmul(ps[:, 0, 0:NT * NE], m.ones[0:P, 0:P], flat, start=True, stop=True)
            pe.matmul(ps[:, 1, 0:NT * NE], m.after[0:P, 0:P], flat, start=True, stop=True).then_inc(s_pe, 1)


def send_rows(nc, m, ctx, sem):
    none = ctx.enter_context(nc.sbuf_tensor("n_none", [EP, ETX], U32))
    s_zero = sem("n_zero")
    s_fill = sem("n_fill")
    s_sent = sem("n_sent")
    s_back = sem("n_back")

    def on_pool(pool):
        pool.memset(none[:, :], 0).then_inc(s_zero, 1)
        pool.wait_ge(s_fill, 16)
        for j in range(NT):
            for k in range(TOP):
                pool.indirect_dma_start(
                    out=m.list_d[:, :], out_offset=bass.IndirectOffsetOnAxis(ap=m.place[:, j, k:k + 1], axis=0),
                    in_=m.number[:, j:j + 1], in_offset=None).then_inc(s_sent, 16)
        pool.wait_ge(s_sent, 16 * NT * TOP)

    def fill(sp):
        sp.wait_ge(s_zero, 1)
        with nc.allow_non_contiguous_dma(reason="one word a row, once"):
            sp.dma_start(m.list_d.rearrange("(p t) o -> p (t o)", p=EP), none[:, :]).then_inc(s_fill, 16)

    def read_back(sp):
        sp.wait_ge(s_fill, 16)
        sp.wait_ge(s_sent, 16 * NT * TOP)
        with nc.allow_non_contiguous_dma(reason="one word a row, once"):
            sp.dma_start(m.rows_of[:, :], m.list_d.rearrange("(t p) o -> p (t o)", p=EP)).then_inc(s_back, 16)
        sp.wait_ge(s_back, 16)

    return on_pool, fill, read_back


@stage
def build_experts(nc, m, a):
    with ExitStack() as ctx:
        sem = Sems(nc, ctx)

        def sb(name, shape, dt=F32):
            return ctx.enter_context(nc.sbuf_tensor(f"e_{name}", shape, dt))

        w1, w2 = m.w1, m.w2
        b1 = sb("b1", [128, NE, NF])
        b2 = sb("b2", [128, NE, D])
        idx = [sb(f"idx{r}", [EP, 1], U32) for r in range(ER)]
        rows = [sb(f"rows{r}", [EP, D]) for r in range(ER)]
        xt = [sb(f"xt{b}", [128, 2, EP]) for b in range(2)]
        h = sb("h", [EP, FF])
        ht = sb("ht", [128, NF, EP])
        y = [sb(f"y{b}", [EP, D]) for b in range(2)]
        ps_x = ctx.enter_context(nc.psum_tensor("e_psx", [128, 4, EP], F32))
        ps_h = ctx.enter_context(nc.psum_tensor("e_psh", [EP, FF], F32))
        ps_t = ctx.enter_context(nc.psum_tensor("e_pst", [128, NF, EP], F32))
        ps_y = [ctx.enter_context(nc.psum_tensor(f"e_psy{b}", [EP, 512], F32)) for b in range(2)]
        s_w2 = sem("e_w2_in")
        s_b = sem("e_b")
        s_idx = sem("e_idx")
        s_go = sem("e_go")
        s_x = [sem(f"e_x{r}") for r in range(ER)]
        s_tr = sem("e_tr")
        s_xt = sem("e_xt")
        s_h = sem("e_h")
        s_hs = sem("e_hs")
        s_ht = sem("e_ht")
        s_g = sem("e_g")
        s_y = sem("e_y")
        s_ys = sem("e_ys")
        s_out = [sem(f"e_out{b}") for b in range(2)]
        block = ctx.enter_context(nc.Block())

        @block.sync
        def _(sp):
            with nc.allow_non_contiguous_dma(reason="biases down the partitions"):
                sp.dma_start(b1[:, :, :], a["L1_ffn_b1p"].rearrange("e (c p) -> p e c", p=128)).then_inc(s_b, 16)

            for e in range(EARLY, NE):
                sp.dma_start(w2[:, e, :, :], a["L1_ffn_W2p"][e].rearrange("(c p) d -> p c d", p=128)
                             ).then_inc(s_w2, 16)

            def store(t, b):
                sp.wait_ge(s_ys, t + 1)
                sp.dma_start(m.y_d[ds(t * EP, EP), :], y[b][:, :]).then_inc(s_out[b], 16)

            with sp.Fori(0, ET // 2) as it:
                for b in range(2):
                    store(2 * it + b, b)
            for b in range(2):
                sp.wait_ge(s_out[b], 16 * ET // 2)

        @block.gpsimd
        def _(pool):
            def gather(t, r):
                pool.wait_ge(s_idx, t + 1)
                pool.sem_inc(s_go, 1)
                if not (known(t) and t < ER):
                    pool.wait_ge(s_tr, t - ER + 1)
                    pool.sem_inc(s_go, 1)
                pool.indirect_dma_start(out=rows[r][:, :], out_offset=None, in_=m.h_d[:, :],
                                        in_offset=bass.IndirectOffsetOnAxis(ap=idx[r][:, :], axis=0)
                                        ).then_inc(s_x[r], 16)

            for t in range(ER):
                gather(t, t)
            with pool.Fori(1, ET // ER) as it:
                for r in range(ER):
                    gather(ER * it + r, r)
            for r in range(2):
                gather(ET + r, r)
            for r in range(2):
                pool.wait_ge(s_x[r], 16 * (ET // ER + 1))

        @block.tensor
        def _(pe):
            def turn(t, it, r):
                pe.wait_ge(s_x[r], 16 * it + 16)
                if not (known(t) and t < 1):
                    pe.wait_ge(s_xt, t)
                for k in range(2):
                    last = pe.transpose(ps_x[:, k, :], rows[r][:, k * 128:(k + 1) * 128], m.ident[:, :])
                last.then_inc(s_tr, 1)

            def layer1(t, b):
                e = pe.value_load(m.expert[0:1, ds(t, 1)], min_val=0, max_val=NE - 1)
                pe.wait_ge(s_xt, t + 1)
                if not (known(t) and t < 1):
                    pe.wait_ge(s_hs, t)
                for i in range(2):
                    for k in range(2):
                        last = pe.matmul(ps_h[:, i * 512:(i + 1) * 512], xt[b][:, k, :],
                                         w1[:, e, k, i * 512:(i + 1) * 512], start=k == 0, stop=k == 1)
                last.then_inc(s_h, 1)

            def turn_h(t):
                pe.wait_ge(s_hs, t + 1)
                for c in range(NF):
                    last = pe.transpose(ps_t[:, c, :], h[:, c * 128:(c + 1) * 128], m.ident[:, :])
                last.then_inc(s_ht, 1)

            def layer2(t, b):
                e = pe.value_load(m.expert[0:1, ds(t, 1)], min_val=0, max_val=NE - 1)
                pe.wait_ge(s_g, t + 1)
                for c in range(NF):
                    last = pe.matmul(ps_y[b][:, 0:D], ht[:, c, :], w2[:, e, c, :], start=c == 0, stop=c == NF - 1)
                last.then_inc(s_y, 1)

            turn(0, 0, 0)
            turn(1, 0, 1)
            layer1(0, 0)
            turn_h(0)
            pe.wait_ge(s_w2, 16 * (NE - EARLY))
            with pe.Fori(0, ET // ER) as it:
                for r in range(ER):
                    t, b = ER * it + r, r % 2
                    turn(t + 2, it if r < ER - 2 else it + 1, (r + 2) % ER)
                    layer1(t + 1, 1 - b)
                    layer2(t, b)
                    turn_h(t + 1)

        @block.scalar
        def _(act):
            def index(t, r):
                act.activation(idx[r][:, :], m.rows_of[:, ds(t, 1)], ACT.Copy).then_inc(s_idx, 1)

            def turned(t, b):
                act.wait_ge(s_tr, t + 1)
                act.activation(xt[b][:, :, :], ps_x[:, 0:2, :], ACT.Copy).then_inc(s_xt, 1)

            def gelu(t):
                e = act.value_load(m.expert[0:1, ds(t, 1)], min_val=0, max_val=NE - 1)
                act.wait_ge(s_ht, t + 1)
                for c in range(NF):
                    last = act.activation(ht[:, c, :], ps_t[:, c, :], ACT.Gelu, bias=b1[:, e, c:c + 1])
                last.then_inc(s_g, 1)

            for e in range(NE):
                act.dma_start(b2[:, e, :], a["L1_ffn_b2p"][e].rearrange("(o d) -> o d", o=1).to_broadcast([128, D])
                              ).then_inc(s_b, 16)
            for t in range(ER):
                index(t, t)
            turned(0, 0)
            turned(1, 1)
            act.wait_ge(s_b, 16 * NE + 16)
            gelu(0)
            with act.Fori(0, ET // ER) as it:
                for r in range(ER):
                    t, b = ER * it + r, r % 2
                    act.wait_ge(s_h, t + 2)
                    turned(t + 2, b)
                    act.wait_ge(s_x[r], 16 * it + 16)
                    index(t + ER, r)
                    gelu(t + 1)

        @block.vector
        def _(dve):
            def first(t):
                dve.wait_ge(s_h, t + 1)
                if not (known(t) and t < 1):
                    dve.wait_ge(s_ht, t)
                dve.tensor_copy(h[:, :], ps_h[:, :]).then_inc(s_hs, 1)

            dve.wait_ge(s_b, 16 * NE + 16)
            first(0)
            dve.wait_ge(s_ht, 1)

            def second(t, it, b):
                e = dve.value_load(m.expert[0:1, ds(t, 1)], min_val=0, max_val=NE - 1)
                dve.wait_ge(s_y, t + 1)
                if not known(it):
                    dve.wait_ge(s_out[b], 16 * it)
                dve.tensor_tensor(y[b][:, :], ps_y[b][:, 0:D], b2[:, e, :], ALU.add).then_inc(s_ys, 1)

            for t in range(2):
                first(t + 1)
                second(t, 0, t)
            with dve.Fori(1, ET // 2) as it:
                for b in range(2):
                    first(2 * it + b + 1)
                    second(2 * it + b, it, b)


@stage
def combine_experts(nc, m):
    with ExitStack() as ctx:
        sem = Sems(nc, ctx)
        place = [ctx.enter_context(nc.sbuf_tensor(f"c_place{k}", [P, G], U32)) for k in range(TOP)]
        y = [[ctx.enter_context(nc.sbuf_tensor(f"c_y{u}{k}", [P, D], F32)) for k in range(TOP)] for u in range(G)]
        s_slot = sem("c_slot")
        s_go = sem("c_go")
        s_y = [sem(f"c_y{u}") for u in range(G)]
        s_add = sem("c_add")
        s_done = sem("c_done")
        block = ctx.enter_context(nc.Block())

        @block.scalar
        def _(act):
            def slots(g):
                for k in range(TOP):
                    act.activation(place[k][:, :], m.place[:, ds(g * G, G), k], ACT.Copy).then_inc(s_slot, 1)

            slots(0)
            with act.Fori(1, NG) as g:
                for u in range(G):
                    act.wait_ge(s_y[u], 16 * TOP * g)
                slots(g)

        @block.gpsimd
        def _(pool):
            def gather(g):
                pool.wait_ge(s_slot, TOP * g + TOP)
                pool.sem_inc(s_go, 1)
                if not known(g):
                    pool.wait_ge(s_done, g)
                    pool.sem_inc(s_go, 1)
                for u in range(G):
                    for k in range(TOP):
                        pool.indirect_dma_start(out=y[u][k][:, :], out_offset=None, in_=m.y_d[:, :],
                                                in_offset=bass.IndirectOffsetOnAxis(ap=place[k][:, u:u + 1], axis=0)
                                                ).then_inc(s_y[u], 16)

            gather(0)
            with pool.Fori(1, NG) as g:
                gather(g)

        @block.vector
        def _(dve):
            with dve.Fori(0, NG) as g:
                for u in range(G):
                    dve.wait_ge(s_y[u], 16 * TOP * g + 16 * TOP)
                    x = m.x[:, g * G + u, :]
                    for k in range(TOP):
                        if u or k:
                            dve.wait_ge(s_add, g * G * TOP + u * TOP + k)
                        dve.scalar_tensor_tensor(x, y[u][k][:, :], m.gate[:, g * G + u, k:k + 1], x,
                                                 ALU.mult, ALU.add).then_inc(s_add, 1)
                dve.wait_ge(s_add, (g + 1) * G * TOP)
                dve.sem_inc(s_done, 1)


@stage
def move(nc, tag, loads):
    with ExitStack() as ctx:
        sem = Sems(nc, ctx)
        s = [sem(f"mv_{tag}{i}") for i in range(2)]
        block = ctx.enter_context(nc.Block())

        def issue(eng, mine, s_mine):
            for dst, src in mine:
                eng.dma_start(dst, src).then_inc(s_mine, 16)
            if mine:
                eng.wait_ge(s_mine, 16 * len(mine))

        @block.sync
        def _(sp):
            issue(sp, loads[0::2], s[0])

        @block.scalar
        def _(act):
            issue(act, loads[1::2], s[1])


class Memory:
    pass


def build(nc, a, out):
    m = Memory()
    with ExitStack() as top:
        def sb(name, shape, dt=F32, to=top):
            return to.enter_context(nc.sbuf_tensor(name, shape, dt))

        def dram(name, shape, dt=F32):
            return nc.dram_tensor(name, shape, dt, kind="Internal").ap()

        m.rec_d = dram("rec_d", [TX * EP, REC])
        m.row_d = dram("row_d", [2, E], BF16)
        m.k_d = dram("k_d", [N, D])
        m.v_d = dram("v_d", [N, D])
        m.h_d = dram("h_d", [N, D])
        m.ends_d = dram("ends_d", [4 * NBLK, 128])
        m.carry_d = dram("carry_d", [2 * NBLK, 128])
        m.list_d = dram("list_d", [ETX * EP, 1], U32)
        m.y_d = dram("y_d", [ET * EP, D])
        m.wrow_d = dram("wrow_d", [N])

        m.ident = sb("ident", [128, 128])
        m.ident_b = sb("ident_b", [128, 128], BF16)
        m.ones = sb("ones", [128, 128])
        m.before = sb("before", [128, 128])
        m.after = sb("after", [128, 128])
        m.iota = sb("iota", [128, T])
        m.part = sb("part", [128, 1])
        m.x = sb("x", [P, NT, D])
        edges = top.enter_context(ExitStack())
        m.node_tile = sb("node_tile", [1, T], I32, to=edges)
        m.h = sb("h", [P, NT, D], to=edges)
        agg_full = sb("agg", [128, NT, 448], to=edges)
        m.agg = agg_full[0:P, :, :]
        m.spare = agg_full[:, :, :].rearrange("p j c -> p (j c)")
        m.rec = sb("rec", [EP, TX, REC], to=edges)
        m.src = sb("src", [EP, TX], U32, to=edges)
        m.unit = sb("unit", [EP, TX, 3], to=edges)
        m.unit2 = sb("unit2", [EP, TX], to=edges)
        rows = lambda ap: ap.rearrange("(j p) d -> p j d", p=P)
        vec = lambda ap, n=P: ap.rearrange("(o d) -> o d", o=1).to_broadcast([n, ap.shape[0]])
        half = lambda ap: ap.rearrange("(k p) n -> p k n", p=128)

        build_constants(nc, m)
        build_sort(nc, m, a)
        build_reload(nc, m)

        with ExitStack() as l0:
            m.v = sb("v", [P, NT, D], to=l0)
            m.s = sb("s", [EP, T, H], to=l0)
            m.rel = sb("rel", [NREL, HD], to=l0)
            l0q = l0.enter_context(ExitStack())
            m.q = sb("q", [P, NT, D], to=l0q)
            move(nc, "x", [(m.x[:, :, :], rows(a["x"])), (m.rel[:, :], a["L0_gnn_rel_w"])])
            layer_norm(nc, m, "n0", m.x, m.h)
            with ExitStack() as c1:
                keys = m.spare[0:P, 0:NT * D].rearrange("p (j d) -> p j d", d=D)
                qe, *bias = [m.spare[0:P, (NT + i) * D:(NT + i + 1) * D] for i in range(4)]
                wqkv = [sb(f"wqkv{i}", [128, 2, D], to=c1) for i in range(3)]
                move(nc, "qkv", [(qe[:, :], vec(a["L0_gnn_query_emb"]))]
                     + [(bias[i][:, :], vec(a["L0_gnn_b" + c])) for i, c in enumerate("qkv")]
                     + [(wqkv[i][:, :, :], half(a["L0_gnn_W" + c])) for i, c in enumerate("qkv")])
                scale_qkv(nc, m, qe, bias[0])

                def enhance(dve, g, slot, ch):
                    return dve.tensor_tensor(slot[:, :, :], m.h[:, ds(g * G, G), :],
                                             qe[:, None, :].to_broadcast([P, G, D]), ALU.add)

                def take(dve, g, c, ps, ch):
                    b = bias[c][:, None, :].to_broadcast([P, G, D])
                    if c == 0:
                        return dve.scalar_tensor_tensor(m.q[:, ds(g * G, G), :], ps, 0.125, b, ALU.mult, ALU.add)
                    to = keys[:, ds(g * G, G), :] if c == 1 else m.v[:, ds(g * G, G), :]
                    return dve.tensor_tensor(to, ps, b, ALU.add)

                project(nc, m, "qkv", enhance, wqkv, D, take)
            move(nc, "kv", [(rows(m.k_d), keys), (rows(m.v_d), m.v[:, :, :])])
            build_scores(nc, m)
            l0q.close()
            build_weights(nc, m)
            build_values(nc, m)
            m.q = sb("y", [P, NT, D], to=l0)
            with ExitStack() as c1:
                rd = sb("rd", [P, NT, H], to=c1)
                dz = sb("dz", [P, NT, H], to=c1)
                bo = sb("bo", [P, D], to=c1)
                wo = sb("wo", [128, 2, D], to=c1)
                tmp = sb("tmp", [P, G, D], to=c1)
                move(nc, "wo", [(bo[:, :], vec(a["L0_gnn_bo"])), (wo[:, :, :], half(a["L0_gnn_Wo"]))])
                divide_sums(nc, m, rd, dz)
                hd = lambda ap: ap.rearrange("p u (h d) -> p u h d", h=H)

                def normalise(dve, g, slot, ch):
                    gs = ds(g * G, G)
                    shape = [P, G, H, HD]
                    ch(dve.tensor_tensor(hd(slot[:, :, :]), hd(m.agg[:, gs, 0:D]),
                                         rd[:, gs, :, None].to_broadcast(shape), ALU.mult))
                    ch(dve.tensor_tensor(hd(tmp[:, :, :]), hd(m.v[:, gs, :]), dz[:, gs, :, None].to_broadcast(shape),
                                         ALU.mult))
                    return dve.tensor_tensor(slot[:, :, :], slot[:, :, :], tmp[:, :, :], ALU.add)

                def residual(dve, g, c, ps, ch):
                    ch(dve.tensor_tensor(tmp[:, :, :], ps, bo[:, None, :].to_broadcast([P, G, D]), ALU.add))
                    return dve.tensor_tensor(m.q[:, ds(g * G, G), :], tmp[:, :, :], m.h[:, ds(g * G, G), :], ALU.add)

                project(nc, m, "wo", normalise, [wo], D, residual, own=3)
            with ExitStack() as c1:
                gb = [sb(f"gb{i}", [P, D], to=c1) for i in range(2)]
                move(nc, "gb", [(gb[0][:, :], vec(a["L0_gnn_gamma"])), (gb[1][:, :], vec(a["L0_gnn_beta"]))])
                layer_norm(nc, m, "n1", m.q, m.v, gb[0], gb[1])
            add_all(nc, "l0", [(m.x[:, :, :], m.x[:, :, :], m.v[:, :, :])])

        layer_norm(nc, m, "n2", m.x, m.h)
        with ExitStack() as c0:
            m.h_t = sb("h_t0", [128, 2, N], to=c0)
            m.w = sb("w", [P, NT], to=c0)
            with ExitStack() as c1:
                wr = sb("wr", [128, 2, 1], to=c1)
                br = sb("br", [P, 1], to=c1)
                with nc.allow_non_contiguous_dma(reason="256 words, once"):
                    move(nc, "wr", [(wr[:, :, :], half(a["L0_ffn_wr"])), (br[:, :], vec(a["L0_ffn_br"]))])

                def copy_rows(dve, g, slot, ch):
                    return dve.tensor_copy(slot[:, :, :], m.h[:, ds(g * G, G), :])

                def keep(g, k):
                    return m.h_t[:, k, ds(g * G * P, G * P)].rearrange("p (u n) -> p u n", u=G)

                def take_w(dve, g, c, ps, ch):
                    return dve.tensor_scalar(m.w[:, ds(g * G, G)], ps[:, :, 0], br[:, 0:1], None, ALU.add)

                project(nc, m, "wr", copy_rows, [wr], 1, take_w, keep=keep)
            build_top(nc, m)
            add_all(nc, "f0", [(m.x[:, :, :], m.x[:, :, :], m.h[:, :, :])])
            feed_forward(nc, m, "f0", ACT.Gelu_apprx_tanh,
                         [a["L0_ffn_w1"], a["L0_ffn_b1"], a["L0_ffn_w2"], a["L0_ffn_b2"]],
                         gate=lambda g: m.w[:, ds(g * G, G), None])

        layer_norm(nc, m, "n3", m.x, m.h)
        with ExitStack() as c0:
            m.w_h = sb("w_h", [128, 64], to=c0)
            m.w_o = sb("w_o", [128, 192], to=c0)
            m.w_d = sb("w_d", [128, 2, 192], to=c0)
            m.w_s = sb("w_s", [64, 64], to=c0)
            m.w_l = sb("w_l", [128, 64], to=c0)
            move(nc, "h", [(rows(m.h_d), m.h[:, :, :]), (m.w_s[:, :], a["L1_gnn_lin_scalar_w"])])
            scale_logits(nc, m)
            build_geometric_weights(nc, m, a)
            build_geometric(nc, m)
            with ExitStack() as c1:
                tmp = sb("tmp1", [P, G, D], to=c1)

                def vectors(dve, g, slot, ch):
                    ch(dve.memset(slot[:, :, 192:256], 0.0))
                    return dve.tensor_copy(slot[:, :, 0:192].rearrange("p u (k c) -> p u k c", k=3),
                                           m.agg[:, ds(g * G, G), 64:256].rearrange("p u (c k) -> p u k c", k=3))

                def joined(dve, g, c, ps, ch):
                    gs = ds(g * G, G)
                    ch(dve.tensor_copy(tmp[:, :, 0:64], m.agg[:, gs, 0:64]))
                    ch(dve.tensor_tensor(tmp[:, :, 64:256].rearrange("p u (c k) -> p u k c", k=3),
                                         ps.rearrange("p u (k c) -> p u k c", k=3),
                                         m.agg[:, gs, 256:448].rearrange("p u (k c) -> p u k c", k=3), ALU.add))
                    ch(dve.tensor_tensor(tmp[:, :, :], tmp[:, :, :], m.h[:, gs, :], ALU.add))
                    return dve.tensor_tensor(m.x[:, gs, :], m.x[:, gs, :], tmp[:, :, :], ALU.add)

                project(nc, m, "wd", vectors, [m.w_d], 192, joined, own=4)

        edges.close()
        m.mask = sb("mask1", [P, NT, NE])
        m.gate = sb("gate", [P, NT, TOP])
        m.place = sb("place", [P, NT, TOP], U32)
        m.number = sb("number", [P, NT], U32)
        m.expert = sb("expert", [1, ETX], I32)
        m.rows_of = sb("rows_of", [EP, ETX], U32)
        with ExitStack() as c0:
            m.h_t = sb("h_t1", [128, 2, N], to=c0)
            with ExitStack() as c1:
                m.h = sb("h1", [P, NT, D], to=c1)
                wr = sb("wr1", [128, 2, NE], to=c1)
                layer_norm(nc, m, "n4", m.x, m.h)
                move(nc, "wr1", [(rows(m.h_d), m.h[:, :, :]), (wr[:, :, :], half(a["L1_ffn_Wr"]))])

                def take_l(dve, g, c, ps, ch):
                    return dve.tensor_copy(m.mask[:, ds(g * G, G), :], ps)

                def keep1(g, k):
                    return m.h_t[:, k, ds(g * G * P, G * P)].rearrange("p (u n) -> p u n", u=G)

                project(nc, m, "wr1", lambda dve, g, slot, ch: dve.tensor_copy(slot[:, :, :], m.h[:, ds(g * G, G), :]),
                        [wr], NE, take_l, keep=keep1)
            build_router(nc, m)

            m.w1 = sb("e_w1", [128, NE, 2, FF], to=c0)
            m.w2 = sb("e_w2", [128, NE, NF, D], to=c0)

            room = m.w2[:, EARLY:NE, :, :].rearrange("p e c d -> p (e c d)")[:, 0:NF * G * P]

            def load_experts(sp, s_done):
                for e in range(NE):
                    sp.dma_start(m.w1[:, e, :, :], a["L1_ffn_W1p"][e].rearrange("(k p) f -> p k f", p=128)
                                 ).then_inc(s_done, 16)
                for e in range(EARLY):
                    sp.dma_start(m.w2[:, e, :, :], a["L1_ffn_W2p"][e].rearrange("(c p) d -> p c d", p=128)
                                 ).then_inc(s_done, 16)
                return 16 * (NE + EARLY)

            feed_forward(nc, m, "f1", ACT.Gelu,
                         [a["L1_ffn_W1s"], a["L1_ffn_b1s"], a["L1_ffn_W2s"], a["L1_ffn_b2s"]], later=load_experts, rows=True,
                         room=room.rearrange("p (c n) -> p c n", c=NF))
            build_experts(nc, m, a)
        combine_experts(nc, m)
        move(nc, "out", [(rows(out), m.x[:, :, :])])


@stage
def scale_qkv(nc, m, qe, bq):
    with ExitStack() as ctx:
        s = Sems(nc, ctx)("sc_qkv")
        block = ctx.enter_context(nc.Block())

        @block.vector
        def _(dve):
            ch = Chain(dve, s)
            ch(dve.tensor_scalar(qe[:, :], qe[:, :], 0.1, None, ALU.mult))
            ch(dve.tensor_scalar(bq[:, :], bq[:, :], 0.125, None, ALU.mult))
            ch(dve.tensor_scalar(m.rel[:, :], m.rel[:, :], 0.2, None, ALU.mult))


@stage
def scale_logits(nc, m):
    with ExitStack() as ctx:
        s = Sems(nc, ctx)("sc_log")
        block = ctx.enter_context(nc.Block())

        @block.vector
        def _(dve):
            Chain(dve, s)(dve.tensor_scalar(m.w_s[:, :], m.w_s[:, :], 0.125, None, ALU.mult))


@stage
def divide_sums(nc, m, rd, dz):
    with ExitStack() as ctx:
        s = Sems(nc, ctx)("sc_div")
        block = ctx.enter_context(nc.Block())

        @block.vector
        def _(dve):
            ch = Chain(dve, s)
            ch(dve.tensor_scalar(dz[:, :, :], m.agg[:, :, D:D + H], 0.0, None, ALU.is_equal))
            ch(dve.tensor_tensor(rd[:, :, :], m.agg[:, :, D:D + H], dz[:, :, :], ALU.add))
            ch(dve.reciprocal(rd[:, :, :], rd[:, :, :]))


_INS = ["x", "src", "dst", "edge_attr_3", "edge_type_64", "L0_gnn_query_emb", "L0_gnn_Wq", "L0_gnn_bq", "L0_gnn_Wk",
        "L0_gnn_bk", "L0_gnn_Wv", "L0_gnn_bv", "L0_gnn_rel_w", "L0_gnn_Wo", "L0_gnn_bo", "L0_gnn_gamma",
        "L0_gnn_beta", "L0_ffn_wr", "L0_ffn_br", "L0_ffn_w1", "L0_ffn_b1", "L0_ffn_w2", "L0_ffn_b2",
        "L1_gnn_lin_src_w0", "L1_gnn_lin_src_w1", "L1_gnn_tp1_w00", "L1_gnn_tp1_w11", "L1_gnn_tp1_w01",
        "L1_gnn_tp1_w10", "L1_gnn_tp2_w00", "L1_gnn_tp2_w11", "L1_gnn_tp2_w01", "L1_gnn_tp2_w10",
        "L1_gnn_lin_hidden_w0", "L1_gnn_lin_hidden_w1", "L1_gnn_lin_scalar_w", "L1_ffn_Wr", "L1_ffn_W1s",
        "L1_ffn_b1s", "L1_ffn_W2s", "L1_ffn_b2s", "L1_ffn_W1p", "L1_ffn_b1p", "L1_ffn_W2p", "L1_ffn_b2p"]


def kernel(**inputs):
    import numpy as _np
    import concourse.bacc as _bacc
    from concourse import mybir as _mybir
    from concourse.bass_utils import run_bass_kernel_spmd as _run

    nc = _bacc.Bacc("TRN2", target_bir_lowering=False, num_devices=1)
    arrays, args = {}, {}
    for name in _INS:
        x = _np.ascontiguousarray(inputs[name])
        arrays[f"in_{name}"] = x
        args[name] = nc.dram_tensor(f"in_{name}", x.shape, _mybir.dt.from_np(x.dtype), kind="ExternalInput").ap()
    out = nc.dram_tensor("out_0", (N, D), _mybir.dt.float32, kind="ExternalOutput").ap()
    build(nc, args, out)
    r = _run(nc, [arrays], core_ids=[0])
    return r.results[0]["out_0"]
```
